# Optimizing a Trainium2 kernel written in Bass

```python
import numpy as np
import jax
import jax.numpy as jnp

def _softmax(x, axis=-1):
    return jax.nn.softmax(x, axis=axis)

def _gelu(x):
    return jax.nn.gelu(x, approximate=True)

def _silu(x):
    return jax.nn.silu(x)

def _sigmoid(x):
    return jax.nn.sigmoid(x)

def _layernorm(x, axis=-1, eps=1e-05):
    m = jnp.mean(x, axis=axis, keepdims=True)
    v = jnp.var(x, axis=axis, keepdims=True)
    return (x - m) / jnp.sqrt(v + eps)

def _scatter_add(tgt, idx, src, axis=0):
    return tgt.at[idx].add(src)

def _segment_sum(src, seg, n):
    return jax.ops.segment_sum(src, seg, n)
kernel_name = 'mk_gnn_resnorm_d2_gnn_r32_78d33a'

def setup_inputs(seed: int=0):
    np.random.seed(seed)
    _w = jnp.asarray

    def _rec_inputs():
        import jax
        import jax.numpy as jnp
        _gk = jax.random.key(seed)
        x = -0.000202 + 1 * jax.random.normal(jax.random.fold_in(_gk, 1), (50000, 128), jnp.float32)
        src = jax.random.randint(jax.random.fold_in(_gk, 2), (50000,), 0, 50000, jnp.int32)
        dst = jax.random.randint(jax.random.fold_in(_gk, 3), (50000,), 0, 50000, jnp.int32)
        _o = jnp.argsort(dst, stable=True)
        src = src[_o]
        dst = dst[_o]
        edge_attr_2 = 0.000452788 + 0.999756 * jax.random.normal(jax.random.fold_in(_gk, 11), (50000, 2), jnp.float32)
        return (x, src, dst, edge_attr_2)
    x, src, dst, edge_attr_2 = _rec_inputs()

    def _L0_gnn_setup():
        import jax, jax.numpy as jnp
        import numpy as np
        N, E, D, H, O = (50000, 25000, 128, 128, 128)
        BN_EPS = 1e-05
        key = jax.random.key(seed)
        ks = jax.random.split(key, 6)
        x = jax.random.normal(ks[0], (N, D), dtype=jnp.float32)
        edge_index = jax.random.randint(ks[1], (2, E), 0, N, dtype=jnp.int64)
        W_msg = jax.random.normal(ks[2], (2 * D, H), dtype=jnp.float32) * (1.0 / np.sqrt(2 * D))
        b_msg = jnp.zeros((H,), dtype=jnp.float32)
        W_upd = jax.random.normal(ks[3], (D + H, O), dtype=jnp.float32) * (1.0 / np.sqrt(D + H))
        b_upd = jnp.zeros((O,), dtype=jnp.float32)
        prelu_a = jnp.full((1,), 0.25, dtype=jnp.float32)
        gamma = jnp.ones((O,), dtype=jnp.float32)
        beta = jnp.zeros((O,), dtype=jnp.float32)
        return {'x': x, 'edge_index': edge_index, 'W_msg': W_msg, 'b_msg': b_msg, 'W_upd': W_upd, 'b_upd': b_upd, 'prelu_a': prelu_a, 'gamma': gamma, 'beta': beta}
    _L0_gnn_all = _L0_gnn_setup()
    _L0_gnn_in = {k: v for k, v in _L0_gnn_all.items() if k in ('W_msg', 'b_msg', 'W_upd', 'b_upd', 'prelu_a', 'gamma', 'beta')}
    del _L0_gnn_all

    def _L1_gnn_setup():
        import jax, jax.numpy as jnp
        import numpy as np
        N, IN_DIM, HID, OUT_DIM, H, EDGE_DIM, E = (50000, 128, 128, 128, 4, 2, 25000)
        C = HID // H
        NEG_SLOPE = 0.2

        def _gatv2_encoder(x, edge_index, edge_attr, w_in, b_in, w_l, b_l, w_r, b_r, w_e, att, bias_conv, w_out, b_out):
            n = x.shape[0]
            h = jax.nn.elu(x @ w_in + b_in)
            x_l = (h @ w_l + b_l).reshape(n, H, C)
            x_r = (h @ w_r + b_r).reshape(n, H, C)
            loop = jnp.arange(n)
            src = jnp.concatenate([edge_index[0], loop])
            dst = jnp.concatenate([edge_index[1], loop])
            ea = jnp.concatenate([edge_attr, jnp.broadcast_to(edge_attr.mean(0), (n, edge_attr.shape[1]))], axis=0)
            e_feat = (ea @ w_e).reshape(-1, H, C)
            z = jax.nn.leaky_relu(x_l[src] + x_r[dst] + e_feat, NEG_SLOPE)
            alpha = jnp.einsum('ehc,hc->eh', z, att)
            m = jax.ops.segment_max(alpha, dst, num_segments=n)
            ex = jnp.exp(alpha - m[dst])
            s = jax.ops.segment_sum(ex, dst, num_segments=n)
            a = ex / s[dst]
            msg = x_l[src] * a[:, :, None]
            agg = jax.ops.segment_sum(msg, dst, num_segments=n).reshape(n, H * C)
            h2 = jax.nn.elu(agg + bias_conv)
            return h2 @ w_out + b_out
        key = jax.random.key(seed)
        ks = jax.random.split(key, 16)
        s_in = 1.0 / np.sqrt(IN_DIM)
        s_h = 1.0 / np.sqrt(HID)
        s_e = 1.0 / np.sqrt(EDGE_DIM)
        return {'x': jax.random.normal(ks[0], (N, IN_DIM), jnp.float32), 'edge_index': jax.random.randint(ks[1], (2, E), 0, N, jnp.int64), 'edge_attr': jax.random.normal(ks[2], (E, EDGE_DIM), jnp.float32), 'w_in': jax.random.normal(ks[3], (IN_DIM, HID), jnp.float32) * s_in, 'b_in': jnp.zeros((HID,), jnp.float32), 'w_l': jax.random.normal(ks[4], (HID, H * C), jnp.float32) * s_h, 'b_l': jnp.zeros((H * C,), jnp.float32), 'w_r': jax.random.normal(ks[5], (HID, H * C), jnp.float32) * s_h, 'b_r': jnp.zeros((H * C,), jnp.float32), 'w_e': jax.random.normal(ks[6], (EDGE_DIM, H * C), jnp.float32) * s_e, 'att': jax.random.normal(ks[7], (H, C), jnp.float32) * (1.0 / np.sqrt(C)), 'bias_conv': jnp.zeros((H * C,), jnp.float32), 'w_out': jax.random.normal(ks[8], (HID, OUT_DIM), jnp.float32) * s_h, 'b_out': jnp.zeros((OUT_DIM,), jnp.float32)}
    _L1_gnn_all = _L1_gnn_setup()
    _L1_gnn_in = {k: v for k, v in _L1_gnn_all.items() if k in ('w_in', 'b_in', 'w_l', 'b_l', 'w_r', 'b_r', 'w_e', 'att', 'bias_conv', 'w_out', 'b_out')}
    del _L1_gnn_all
    return {'x': x, 'src': src, 'dst': dst, 'edge_attr_2': edge_attr_2, 'L0_gnn_W_msg': _L0_gnn_in['W_msg'], 'L0_gnn_b_msg': _L0_gnn_in['b_msg'], 'L0_gnn_W_upd': _L0_gnn_in['W_upd'], 'L0_gnn_b_upd': _L0_gnn_in['b_upd'], 'L0_gnn_prelu_a': _L0_gnn_in['prelu_a'], 'L0_gnn_gamma': _L0_gnn_in['gamma'], 'L0_gnn_beta': _L0_gnn_in['beta'], 'L1_gnn_w_in': _L1_gnn_in['w_in'], 'L1_gnn_b_in': _L1_gnn_in['b_in'], 'L1_gnn_w_l': _L1_gnn_in['w_l'], 'L1_gnn_b_l': _L1_gnn_in['b_l'], 'L1_gnn_w_r': _L1_gnn_in['w_r'], 'L1_gnn_b_r': _L1_gnn_in['b_r'], 'L1_gnn_w_e': _L1_gnn_in['w_e'], 'L1_gnn_att': _L1_gnn_in['att'], 'L1_gnn_bias_conv': _L1_gnn_in['bias_conv'], 'L1_gnn_w_out': _L1_gnn_in['w_out'], 'L1_gnn_b_out': _L1_gnn_in['b_out']}

def reference(x, src, dst, edge_attr_2, L0_gnn_W_msg, L0_gnn_b_msg, L0_gnn_W_upd, L0_gnn_b_upd, L0_gnn_prelu_a, L0_gnn_gamma, L0_gnn_beta, L1_gnn_w_in, L1_gnn_b_in, L1_gnn_w_l, L1_gnn_b_l, L1_gnn_w_r, L1_gnn_b_r, L1_gnn_w_e, L1_gnn_att, L1_gnn_bias_conv, L1_gnn_w_out, L1_gnn_b_out):
    import jax
    import jax.numpy as jnp

    def _L0_gnn_ref(x, edge_index, W_msg, b_msg, W_upd, b_upd, prelu_a, gamma, beta):
        import jax, jax.numpy as jnp
        import numpy as np
        N, E, D, H, O = (50000, 25000, 128, 128, 128)
        BN_EPS = 1e-05
        src, dst = (edge_index[0], edge_index[1])
        n = x.shape[0]
        msg_in = jnp.concatenate([x[src], x[dst]], axis=-1)
        m = jax.nn.relu(msg_in @ W_msg + b_msg)
        agg = jax.ops.segment_sum(m, dst, num_segments=n)
        cnt = jax.ops.segment_sum(jnp.ones((m.shape[0],), m.dtype), dst, num_segments=n)
        agg = agg / jnp.maximum(cnt, 1.0)[:, None]
        h = jnp.concatenate([x, agg], axis=-1) @ W_upd + b_upd
        h = jnp.where(h >= 0, h, prelu_a[0] * h)
        mean = jnp.mean(h, axis=0)
        var = jnp.mean(jnp.square(h - mean), axis=0)
        out = (h - mean) * jax.lax.rsqrt(var + BN_EPS) * gamma + beta
        return out

    def _L1_gnn_ref(x, edge_index, edge_attr, w_in, b_in, w_l, b_l, w_r, b_r, w_e, att, bias_conv, w_out, b_out):
        import jax, jax.numpy as jnp
        import numpy as np
        N, IN_DIM, HID, OUT_DIM, H, EDGE_DIM, E = (50000, 128, 128, 128, 4, 2, 25000)
        C = HID // H
        NEG_SLOPE = 0.2

        def _gatv2_encoder(x, edge_index, edge_attr, w_in, b_in, w_l, b_l, w_r, b_r, w_e, att, bias_conv, w_out, b_out):
            n = x.shape[0]
            h = jax.nn.elu(x @ w_in + b_in)
            x_l = (h @ w_l + b_l).reshape(n, H, C)
            x_r = (h @ w_r + b_r).reshape(n, H, C)
            loop = jnp.arange(n)
            src = jnp.concatenate([edge_index[0], loop])
            dst = jnp.concatenate([edge_index[1], loop])
            ea = jnp.concatenate([edge_attr, jnp.broadcast_to(edge_attr.mean(0), (n, edge_attr.shape[1]))], axis=0)
            e_feat = (ea @ w_e).reshape(-1, H, C)
            z = jax.nn.leaky_relu(x_l[src] + x_r[dst] + e_feat, NEG_SLOPE)
            alpha = jnp.einsum('ehc,hc->eh', z, att)
            m = jax.ops.segment_max(alpha, dst, num_segments=n)
            ex = jnp.exp(alpha - m[dst])
            s = jax.ops.segment_sum(ex, dst, num_segments=n)
            a = ex / s[dst]
            msg = x_l[src] * a[:, :, None]
            agg = jax.ops.segment_sum(msg, dst, num_segments=n).reshape(n, H * C)
            h2 = jax.nn.elu(agg + bias_conv)
            return h2 @ w_out + b_out
        return _gatv2_encoder(x, edge_index, edge_attr, w_in, b_in, w_l, b_l, w_r, b_r, w_e, att, bias_conv, w_out, b_out)
    edge_index = jnp.stack([src, dst])
    x = _layernorm(x + _L0_gnn_ref(x, edge_index, L0_gnn_W_msg, L0_gnn_b_msg, L0_gnn_W_upd, L0_gnn_b_upd, L0_gnn_prelu_a, L0_gnn_gamma, L0_gnn_beta), axis=-1)
    x = _layernorm(x + _L1_gnn_ref(x, edge_index, edge_attr_2, L1_gnn_w_in, L1_gnn_b_in, L1_gnn_w_l, L1_gnn_b_l, L1_gnn_w_r, L1_gnn_b_r, L1_gnn_w_e, L1_gnn_att, L1_gnn_bias_conv, L1_gnn_w_out, L1_gnn_b_out), axis=-1)
    return x

_drawn_inputs = setup_inputs


def setup_inputs(seed=0):
    import zlib

    import numpy as np

    out = dict(_drawn_inputs(seed))
    spreads = {'L0_gnn_b_msg': (0.0, 0.1),
     'L0_gnn_b_upd': (0.0, 0.1),
     'L0_gnn_gamma': (1.0, 0.2),
     'L0_gnn_beta': (0.0, 0.1),
     'L1_gnn_b_in': (0.0, 0.1),
     'L1_gnn_b_l': (0.0, 0.1),
     'L1_gnn_b_r': (0.0, 0.8),
     'L1_gnn_bias_conv': (0.0, 0.1),
     'L1_gnn_b_out': (0.0, 0.1)}
    factors = {}
    for name, (base, spread) in spreads.items():
        noise = np.random.default_rng([zlib.crc32(name.encode()), seed]).standard_normal(out[name].shape)
        drawn = base * np.exp(spread * noise) if base else spread * noise
        out[name] = jnp.asarray(drawn.astype(out[name].dtype))
    for name, factor in factors.items():
        out[name] = (out[name] * factor).astype(out[name].dtype)
    return out
```

```python
from contextlib import ExitStack

import concourse.bass as bass
from concourse import mybir
from concourse.alu_op_type import AluOpType as ALU

P = 128
D = 128
HEADS, C = 4, 32
TILES = 4
G = P * TILES
ROW3 = D + HEADS
ROWA = ROW3 + HEADS
BIG = 1.0e30
SKIP = 1 << 20
EPS = 1.0e-5
SLOPE = 0.2
LN_STEPS = 14

PARTS = 3
PAIRS = PARTS * PARTS

F32, I32, BF16 = mybir.dt.float32, mybir.dt.int32, mybir.dt.bfloat16
ACT = mybir.ActivationFunctionType
AX = mybir.AxisListType


def group_rows(table, g, width):
    return table[bass.ds(g * G, G), 0:width].rearrange("(p k) w -> p k w", k=TILES)


def slots(first, count):
    return first * count


def need(eng, sem, value, gate=None):
    if isinstance(value, int) and value <= 0:
        return
    eng.wait_ge(sem, value)
    if gate is not None:
        eng.sem_inc(gate, 1)


def run_stages(eng, stages, groups):
    def step(i, u, least, most):
        for stage, lag in stages:
            if least <= lag <= most:
                stage(i + (u - lag) // 2, (u - lag) % 2)
    deepest = max(lag for _, lag in stages)
    first = (deepest + 1) // 2 if deepest else 1
    for g in range(2 * first):
        step(g // 2, g % 2, 0, g)
    with eng.Fori(first, groups // 2) as i:
        for u in range(2):
            step(i, u, 0, deepest)
    for g in range(groups, groups + deepest):
        step(g // 2, g % 2, g - groups + 1, deepest)


def run_groups(eng, body, groups):
    for u in range(2):
        body(0, u)
    with eng.Fori(1, groups // 2) as i:
        for u in range(2):
            body(i, u)


def inv_sqrt(nc, chain, y, v, t):
    chain(nc.vector.tensor_scalar(v, v, EPS, None, ALU.add))
    chain(nc.vector.tensor_scalar(t.bitcast(I32), v.bitcast(I32), 1, None, ALU.logical_shift_right))
    chain(nc.vector.tensor_scalar(y.bitcast(I32), t.bitcast(I32), -1.0, float(0x5F3759DF), ALU.mult, ALU.add))
    for _ in range(3):
        chain(nc.vector.scalar_tensor_tensor(t, y, -0.5, y, ALU.mult, ALU.mult))
        chain(nc.vector.tensor_tensor(t, t, v, ALU.mult))
        chain(nc.vector.scalar_tensor_tensor(y, t, 1.5, y, ALU.add, ALU.mult))


def layer_norm(nc, dve, gate, chain, src, stats, mv, rstd, shift):
    for k in range(TILES):
        last = nc.vector.bn_stats(stats[:, k, :], src[:, k, :])
    chain(last)
    dve.sem_inc(gate, 1)
    for k in range(TILES):
        last = nc.vector.bn_aggr(mv[:, k, :], stats[:, k, :])
    chain(last)
    inv_sqrt(nc, chain, rstd, mv[:, :, 1], stats[:, :, 0])
    return nc.vector.scalar_tensor_tensor(shift, mv[:, :, 0], -1.0, rstd,
                                          ALU.mult, ALU.mult)


def build(nc, x, src_col, dst_col, next_col, dst_row, next_row, prev_row, before_row, ea_row,
          W_msg, b_msg, W_upd, b_upd, prelu_a, gamma, beta,
          w_in, b_in, w_l, b_l, w_r, b_r, w_e, att, bias_conv, w_out, b_out, out, n_nodes, n_edges):
    NP = x.shape[0]
    GROUPS = NP // G
    EG = dst_row.shape[0]
    ET = EG * TILES
    VALID = n_nodes - (GROUPS - 1) * G
    assert GROUPS % 2 == 0 and EG % 2 == 0 and VALID % TILES == 0 and VALID > 0
    HALF = GROUPS // 2
    EHALF = EG // 2

    def scratch(name, shape):
        return nc.dram_tensor(name, shape, F32, kind="Internal").ap()

    sums0 = scratch("sums0", (NP, D))
    h_t = scratch("h_t", (D, NP))
    x1_t = scratch("x1", (NP, D))
    xl_t = scratch("xl", (NP, ROW3))
    xr_t = scratch("xr", (NP, D))
    sums1 = scratch("sums1", (NP, ROWA))
    masks = scratch("masks", (EG, 3, G))
    ea_parts = nc.dram_tensor("ea_parts", (EG, PAIRS * 2, G), BF16, kind="Internal").ap()
    we_parts = nc.dram_tensor("we_parts", (3, 2, D), BF16, kind="Internal").ap()

    top = ExitStack()
    with top:
        def sb(name, shape, dt=F32, ctx=top):
            return ctx.enter_context(nc.sbuf_tensor(name, shape, dt))

        def pb(name, shape=(P, G), ctx=top):
            return ctx.enter_context(nc.psum_tensor(name, list(shape), F32))

        def sem(name):
            return top.enter_context(nc.semaphore(name))

        def sem2(name):
            return [sem(f"{name}{u}") for u in range(2)]

        ident = sb("ident", [P, P])
        ones_col = sb("ones_col", [P, 1])
        wm = sb("wm", [P, 2, D])
        wu = sb("wu", [P, 2, D])
        win = sb("win", [P, D])
        wlr = sb("wlr", [P, 2, D])
        wsum = sb("wsum", [P, D])
        wout = sb("wout", [P, D])
        we = sb("we", [2, D])
        we18 = sb("we18", [PAIRS * 2, D], BF16)
        attb = sb("attb", [P, HEADS])
        cols = sb("cols", [P, 12])
        bmsg, bupd, gam, bet, bin_, bl, br, bconv, alpha, binm1, bz, bself = (cols[:, j:j + 1] for j in range(12))
        cols2 = sb("cols2", [P, 8])
        bc, bcm1, bn_scale, bn_shift, ebias = (cols2[:, j:j + 1] for j in range(5))
        bout = sb("bout", [P, D])
        srcc = sb("srcc", [P, ET], I32)
        dstc = sb("dstc", [P, ET], I32)
        nextc = sb("nextc", [P, ET], I32)
        dstf = sb("dstf", [P, ET])
        idx = sb("idx", [P, EG, 3, TILES], I32)
        bn = sb("bn", [P, GROUPS - 1 + TILES, 6])
        bnmv = sb("bnmv", [P, 2])
        step = sem("step")
        gate, gate_sp, gate_pe, gate_dve = sem("gate"), sem("gate_sp"), sem("gate_pe"), sem("gate_dve")
        steps = {"n": 0}

        with ExitStack() as ctx:
            rows = sb("rows", [EG, 4, G], I32, ctx)
            rowf = sb("rowf", [EG, 4, G], F32, ctx)
            befo = sb("befo", [EG, 1], I32, ctx)
            befof = sb("befof", [EG, 1], F32, ctx)
            mask = sb("mask", [EG, 3, G], F32, ctx)
            keep = sb("keep", [P, ET], F32, ctx)
            eag = sb("eag", [EG, 2, G], F32, ctx)
            eas = sb("eas", [EG, 2], F32, ctx)
            emean = sb("emean", [2, 1], F32, ctx)
            eap = sb("eap", [EG, PARTS, 2, G], BF16, ctx)
            earest = sb("earest", [EG, 2, G], F32, ctx)
            wep = sb("wep", [2, PARTS, D], BF16, ctx)
            werest = sb("werest", [2, D], F32, ctx)
            zero0 = sb("zero0", [P, TILES * D], F32, ctx)
            zero1 = sb("zero1", [P, TILES, ROWA], F32, ctx)
            ps = pb("ps_setup", ctx=ctx)
            loaded, bias_in = sem("loaded"), sem("bias_in")
            zeros, cleared, id0, id1 = sem("zeros"), sem("cleared"), sem("id0"), sem("id1")
            mask_ready, masks_out = sem("mask_ready"), sem("masks_out")
            sum_ready, mean_sum, mean_ready, ebias_ready = sem("sum_ready"), sem("mean_sum"), sem("mean_ready"), sem("ebias_ready")
            att0, att_in = sem("att0"), sem("att_in")
            pst = sem("pstep_setup")
            parts_ready, parts_out, we_in = sem("parts_ready"), sem("parts_out"), sem("we_in")
            n_loads = 17
            block = ctx.enter_context(nc.Block())

            @block.sync
            def _(sp):
                def load(dst, src):
                    sp.dma_start(dst, src).then_inc(loaded, 16)
                load(srcc[:, :], src_col)
                load(dstc[:, :], dst_col)
                load(nextc[:, :], next_col)
                load(rows[:, 0, :], dst_row)
                load(rows[:, 1, :], next_row)
                load(rows[:, 2, :], prev_row)
                load(befo[:, :], before_row)
                load(eag[:, :, :], ea_row)
                for j in range(2):
                    load(wm[:, j, :], W_msg[j * D:(j + 1) * D, :])
                    load(wu[:, j, :], W_upd[j * D:(j + 1) * D, :])
                load(win[:, :], w_in)
                load(wlr[:, 0, :], w_l)
                load(wlr[:, 1, :], w_r)
                load(wout[:, :], w_out)
                load(we[:, :], w_e)
                sp.wait_ge(zeros, 3)
                for g in range(GROUPS):
                    sp.dma_start(group_rows(sums0, g, D), zero0[:, :].rearrange("p (k w) -> p k w", k=TILES)).then_inc(cleared, 16)
                sp.wait_ge(mask_ready, 1)
                sp.dma_start(masks, mask[:, :, :]).then_inc(masks_out, 16)
                sp.wait_ge(parts_ready, 1)
                for j in range(PARTS):
                    sp.dma_start(ea_parts[:, j * 2 * PARTS:(j + 1) * 2 * PARTS, :].rearrange("g (a d) q -> g a d q", a=PARTS),
                                 eap[:, :, :, :]).then_inc(parts_out, 16)
                sp.dma_start(we_parts.rearrange("a d f -> d a f"), wep[:, :, :]).then_inc(parts_out, 16)
                sp.wait_ge(parts_out, 16 * (PARTS + 1))
                for j in range(PARTS):
                    for a in range(PARTS):
                        row = (j * PARTS + a) * 2
                        sp.dma_start(we18[row:row + 2, :], we_parts[j, :, :]).then_inc(we_in, 16)
                sp.wait_ge(we_in, 16 * PAIRS)
                sp.wait_ge(masks_out, 16)
                sp.wait_ge(cleared, 16 * 2 * GROUPS)

            @block.scalar
            def _(act):
                for col, vec in ((bmsg, b_msg), (bupd, b_upd), (gam, gamma), (bet, beta), (bin_, b_in), (bl, b_l),
                                 (br, b_r), (bconv, bias_conv)):
                    act.dma_start(col, vec.rearrange("(p o) -> p o", o=1)).then_inc(bias_in, 16)
                act.dma_start(alpha, prelu_a.partition_broadcast(P)).then_inc(bias_in, 16)
                act.dma_start(bout[:, :], b_out.partition_broadcast(P)).then_inc(bias_in, 16)
                act.wait_ge(att0, 1)
                for h in range(HEADS):
                    act.dma_start(attb[h * C:(h + 1) * C, h:h + 1], att[h:h + 1, :].rearrange("o c -> c o")).then_inc(att_in, 16)
                act.wait_ge(zeros, 3)
                for g in range(GROUPS):
                    act.dma_start(group_rows(sums1, g, ROWA), zero1[:, :, :]).then_inc(cleared, 16)
                act.wait_ge(att_in, 16 * HEADS)

            @block.gpsimd
            def _(pool):
                nc.gpsimd.memset(ident[:, :], 0.0).then_inc(id0, 1)
                pool.wait_ge(id0, 1)
                nc.gpsimd.affine_select(out=ident[:, :], in_=ident[:, :], compare_op=ALU.not_equal, fill=1.0, base=0,
                                        pattern=[[-1, P]], channel_multiplier=1).then_inc(id1, 1)
                pool.wait_ge(id1, 1)

            @block.tensor
            def _(pe):
                pe.wait_ge(sum_ready, 1)
                nc.tensor.matmul(ps[0:2, 0:1], eas[:, :], ones_col[0:EG, :], start=True, stop=True).then_inc(mean_sum, 1)
                pe.wait_ge(mean_ready, 1)
                nc.tensor.matmul(ps[:, 1:2], we[:, :], emean[:, :], start=True, stop=True).then_inc(ebias_ready, 1)

            @block.vector
            def _(dve):
                n = [0]

                def chain(ins):
                    n[0] += 1
                    ins.then_inc(pst, 1)
                    dve.wait_ge(pst, n[0])

                nc.vector.memset(zero0[:, :], 0.0).then_inc(zeros, 1)
                chain(nc.vector.memset(zero1[:, :, :], 0.0))
                nc.vector.memset(zero1[:, :, ROW3:ROWA], -BIG).then_inc(zeros, 1)
                nc.vector.memset(ones_col[:, :], 1.0).then_inc(zeros, 1)
                nc.vector.memset(attb[:, :], 0.0).then_inc(att0, 1)
                dve.wait_ge(loaded, 16 * n_loads)
                dve.wait_ge(bias_in, 16 * 10)
                chain(nc.vector.tensor_copy(dstf[:, :], dstc[:, :]))
                chain(nc.vector.tensor_tensor(keep[:, :], dstc[:, :], nextc[:, :], ALU.is_equal))
                by_group = "p (g k) -> p g k"
                chain(nc.vector.scalar_tensor_tensor(idx[:, :, 2, :], keep[:, :].rearrange(by_group, k=TILES), float(SKIP),
                                                     dstf[:, :].rearrange(by_group, k=TILES), ALU.mult, ALU.add))
                chain(nc.vector.tensor_copy(idx[:, :, 0, :], srcc[:, :].rearrange(by_group, k=TILES)))
                chain(nc.vector.tensor_copy(idx[:, :, 1, :], dstc[:, :].rearrange(by_group, k=TILES)))
                chain(nc.vector.tensor_copy(befof[:, :], befo[:, :]))
                chain(nc.vector.tensor_copy(rowf[:, 0:3, :], rows[:, 0:3, :]))
                chain(nc.vector.tensor_tensor(mask[:, 0, :], rowf[:, 0, :], rowf[:, 2, :], ALU.not_equal))
                chain(nc.vector.tensor_tensor(mask[:, 1, :], rowf[:, 0, :], rowf[:, 1, :], ALU.not_equal))
                chain(nc.vector.memset(mask[:, 1, :].rearrange("g (k p) -> g k p", p=P)[:, :, 0:1], 1.0))
                chain(nc.vector.tensor_scalar(mask[:, 0:2, :], mask[:, 0:2, :], -BIG, None, ALU.mult))
                for k in range(TILES - 1):
                    nc.vector.tensor_scalar(mask[:, 2, k * P:(k + 1) * P], rowf[:, 0, k * P:(k + 1) * P],
                                            rowf[:, 0, (k + 1) * P:(k + 1) * P + 1], None, ALU.is_equal)
                nc.vector.tensor_scalar(mask[:, 2, (TILES - 1) * P:], rowf[:, 0, (TILES - 1) * P:], befof[:, 0:1], None,
                                        ALU.is_equal).then_inc(mask_ready, 1)
                for parts, rest, full in ((eap[:, :, :, :].rearrange("g a d q -> g a (d q)"), earest[:, :, :].rearrange("g d q -> g (d q)"),
                                           eag[:, :, :].rearrange("g d q -> g (d q)")), (wep[:, :, :], werest[:, :], we[:, :])):
                    chain(nc.vector.tensor_copy(parts[:, 0, :], full))
                    chain(nc.vector.tensor_tensor(rest, full, parts[:, 0, :], ALU.subtract))
                    chain(nc.vector.tensor_copy(parts[:, 1, :], rest))
                    chain(nc.vector.tensor_tensor(rest, rest, parts[:, 1, :], ALU.subtract))
                    chain(nc.vector.tensor_copy(parts[:, 2, :], rest))
                dve.sem_inc(parts_ready, 1)
                chain(nc.vector.tensor_reduce(eas[:, :], eag[:, :, :], AX.X, ALU.add))
                dve.sem_inc(sum_ready, 1)
                dve.wait_ge(mean_sum, 1)
                nc.vector.tensor_scalar(emean[:, :], ps[0:2, 0:1], 1.0 / n_edges, None, ALU.mult).then_inc(mean_ready, 1)
                chain(nc.vector.tensor_tensor(bz, bl, br, ALU.add))
                chain(nc.vector.tensor_scalar(binm1, bin_, -1.0, None, ALU.add))
                chain(nc.vector.tensor_tensor(bc, bconv, bl, ALU.add))
                chain(nc.vector.tensor_scalar(bcm1, bc, -1.0, None, ALU.add))
                chain(nc.vector.tensor_tensor(wsum[:, :], wlr[:, 0, :], wlr[:, 1, :], ALU.add))
                dve.wait_ge(ebias_ready, 1)
                chain(nc.vector.tensor_tensor(bself, bz, ps[:, 1:2], ALU.add))

        with ExitStack() as ctx:
            gidx = [sb(f"gidx{u}", [P, 2, TILES], I32, ctx) for u in range(2)]
            sidx = [sb(f"sidx{u}", [P, TILES], I32, ctx) for u in range(2)]
            xe = [sb(f"xe{u}", [P, 2, TILES, D], F32, ctx) for u in range(2)]
            drow = [sb(f"drow{u}", [P, G], I32, ctx) for u in range(2)]
            frow = [sb(f"frow{u}", [1, G], F32, ctx) for u in range(2)]
            same = [sb(f"same{u}", [P, TILES, P], F32, ctx) for u in range(2)]
            xT = [sb(f"xT{j}", [P, G], F32, ctx) for j in range(2)]
            mT = sb("mT", [P, G], F32, ctx)
            mu = [sb(f"mu{u}", [P, TILES, D + 1], F32, ctx) for u in range(2)]
            carry = [sb(f"carry{j}", [1, D + 1], F32, ctx) for j in range(2)]
            rcnt = sb("rcnt", [P, TILES], F32, ctx)
            osum = [sb(f"osum{u}", [P, TILES, D], F32, ctx) for u in range(2)]
            ps_x = [pb(f"ps_x{j}", ctx=ctx) for j in range(2)]
            ps_m, ps_u = pb("ps_m", ctx=ctx), pb("ps_u", ctx=ctx)
            ps_a = [pb(f"ps_a{k}", ctx=ctx) for k in range(TILES)]

            gidx_set, sidx_set = sem2("gidx_set"), sem2("sidx_set")
            gathered, scattered, rows_in = sem2("gathered"), sem2("scattered"), sem2("rows_in")
            gathered_t = [sem2(f"xposed{j}_") for j in range(2)]
            xT_ready = [sem(f"xT_ready{j}") for j in range(2)]
            m_ps, m_sb, u_ps, u_sb = sem("m_ps"), sem("m_sb"), sem("u_ps"), sem("u_sb")
            same_ready, agg_ps, carry_ready = sem2("same_ready"), sem("agg_ps"), sem("carry_ready")
            osum_ready = sem2("osum_ready")
            init = sem("init_p1")
            rc = sem("rcnt_ready")
            block = ctx.enter_context(nc.Block())

            @block.sync
            def _(sp):
                def group(i, u):
                    g = i * 2 + u
                    need(sp, same_ready[u], i, gate_sp)
                    need(sp, agg_ps, (g - 1) * TILES, gate_sp)
                    sp.dma_start(drow[u][:, :], dst_row[bass.ds(g, 1), :].rearrange("o q -> (o q)").partition_broadcast(P)
                                 ).then_inc(rows_in[u], 16)
                    sp.dma_start(frow[u][:, :], masks[bass.ds(g, 1), 2, :]).then_inc(rows_in[u], 16)
                run_groups(sp, group, EG)

            @block.gpsimd
            def _(pool):
                def hold(sem_, value):
                    need(pool, sem_, value, gate)

                def gather(i, u):
                    g = i * 2 + u
                    for j in range(2):
                        hold(gathered_t[j][u], i)
                    hold(gathered[u], i * (16 * 2 * TILES))
                    nc.gpsimd.tensor_copy(gidx[u][:, :, :], idx[:, bass.ds(g, 1), 0:2, :].rearrange("p o j k -> p (o j) k")
                                          ).then_inc(gidx_set[u], 1)
                    hold(gidx_set[u], i + 1)
                    for j in range(2):
                        for k in reversed(range(TILES)):
                            pool.indirect_dma_start(
                                out=xe[u][:, j, k, :], out_offset=None, in_=x,
                                in_offset=bass.IndirectOffsetOnAxis(ap=gidx[u][:, j, k:k + 1], axis=0)).then_inc(gathered[u], 16)

                def scatter(i, u):
                    g = i * 2 + u
                    hold(scattered[u], i * (16 * TILES))
                    nc.gpsimd.tensor_copy(sidx[u][:, :], idx[:, bass.ds(g, 1), 2, :].rearrange("p o k -> p (o k)")
                                          ).then_inc(sidx_set[u], 1)
                    hold(sidx_set[u], i + 1)
                    hold(osum_ready[u], i + 1)
                    for k in range(TILES):
                        pool.indirect_dma_start(
                            out=sums0, out_offset=bass.IndirectOffsetOnAxis(ap=sidx[u][:, k:k + 1], axis=0),
                            in_=osum[u][:, k, :], in_offset=None, bounds_check=NP - 1, oob_is_err=False).then_inc(scattered[u], 16)

                for u in range(2):
                    gather(0, u)
                with pool.Fori(1, EHALF) as i:
                    for u in range(2):
                        scatter(i - 1, u)
                        gather(i, u)
                for u in range(2):
                    scatter(EHALF - 1, u)
                for u in range(2):
                    pool.wait_ge(scattered[u], 16 * TILES * EHALF)

            @block.tensor
            def _(pe):
                pe.wait_ge(init, 1)

                def group(i, u):
                    g = i * 2 + u
                    pe.wait_ge(gathered[u], (i + 1) * (16 * 2 * TILES))
                    for j in range(2):
                        need(pe, xT_ready[j], g)
                        for k in range(TILES):
                            last = nc.tensor.transpose(ps_x[j][:, k * P:(k + 1) * P], xe[u][:, j, k, :], ident[:, :])
                        last.then_inc(gathered_t[j][u], 1)
                    pe.wait_ge(xT_ready[0], g + 1)
                    need(pe, m_sb, g)
                    nc.tensor.matmul(ps_m[:, :], wm[:, 0, :], xT[0][:, :], start=True, stop=False)
                    pe.wait_ge(xT_ready[1], g + 1)
                    nc.tensor.matmul(ps_m[:, :], wm[:, 1, :], xT[1][:, :], start=False, stop=True).then_inc(m_ps, 1)
                    pe.wait_ge(m_sb, g + 1)
                    need(pe, u_sb, g)
                    for k in range(TILES):
                        last = nc.tensor.matmul(ps_u[:, k * D:(k + 1) * D], mT[:, k * P:(k + 1) * P], wu[:, 1, :],
                                                start=True, stop=True)
                    last.then_inc(u_ps, 1)
                    pe.wait_ge(same_ready[u], i + 1)
                    pe.wait_ge(u_sb, g + 1)
                    pe.wait_ge(rows_in[u], (i + 1) * 32)
                    need(pe, osum_ready[1 - u], i + u)
                    for n, k in enumerate(reversed(range(TILES))):
                        nc.tensor.matmul(ps_a[k][:, 0:D + 1], same[u][:, k, :], mu[u][:, k, :], start=True, stop=False)
                        t = g * TILES + n
                        need(pe, carry_ready, t)
                        nc.tensor.matmul(ps_a[k][:, 0:D + 1], frow[u][:, k * P:(k + 1) * P], carry[(n + 1) % 2][:, :],
                                         start=False, stop=True).then_inc(agg_ps, 1)
                run_groups(pe, group, EG)

            @block.scalar
            def _(act):
                def group(i, u):
                    g = i * 2 + u
                    act.wait_ge(gathered_t[0][u], i + 1)
                    need(act, m_ps, g)
                    nc.scalar.activation(xT[0][:, :], ps_x[0][:, :], ACT.Copy).then_inc(xT_ready[0], 1)
                    act.wait_ge(m_ps, g + 1)
                    need(act, u_ps, g)
                    nc.scalar.activation(mT[:, :], ps_m[:, :], ACT.Relu, bias=bmsg).then_inc(m_sb, 1)
                    for n, k in enumerate(reversed(range(TILES))):
                        act.wait_ge(agg_ps, g * TILES + (n + 1))
                        nc.scalar.activation(carry[n % 2][:, :], ps_a[k][0:1, 0:D + 1], ACT.Copy).then_inc(carry_ready, 1)
                run_groups(act, group, EG)

            @block.vector
            def _(dve):
                for u in range(2):
                    nc.vector.memset(mu[u][:, :, :], 1.0)
                nc.vector.memset(carry[0][:, :], 0.0)
                nc.vector.memset(carry[1][:, :], 0.0).then_inc(init, 1)
                dve.wait_ge(init, 1)

                def group(i, u):
                    g = i * 2 + u
                    dve.wait_ge(rows_in[u], (i + 1) * 32)
                    need(dve, agg_ps, (g - 1) * TILES)
                    nc.vector.tensor_tensor(same[u][:, :, :], drow[u][:, :].rearrange("p (k q) -> p k q", k=TILES),
                                            dstf[:, bass.ds(g * TILES, TILES)].unsqueeze(2).broadcast_to([P, TILES, P]),
                                            ALU.is_equal).then_inc(same_ready[u], 1)
                    dve.wait_ge(gathered_t[1][u], i + 1)
                    need(dve, m_ps, g)
                    nc.vector.tensor_copy(xT[1][:, :], ps_x[1][:, :]).then_inc(xT_ready[1], 1)
                    dve.wait_ge(u_ps, g + 1)
                    nc.vector.tensor_copy(mu[u][:, :, 0:D], ps_u[:, :].rearrange("p (k d) -> p k d", k=TILES)).then_inc(u_sb, 1)
                    need(dve, scattered[u], i * (16 * TILES))
                    for n, k in enumerate(reversed(range(TILES))):
                        dve.wait_ge(carry_ready, g * TILES + (n + 1))
                        nc.vector.reciprocal(rcnt[:, k:k + 1], ps_a[k][:, D:D + 1]).then_inc(rc, 1)
                        dve.wait_ge(rc, g * TILES + (n + 1))
                        last = nc.vector.tensor_scalar(osum[u][:, k, :], ps_a[k][:, 0:D], rcnt[:, k:k + 1], None, ALU.mult)
                    last.then_inc(osum_ready[u], 1)
                run_groups(dve, group, EG)

        with ExitStack() as ctx:
            xn = [sb(f"xn{u}", [P, TILES, D], F32, ctx) for u in range(2)]
            sn = [sb(f"sn{u}", [P, TILES, D], F32, ctx) for u in range(2)]
            xT = sb("xTn", [P, G], F32, ctx)
            hb, neg = sb("hb", [P, G], F32, ctx), sb("neg", [P, G], F32, ctx)
            hT = [sb(f"hT{u}", [P, G], F32, ctx) for u in range(2)]
            ps_x, ps_h = [pb(f"ps_xn{u}", ctx=ctx) for u in range(2)], [pb(f"ps_hn{u}", ctx=ctx) for u in range(2)]
            rows_in, stored = sem2("n1_in"), sem2("n1_stored")
            xt_ps, xt_sb, h_ps, h_sb, stat = sem("n1_xt_ps"), sem("n1_xt_sb"), sem("n1_h_ps"), sem("n1_h_sb"), sem("n1_stat")
            hb_sb, neg_sb, bn_step = sem("n1_hb"), sem("n1_neg"), sem("bn_step")
            block = ctx.enter_context(nc.Block())

            @block.sync
            def _(sp):
                def group(i, u):
                    g = i * 2 + u
                    need(sp, h_ps, g - 1, gate_sp)
                    sp.dma_start(xn[u][:, :, :], group_rows(x, g, D)).then_inc(rows_in[u], 16)
                    sp.dma_start(sn[u][:, :, :], group_rows(sums0, g, D)).then_inc(rows_in[u], 16)
                run_groups(sp, group, GROUPS)

            @block.gpsimd
            def _(pool):
                def group(i, u):
                    g = i * 2 + u
                    pool.wait_ge(h_sb, g + 1)
                    pool.sem_inc(gate, 1)
                    pool.dma_start(h_t[:, bass.ds(g * G, G)], hT[u][:, :]).then_inc(stored[u], 16)
                run_groups(pool, group, GROUPS)
                for u in range(2):
                    pool.wait_ge(stored[u], 16 * HALF)

            @block.tensor
            def _(pe):
                def group(i, u):
                    g = i * 2 + u
                    pe.wait_ge(rows_in[u], (i + 1) * 32)
                    need(pe, xt_sb, g - 1)
                    for k in range(TILES):
                        last = nc.tensor.transpose(ps_x[u][:, k * P:(k + 1) * P], xn[u][:, k, :], ident[:, :])
                    last.then_inc(xt_ps, 1)
                    pe.wait_ge(xt_sb, g + 1)
                    need(pe, hb_sb, g - 1)
                    nc.tensor.matmul(ps_h[u][:, :], wu[:, 0, :], xT[:, :], start=True, stop=False)
                    for k in range(TILES):
                        last = nc.tensor.matmul(ps_h[u][:, k * P:(k + 1) * P], sn[u][:, k, :], ident[:, :],
                                                start=False, stop=k == TILES - 1)
                    last.then_inc(h_ps, 1)
                run_groups(pe, group, GROUPS)

            @block.scalar
            def _(act):
                def group(i, u):
                    g = i * 2 + u
                    act.wait_ge(xt_ps, g + 1)
                    need(act, h_ps, g)
                    nc.scalar.activation(xT[:, :], ps_x[u][:, :], ACT.Copy).then_inc(xt_sb, 1)
                    act.wait_ge(h_ps, g + 1)
                    need(act, h_sb, g)
                    nc.scalar.activation(hb[:, :], ps_h[u][:, :], ACT.Identity, bias=bupd).then_inc(hb_sb, 1)
                run_groups(act, group, GROUPS)

            @block.vector
            def _(dve):
                def group(i, u, valid=P):
                    g = i * 2 + u
                    dve.wait_ge(hb_sb, g + 1)
                    nc.vector.tensor_scalar(neg[:, :], hb[:, :], 0.0, alpha, ALU.min, ALU.mult).then_inc(neg_sb, 1)
                    dve.wait_ge(neg_sb, g + 1)
                    need(dve, stored[u], i * 16)
                    nc.vector.scalar_tensor_tensor(hT[u][:, :], hb[:, :], 0.0, neg[:, :], ALU.max, ALU.add).then_inc(h_sb, 1)
                    dve.wait_ge(h_sb, g + 1)
                    dve.sem_inc(gate_dve, 1)
                    if valid == P:
                        nc.vector.bn_stats(bn[:, bass.ds(g, 1), :].rearrange("p o s -> p (o s)"), hT[u][:, :]).then_inc(stat, 1)
                    else:
                        for k in range(TILES):
                            last = nc.vector.bn_stats(bn[:, g + k, :], hT[u][:, k * P:k * P + valid])
                        last.then_inc(stat, 1)
                for u in range(2):
                    group(0, u)
                with dve.Fori(1, HALF - 1) as i:
                    for u in range(2):
                        group(i, u)
                group(HALF - 1, 0)
                group(HALF - 1, 1, VALID // TILES)
                n = [0]

                def chain(ins):
                    n[0] += 1
                    ins.then_inc(bn_step, 1)
                    dve.wait_ge(bn_step, n[0])
                dve.wait_ge(stat, GROUPS)
                chain(nc.vector.bn_aggr(bnmv[:, :], bn[:, :, :].rearrange("p g s -> p (g s)")))
                inv_sqrt(nc, chain, bn_scale, bnmv[:, 1:2], cols2[:, 5:6])
                chain(nc.vector.tensor_tensor(bn_scale, bn_scale, gam, ALU.mult))
                chain(nc.vector.tensor_tensor(bn_shift, bnmv[:, 0:1], bn_scale, ALU.mult))
                chain(nc.vector.tensor_tensor(bn_shift, bet, bn_shift, ALU.subtract))

        with ExitStack() as ctx:
            xn = [sb(f"xn2{u}", [P, TILES, D], F32, ctx) for u in range(2)]
            hT = [sb(f"hT2{u}", [P, G], F32, ctx) for u in range(2)]
            yT = sb("yT", [P, G], F32, ctx)
            r = sb("r2", [P, TILES, D], F32, ctx)
            x1 = [sb(f"x1{u}", [P, TILES, D], F32, ctx) for u in range(2)]
            x1T = sb("x1T", [P, G], F32, ctx)
            ex, lin, el = sb("ex2", [P, G], F32, ctx), sb("lin2", [P, G], F32, ctx), sb("el2", [P, G], F32, ctx)
            zb, zs = sb("zb", [P, G], F32, ctx), sb("zs", [P, G], F32, ctx)
            xl = [sb(f"xlo{u}", [P, TILES, ROW3], F32, ctx) for u in range(2)]
            xr = [sb(f"xro{u}", [P, TILES, D], F32, ctx) for u in range(2)]
            stats, mv = sb("st2", [P, TILES, 6], F32, ctx), sb("mv2", [P, TILES, 2], F32, ctx)
            rstd, nshift = sb("rstd2", [P, TILES], F32, ctx), sb("nsh2", [P, TILES], F32, ctx)
            ps_y, ps_t, ps_h, ps_z = pb("ps_y", ctx=ctx), pb("ps_t", ctx=ctx), pb("ps_h", ctx=ctx), pb("ps_z", ctx=ctx)
            ps_l, ps_r, ps_s = pb("ps_l", ctx=ctx), pb("ps_r", ctx=ctx), pb("ps_s", ctx=ctx)
            rows_in = sem2("n2_in")
            st_x1, st_l, st_r = sem2("n2_st_x1"), sem2("n2_st_l"), sem2("n2_st_r")
            yt, y_ps, r_sb, nrm, x1_sb, x1t_ps, x1t_sb, h_ps = (sem("n2_" + s) for s in
                ("yt", "y_ps", "r_sb", "nrm", "x1_sb", "x1t_ps", "x1t_sb", "h_ps"))
            ex_sb, lin_sb, el_sb, lr_ps, z_ps, z_sb, s_ps, l_sb, r2_sb = (sem("n2_" + s) for s in
                ("ex_sb", "lin_sb", "el_sb", "lr_ps", "z_ps", "z_sb", "s_ps", "l_sb", "r2_sb"))
            zb_sb = sem("n2_zb")
            dstep = sem("n2_step")
            block = ctx.enter_context(nc.Block())

            @block.sync
            def _(sp):
                def group(i, u):
                    g = i * 2 + u
                    need(sp, r_sb, g - 1, gate_sp)
                    need(sp, yt, g - 1, gate_sp)
                    sp.dma_start(hT[u][:, :], h_t[:, bass.ds(g * G, G)]).then_inc(rows_in[u], 16)
                    sp.dma_start(xn[u][:, :, :], group_rows(x, g, D)).then_inc(rows_in[u], 16)
                run_groups(sp, group, GROUPS)

            @block.gpsimd
            def _(pool):
                def group(i, u):
                    g = i * 2 + u
                    pool.wait_ge(x1_sb, g + 1)
                    pool.sem_inc(gate, 1)
                    pool.dma_start(group_rows(x1_t, g, D), x1[u][:, :, :]).then_inc(st_x1[u], 16)
                    pool.wait_ge(r2_sb, g + 1)
                    pool.sem_inc(gate, 1)
                    pool.dma_start(group_rows(xr_t, g, D), xr[u][:, :, :]).then_inc(st_r[u], 16)
                    pool.wait_ge(l_sb, g * 2 + 2)
                    pool.sem_inc(gate, 1)
                    pool.dma_start(group_rows(xl_t, g, ROW3), xl[u][:, :, :]).then_inc(st_l[u], 16)
                run_groups(pool, group, GROUPS)
                for u in range(2):
                    for s in (st_x1[u], st_l[u], st_r[u]):
                        pool.wait_ge(s, 16 * HALF)

            @block.tensor
            def _(pe):
                def turn_y(i, u):
                    g = i * 2 + u
                    pe.wait_ge(yt, g + 1)
                    need(pe, r_sb, g)
                    for k in range(TILES):
                        last = nc.tensor.transpose(ps_y[:, k * P:(k + 1) * P], yT[:, k * P:(k + 1) * P], ident[:, :])
                    last.then_inc(y_ps, 1)

                def turn_x1(i, u):
                    g = i * 2 + u
                    pe.wait_ge(x1_sb, g + 1)
                    need(pe, x1t_sb, g)
                    for k in range(TILES):
                        last = nc.tensor.transpose(ps_t[:, k * P:(k + 1) * P], x1[u][:, k, :], ident[:, :])
                    last.then_inc(x1t_ps, 1)

                def hidden(i, u):
                    g = i * 2 + u
                    pe.wait_ge(x1t_sb, g + 1)
                    need(pe, lin_sb, g)
                    nc.tensor.matmul(ps_h[:, :], win[:, :], x1T[:, :], start=True, stop=True).then_inc(h_ps, 1)

                def left_right(i, u):
                    g = i * 2 + u
                    pe.wait_ge(el_sb, g + 1)
                    need(pe, zb_sb, g)
                    nc.tensor.matmul(ps_z[:, :], wsum[:, :], el[:, :], start=True, stop=True).then_inc(z_ps, 1)
                    need(pe, l_sb, g * 2)
                    for k in range(TILES):
                        nc.tensor.matmul(ps_l[:, k * D:(k + 1) * D], el[:, k * P:(k + 1) * P], wlr[:, 0, :], start=True, stop=True)
                    need(pe, r2_sb, g)
                    for k in range(TILES):
                        last = nc.tensor.matmul(ps_r[:, k * D:(k + 1) * D], el[:, k * P:(k + 1) * P], wlr[:, 1, :],
                                                start=True, stop=True)
                    last.then_inc(lr_ps, 1)

                def scores(i, u):
                    g = i * 2 + u
                    pe.wait_ge(z_sb, g + 1)
                    need(pe, l_sb, g * 2)
                    for k in range(TILES):
                        last = nc.tensor.matmul(ps_s[:, k * HEADS:(k + 1) * HEADS], zs[:, k * P:(k + 1) * P], attb[:, :],
                                                start=True, stop=True)
                    last.then_inc(s_ps, 1)
                run_stages(pe, [(turn_x1, 1), (turn_y, 0), (left_right, 2), (hidden, 1), (scores, 2)], GROUPS)

            @block.scalar
            def _(act):
                def batch_norm(i, u):
                    g = i * 2 + u
                    act.wait_ge(rows_in[u], (i + 1) * 32)
                    need(act, y_ps, g)
                    nc.scalar.activation(yT[:, :], hT[u][:, :], ACT.Identity, bias=bn_shift, scale=bn_scale).then_inc(yt, 1)

                def normalise(i, u):
                    g = i * 2 + u
                    act.wait_ge(nrm, g + 1)
                    need(act, st_x1[u], i * 16)
                    need(act, x1t_ps, g - 1)
                    for k in range(TILES):
                        last = nc.scalar.activation(x1[u][:, k, :], r[:, k, :], ACT.Identity, bias=nshift[:, k:k + 1],
                                                    scale=rstd[:, k:k + 1])
                    last.then_inc(x1_sb, 1)

                def exponentials(i, u):
                    g = i * 2 + u
                    act.wait_ge(h_ps, g + 1)
                    need(act, el_sb, g)
                    nc.scalar.activation(ex[:, :], ps_h[:, :], ACT.Exp, bias=bin_).then_inc(ex_sb, 1)

                def results(i, u):
                    g = i * 2 + u
                    act.wait_ge(z_ps, g + 1)
                    need(act, z_sb, g)
                    nc.scalar.activation(zb[:, :], ps_z[:, :], ACT.Identity, bias=bself).then_inc(zb_sb, 1)
                    act.wait_ge(lr_ps, g + 1)
                    need(act, st_l[u], i * 16)
                    nc.scalar.activation(xl[u][:, :, 0:D], ps_l[:, :].rearrange("p (k d) -> p k d", k=TILES), ACT.Copy
                                         ).then_inc(l_sb, 1)
                    act.wait_ge(s_ps, g + 1)
                    nc.scalar.activation(xl[u][:, :, D:ROW3], ps_s[:, 0:TILES * HEADS].rearrange("p (k h) -> p k h", k=TILES),
                                         ACT.Copy).then_inc(l_sb, 1)
                run_stages(act, [(normalise, 1), (exponentials, 2), (batch_norm, 0), (results, 2)], GROUPS)

            @block.vector
            def _(dve):
                def elu(i, u):
                    g = i * 2 + u
                    dve.wait_ge(ex_sb, g + 1)
                    nc.vector.tensor_scalar(lin[:, :], ps_h[:, :], binm1, -1.0, ALU.add, ALU.max).then_inc(lin_sb, 1)
                    dve.wait_ge(lin_sb, g + 1)
                    need(dve, lr_ps, g)
                    nc.vector.scalar_tensor_tensor(el[:, :], ex[:, :], 1.0, lin[:, :], ALU.min, ALU.add).then_inc(el_sb, 1)

                def copy_x1t(i, u):
                    g = i * 2 + u
                    dve.wait_ge(x1t_ps, g + 1)
                    need(dve, h_ps, g)
                    nc.vector.tensor_copy(x1T[:, :], ps_t[:, :]).then_inc(x1t_sb, 1)

                def residual(i, u):
                    g = i * 2 + u
                    n = [0]

                    def chain(ins):
                        n[0] += 1
                        ins.then_inc(dstep, 1)
                        dve.wait_ge(dstep, g * LN_STEPS + n[0])
                    dve.wait_ge(y_ps, g + 1)
                    dve.wait_ge(rows_in[u], (i + 1) * 32)
                    need(dve, x1_sb, g)
                    nc.vector.tensor_tensor(r[:, :, :], xn[u][:, :, :], ps_y[:, :].rearrange("p (k d) -> p k d", k=TILES),
                                            ALU.add).then_inc(r_sb, 1)
                    dve.wait_ge(r_sb, g + 1)
                    layer_norm(nc, dve, gate_dve, chain, r, stats, mv, rstd[:, :], nshift[:, :]).then_inc(nrm, 1)
                    assert n[0] == LN_STEPS, n[0]

                def leak(i, u):
                    g = i * 2 + u
                    dve.wait_ge(zb_sb, g + 1)
                    need(dve, s_ps, g)
                    nc.vector.scalar_tensor_tensor(zs[:, :], zb[:, :], SLOPE, zb[:, :], ALU.mult, ALU.max).then_inc(z_sb, 1)

                def copy_xr(i, u):
                    g = i * 2 + u
                    dve.wait_ge(lr_ps, g + 1)
                    need(dve, st_r[u], i * 16)
                    nc.vector.tensor_copy(xr[u][:, :, :], ps_r[:, :].rearrange("p (k d) -> p k d", k=TILES)).then_inc(r2_sb, 1)
                run_stages(dve, [(elu, 2), (copy_x1t, 1), (residual, 0), (leak, 2), (copy_xr, 2)], GROUPS)

        with ExitStack() as ctx:
            gidx = [sb(f"gidxa{u}", [P, 2, TILES], I32, ctx) for u in range(2)]
            sidx = [sb(f"sidxa{u}", [P, TILES], I32, ctx) for u in range(2)]
            gl = [sb(f"gl{u}", [P, TILES, ROW3], F32, ctx) for u in range(2)]
            gr = [sb(f"gr{u}", [P, TILES, D], F32, ctx) for u in range(2)]
            drow = [sb(f"drowa{u}", [P, G], I32, ctx) for u in range(2)]
            frow = [sb(f"frowa{u}", [1, G], F32, ctx) for u in range(2)]
            reset = [sb(f"reset{u}", [HEADS, 2, G], F32, ctx) for u in range(2)]
            ea = [sb(f"ea{u}", [PAIRS * 2, G], BF16, ctx) for u in range(2)]
            same = [sb(f"samea{u}", [P, TILES, P], F32, ctx) for u in range(2)]
            zr = sb("zr", [P, TILES, D], F32, ctx)
            eT = sb("eT", [P, G], F32, ctx)
            zb, zT = sb("zba", [P, G], F32, ctx), sb("zT", [P, G], F32, ctx)
            run = sb("run", [HEADS, G], F32, ctx)
            mx = [sb(f"mx{u}", [HEADS, G + 1], F32, ctx) for u in range(2)]
            off = sb("off", [HEADS, G], F32, ctx)
            dcar = sb("dcar", [HEADS, TILES], F32, ctx)
            ecar = sb("ecar", [1, TILES * HEADS], F32, ctx)
            ecx = [sb(f"ecx{u}", [1, TILES, ROW3], F32, ctx) for u in range(2)]
            pay = [sb(f"pay{u}", [P, TILES, ROW3], F32, ctx) for u in range(2)]
            carry = [sb(f"carrya{j}", [1, ROW3], F32, ctx) for j in range(2)]
            carrs = sb("carrs", [1, ROW3], F32, ctx)
            osum = [sb(f"osuma{u}", [P, TILES, ROWA], F32, ctx) for u in range(2)]
            ps_z, ps_al, ps_t = pb("psa_z", ctx=ctx), pb("psa_al", ctx=ctx), pb("psa_t", ctx=ctx)
            ps_e = pb("psa_e", ctx=ctx)
            ps_a = [pb(f"psa_a{k}", ctx=ctx) for k in range(TILES)]
            WE, WM, WC = 0, TILES * HEADS, 2 * TILES * HEADS

            gidx_set, sidx_set = sem2("a_gidx_set"), sem2("a_sidx_set")
            gathered, scattered, rows_in = sem2("a_gathered"), sem2("a_scattered"), sem2("a_rows_in")
            z_ps, z_sb, al_ps, off_sb, mx_sb, t_ps = (sem("a_" + s) for s in ("z_ps", "z_sb", "al_ps", "off_sb", "mx_sb", "t_ps"))
            e_ps, e_sb, zr_sb = sem("a_e_ps"), sem("a_e_sb"), sem("a_zr")
            w_sb, ecar_sb, ecx_sb, pay_sb, max_out = (sem("a_" + s) for s in ("w_sb", "ecar_sb", "ecx_sb", "pay_sb", "max_out"))
            same_ready, agg_ps, carry_ready, carry_scaled = sem2("a_same"), sem("a_agg_ps"), sem("a_carry"), sem("a_carrs")
            osum_ready, run_sb, dcar_sb = sem2("a_osum"), sem("a_run"), sem("a_dcar")
            init, zb_sb = sem("a_init"), sem("a_zb")
            block = ctx.enter_context(nc.Block())

            @block.sync
            def _(sp):
                def group(i, u):
                    g = i * 2 + u
                    need(sp, same_ready[u], i, gate_sp)
                    need(sp, agg_ps, (g - 1) * TILES, gate_sp)
                    need(sp, mx_sb, g - 1, gate_sp)
                    sp.dma_start(drow[u][:, :], dst_row[bass.ds(g, 1), :].rearrange("o q -> (o q)").partition_broadcast(P)
                                 ).then_inc(rows_in[u], 16)
                    sp.dma_start(frow[u][:, :], masks[bass.ds(g, 1), 2, :]).then_inc(rows_in[u], 16)
                    sp.dma_start(reset[u][:, :, :], masks[bass.ds(g, 1), 0:2, :].rearrange("o j q -> (o j) q").partition_broadcast(HEADS)
                                 ).then_inc(rows_in[u], 16)
                    sp.dma_start(ea[u][:, :], ea_parts[bass.ds(g, 1), :, :].rearrange("o j q -> (o j) q")).then_inc(rows_in[u], 16)
                run_groups(sp, group, EG)

            @block.gpsimd
            def _(pool):
                def hold(sem_, value):
                    need(pool, sem_, value, gate)

                def gather(i, u):
                    g = i * 2 + u
                    hold(pay_sb, g - 1)
                    hold(gathered[u], i * (16 * 2 * TILES))
                    nc.gpsimd.tensor_copy(gidx[u][:, :, :], idx[:, bass.ds(g, 1), 0:2, :].rearrange("p o j k -> p (o j) k")
                                          ).then_inc(gidx_set[u], 1)
                    hold(gidx_set[u], i + 1)
                    for table, rows, j in ((xl_t, gl, 0), (xr_t, gr, 1)):
                        for k in range(TILES):
                            pool.indirect_dma_start(
                                out=rows[u][:, k, :], out_offset=None, in_=table,
                                in_offset=bass.IndirectOffsetOnAxis(ap=gidx[u][:, j, k:k + 1], axis=0)).then_inc(gathered[u], 16)

                def scatter(i, u):
                    g = i * 2 + u
                    hold(scattered[u], i * (16 * TILES))
                    nc.gpsimd.tensor_copy(sidx[u][:, :], idx[:, bass.ds(g, 1), 2, :].rearrange("p o k -> p (o k)")
                                          ).then_inc(sidx_set[u], 1)
                    hold(sidx_set[u], i + 1)
                    hold(osum_ready[u], i + 1)
                    for k in range(TILES):
                        pool.indirect_dma_start(
                            out=sums1, out_offset=bass.IndirectOffsetOnAxis(ap=sidx[u][:, k:k + 1], axis=0),
                            in_=osum[u][:, k, :], in_offset=None, bounds_check=NP - 1, oob_is_err=False).then_inc(scattered[u], 16)

                run_stages(pool, [(scatter, 3), (gather, 0)], EG)
                for u in range(2):
                    pool.wait_ge(scattered[u], 16 * TILES * EHALF)

            @block.tensor
            def _(pe):
                pe.wait_ge(init, 1)

                def edge_term(i, u):
                    g = i * 2 + u
                    pe.wait_ge(rows_in[u], (i + 1) * 64)
                    need(pe, e_sb, g)
                    nc.tensor.matmul(ps_e[:, :], we18[:, :], ea[u][:, :], start=True, stop=True).then_inc(e_ps, 1)

                def turn(i, u):
                    g = i * 2 + u
                    pe.wait_ge(zr_sb, g + 1)
                    need(pe, zb_sb, g)
                    for k in range(TILES):
                        last = nc.tensor.transpose(ps_z[:, k * P:(k + 1) * P], zr[:, k, :], ident[:, :])
                    last.then_inc(z_ps, 1)

                def scores(i, u):
                    g = i * 2 + u
                    pe.wait_ge(z_sb, g + 1)
                    need(pe, off_sb, g)
                    nc.tensor.matmul(ps_al[0:HEADS, :], attb[:, :], zT[:, :], start=True, stop=True).then_inc(al_ps, 1)

                def turn_back(i, u):
                    g = i * 2 + u
                    pe.wait_ge(off_sb, g + 1)
                    pe.wait_ge(dcar_sb, g * 2 + 2)
                    need(pe, max_out, g)
                    pe.sem_inc(gate_pe, 1)
                    for k in range(TILES):
                        nc.tensor.transpose(ps_t[:, WE + k * HEADS:WE + (k + 1) * HEADS], off[:, k * P:(k + 1) * P],
                                            ident[0:HEADS, 0:HEADS])
                        nc.tensor.transpose(ps_t[:, WM + k * HEADS:WM + (k + 1) * HEADS], mx[u][:, k * P:(k + 1) * P],
                                            ident[0:HEADS, 0:HEADS])
                    for k in range(TILES):
                        last = nc.tensor.transpose(ps_t[0:1, WC + k * HEADS:WC + (k + 1) * HEADS], dcar[:, k:k + 1],
                                                   ident[0:HEADS, 0:HEADS])
                    last.then_inc(t_ps, 1)

                def sums(n):
                    k = TILES - 1 - n

                    def stage(i, u):
                        g = i * 2 + u
                        if n == 0:
                            pe.wait_ge(same_ready[u], i + 1)
                            pe.wait_ge(pay_sb, g + 1)
                            need(pe, osum_ready[1 - u], i + u)
                        nc.tensor.matmul(ps_a[k][:, 0:ROW3], same[u][:, k, :], pay[u][:, k, :], start=True, stop=False)
                        pe.wait_ge(carry_scaled, g * TILES + (n + 1))
                        nc.tensor.matmul(ps_a[k][:, 0:ROW3], frow[u][:, k * P:(k + 1) * P], carrs[:, :],
                                         start=False, stop=True).then_inc(agg_ps, 1)
                    return stage
                run_stages(pe, [(edge_term, 0), (sums(0), 1), (turn, 0), (sums(1), 1), (sums(2), 1), (scores, 0),
                                (sums(3), 1), (turn_back, 0)], EG)

            @block.scalar
            def _(act):
                def edge_term(i, u):
                    g = i * 2 + u
                    act.wait_ge(e_ps, g + 1)
                    need(act, zb_sb, g)
                    nc.scalar.activation(eT[:, :], ps_e[:, :], ACT.Identity, bias=bz).then_inc(e_sb, 1)

                def results(i, u):
                    g = i * 2 + u
                    for n, k in enumerate(reversed(range(TILES))):
                        act.wait_ge(carry_ready, g * TILES + (n + 1))
                        last = nc.scalar.activation(osum[u][:, k, 0:ROW3], ps_a[k][:, 0:ROW3], ACT.Copy)
                    last.then_inc(osum_ready[u], 1)

                def weights(i, u):
                    g = i * 2 + u
                    act.wait_ge(t_ps, g + 1)
                    need(act, agg_ps, (g - 1) * TILES)
                    nc.scalar.activation(pay[u][:, :, D:ROW3], ps_t[:, WE:WE + TILES * HEADS].rearrange("p (k h) -> p k h", k=TILES),
                                         ACT.Exp).then_inc(w_sb, 1)
                    need(act, ecx_sb, g)
                    nc.scalar.activation(ecar[:, :], ps_t[0:1, WC:WC + TILES * HEADS], ACT.Exp).then_inc(ecar_sb, 1)
                    need(act, scattered[u], i * (16 * TILES))
                    nc.scalar.activation(osum[u][:, :, ROW3:ROWA], ps_t[:, WM:WM + TILES * HEADS].rearrange("p (k h) -> p k h", k=TILES),
                                         ACT.Copy).then_inc(max_out, 1)
                run_stages(act, [(edge_term, 0), (results, 1), (weights, 0)], EG)

            @block.vector
            def _(dve):
                nc.vector.memset(mx[0][:, :], 0.0)
                nc.vector.memset(mx[1][:, :], 0.0)
                nc.vector.memset(carry[0][:, :], 0.0)
                nc.vector.memset(carry[1][:, :], 0.0).then_inc(init, 1)
                dve.wait_ge(init, 1)

                def add_rows(i, u):
                    g = i * 2 + u
                    dve.wait_ge(gathered[u], (i + 1) * (16 * 2 * TILES))
                    need(dve, z_ps, g)
                    nc.vector.tensor_tensor(zr[:, :, :], gl[u][:, :, 0:D], gr[u][:, :, :], ALU.add).then_inc(zr_sb, 1)

                def compare(i, u):
                    g = i * 2 + u
                    dve.wait_ge(rows_in[u], (i + 1) * 64)
                    need(dve, agg_ps, (g - 1) * TILES)
                    nc.vector.tensor_tensor(same[u][:, :, :], drow[u][:, :].rearrange("p (k q) -> p k q", k=TILES),
                                            dstf[:, bass.ds(g * TILES, TILES)].unsqueeze(2).broadcast_to([P, TILES, P]),
                                            ALU.is_equal).then_inc(same_ready[u], 1)

                def leak(i, u):
                    g = i * 2 + u
                    dve.wait_ge(z_ps, g + 1)
                    dve.wait_ge(e_sb, g + 1)
                    need(dve, z_sb, g)
                    nc.vector.tensor_tensor(zb[:, :], eT[:, :], ps_z[:, :], ALU.add).then_inc(zb_sb, 1)
                    dve.wait_ge(zb_sb, g + 1)
                    need(dve, al_ps, g)
                    nc.vector.scalar_tensor_tensor(zT[:, :], zb[:, :], SLOPE, zb[:, :], ALU.mult, ALU.max).then_inc(z_sb, 1)

                def running_maximum(i, u):
                    g = i * 2 + u
                    dve.wait_ge(al_ps, g + 1)
                    nc.vector.tensor_tensor_scan(run[:, ::-1], reset[u][:, 0, ::-1], ps_al[0:HEADS, ::-1], mx[1 - u][:, 0:1],
                                                 ALU.add, ALU.max).then_inc(run_sb, 1)

                def maxima(i, u):
                    g = i * 2 + u
                    dve.wait_ge(run_sb, g + 1)
                    need(dve, t_ps, g - 1)
                    nc.vector.tensor_copy(mx[u][:, G:G + 1], mx[1 - u][:, 0:1])
                    nc.vector.tensor_tensor_scan(mx[u][:, 0:G], reset[u][:, 1, :], run[:, :], 0.0, ALU.add, ALU.max
                                                 ).then_inc(mx_sb, 1)
                    dve.wait_ge(mx_sb, g + 1)
                    need(dve, t_ps, g)
                    edge = mx[u][:, 0:G].rearrange("h (k q) -> h k q", k=TILES)[:, :, P - 1]
                    nc.vector.tensor_tensor(dcar[:, :], mx[u][:, P:G + 1:P], edge, ALU.subtract).then_inc(dcar_sb, 1)
                    nc.vector.tensor_tensor(off[:, :], ps_al[0:HEADS, :], mx[u][:, 0:G], ALU.subtract).then_inc(off_sb, 1)
                    dve.wait_ge(dcar_sb, g * 2 + 1)
                    nc.vector.tensor_scalar(dcar[:, :], dcar[:, :], 0.0, None, ALU.min).then_inc(dcar_sb, 1)

                def payload(i, u):
                    g = i * 2 + u
                    dve.wait_ge(w_sb, g + 1)
                    for k in range(TILES):
                        last = nc.vector.tensor_tensor(pay[u][:, k, 0:D].rearrange("p (h c) -> p h c", h=HEADS),
                                                       gl[u][:, k, 0:D].rearrange("p (h c) -> p h c", h=HEADS),
                                                       pay[u][:, k, D:ROW3].unsqueeze(2).broadcast_to([P, HEADS, C]), ALU.mult)
                    last.then_inc(pay_sb, 1)
                    dve.wait_ge(ecar_sb, g + 1)
                    e2 = ecar[:, :].rearrange("o (k h) -> o k h", k=TILES)
                    for k in range(TILES):
                        nc.vector.tensor_copy(ecx[u][:, k, 0:D].rearrange("o (h c) -> o h c", h=HEADS),
                                              e2[:, k, :].unsqueeze(2).broadcast_to([1, HEADS, C]))
                    nc.vector.tensor_copy(ecx[u][:, :, D:ROW3], e2).then_inc(ecx_sb, 1)

                def scale(n):
                    def stage(i, u):
                        g = i * 2 + u
                        if n == 0:
                            dve.wait_ge(ecx_sb, g + 1)
                        need(dve, agg_ps, g * TILES + n)
                        need(dve, carry_ready, g * TILES + n)
                        nc.vector.tensor_tensor(carrs[:, :], carry[(n + 1) % 2][:, :], ecx[u][:, TILES - 1 - n, :], ALU.mult
                                                ).then_inc(carry_scaled, 1)
                    return stage

                def take(n):
                    def stage(i, u):
                        g = i * 2 + u
                        dve.wait_ge(agg_ps, g * TILES + (n + 1))
                        nc.vector.tensor_copy(carry[n % 2][:, :], ps_a[TILES - 1 - n][0:1, 0:ROW3]).then_inc(carry_ready, 1)
                    return stage
                run_stages(dve, [(scale(0), 1), (add_rows, 0), (take(0), 1), (scale(1), 1), (compare, 0), (take(1), 1),
                                 (scale(2), 1), (leak, 0), (take(2), 1), (scale(3), 1), (running_maximum, 0), (take(3), 1),
                                 (maxima, 0), (payload, 0)], EG)

        with ExitStack() as ctx:
            sn = [sb(f"sn3{u}", [P, TILES, ROWA], F32, ctx) for u in range(2)]
            ln = [sb(f"ln3{u}", [P, TILES, ROW3], F32, ctx) for u in range(2)]
            x1 = [sb(f"x13{u}", [P, TILES, D], F32, ctx) for u in range(2)]
            xb = sb("xb3", [P, TILES, D], F32, ctx)
            top_ = sb("top3", [P, TILES, HEADS], F32, ctx)
            dd = sb("dd3", [P, 2, TILES, HEADS], F32, ctx)
            ff = sb("ff3", [P, 2, TILES, HEADS], F32, ctx)
            den = sb("den3", [P, TILES, HEADS], F32, ctx)
            a1, a2 = sb("a13", [P, TILES, D], F32, ctx), sb("a23", [P, TILES, D], F32, ctx)
            ex, lin, el = sb("ex3", [P, G], F32, ctx), sb("lin3", [P, G], F32, ctx), sb("el3", [P, G], F32, ctx)
            r = sb("r3", [P, TILES, D], F32, ctx)
            o = [sb(f"o3{u}", [P, TILES, D], F32, ctx) for u in range(2)]
            stats, mv = sb("st3", [P, TILES, 6], F32, ctx), sb("mv3", [P, TILES, 2], F32, ctx)
            rstd, nshift = sb("rstd3", [P, TILES], F32, ctx), sb("nsh3", [P, TILES], F32, ctx)
            ps_g, ps_o = pb("ps3_g", ctx=ctx), pb("ps3_o", ctx=ctx)
            rows_in, stored = sem2("n3_in"), sem2("n3_stored")
            top_sb, ln_step = sem("n3_top"), sem("n3_ln_step")
            d_sb, f_sb, a_sb, a_ps, ex_sb, lin_sb, el_sb, o_ps, xb_sb, r_sb, nrm, o_sb = (sem("n3_" + s) for s in
                ("d", "f", "a", "a_ps", "ex", "lin", "el", "o_ps", "xb", "r", "nrm", "o"))
            dstep = sem("n3_step")
            block = ctx.enter_context(nc.Block())

            @block.sync
            def _(sp):
                def group(i, u):
                    g = i * 2 + u
                    need(sp, a_ps, g - 1, gate_sp)
                    need(sp, xb_sb, g - 1, gate_sp)
                    sp.dma_start(sn[u][:, :, :], group_rows(sums1, g, ROWA)).then_inc(rows_in[u], 16)
                    sp.dma_start(ln[u][:, :, :], group_rows(xl_t, g, ROW3)).then_inc(rows_in[u], 16)
                    sp.dma_start(x1[u][:, :, :], group_rows(x1_t, g, D)).then_inc(rows_in[u], 16)
                run_groups(sp, group, GROUPS)

            @block.gpsimd
            def _(pool):
                def with_bias(i, u):
                    g = i * 2 + u
                    need(pool, rows_in[u], (i + 1) * 48, gate)
                    need(pool, r_sb, g, gate)
                    nc.gpsimd.tensor_tensor(xb[:, :, :], x1[u][:, :, :], bout[:, :].unsqueeze(1).broadcast_to([P, TILES, D]),
                                            ALU.add).then_inc(xb_sb, 1)

                def store(i, u):
                    g = i * 2 + u
                    need(pool, o_sb, g + 1, gate)
                    pool.dma_start(group_rows(out, g, D), o[u][:, :, :]).then_inc(stored[u], 16)
                run_stages(pool, [(with_bias, 1), (store, 2)], GROUPS)
                for u in range(2):
                    pool.wait_ge(stored[u], 16 * HALF)

            @block.tensor
            def _(pe):
                def project(i, u):
                    g = i * 2 + u
                    pe.wait_ge(el_sb, g + 1)
                    need(pe, r_sb, g)
                    for k in range(TILES):
                        last = nc.tensor.matmul(ps_o[:, k * D:(k + 1) * D], el[:, k * P:(k + 1) * P], wout[:, :],
                                                start=True, stop=True)
                    last.then_inc(o_ps, 1)

                def join(i, u):
                    g = i * 2 + u
                    need(pe, lin_sb, g)
                    pe.wait_ge(a_sb, g + 1)
                    for k in range(TILES):
                        nc.tensor.matmul(ps_g[:, k * P:(k + 1) * P], a1[:, k, :], ident[:, :], start=True, stop=False)
                        last = nc.tensor.matmul(ps_g[:, k * P:(k + 1) * P], a2[:, k, :], ident[:, :], start=False, stop=True)
                    last.then_inc(a_ps, 1)
                run_stages(pe, [(project, 1), (join, 0)], GROUPS)

            @block.scalar
            def _(act):
                def exponentials(i, u):
                    g = i * 2 + u
                    act.wait_ge(a_ps, g + 1)
                    need(act, el_sb, g)
                    nc.scalar.activation(ex[:, :], ps_g[:, :], ACT.Exp, bias=bc).then_inc(ex_sb, 1)

                def factors(i, u):
                    g = i * 2 + u
                    act.wait_ge(d_sb, g + 1)
                    need(act, a_sb, g)
                    nc.scalar.activation(ff[:, :, :, :], dd[:, :, :, :], ACT.Exp).then_inc(f_sb, 1)

                def normalise(i, u):
                    g = i * 2 + u
                    act.wait_ge(nrm, g + 1)
                    need(act, stored[u], i * 16)
                    for k in range(TILES):
                        last = nc.scalar.activation(o[u][:, k, :], r[:, k, :], ACT.Identity, bias=nshift[:, k:k + 1],
                                                    scale=rstd[:, k:k + 1])
                    last.then_inc(o_sb, 1)
                run_stages(act, [(exponentials, 1), (factors, 0), (normalise, 2)], GROUPS)

            @block.vector
            def _(dve):

                def heads(t):
                    return t.rearrange("p (h c) -> p h c", h=HEADS)

                def maxima(i, u):
                    g = i * 2 + u
                    dve.wait_ge(rows_in[u], (i + 1) * 48)
                    top_edges, top_loop = sn[u][:, :, ROW3:ROWA], ln[u][:, :, D:ROW3]
                    nc.vector.tensor_tensor(top_[:, :, :], top_edges, top_loop, ALU.max).then_inc(top_sb, 1)
                    dve.wait_ge(top_sb, g + 1)
                    nc.vector.tensor_tensor(dd[:, 0, :, :], top_edges, top_[:, :, :], ALU.subtract)
                    nc.vector.tensor_tensor(dd[:, 1, :, :], top_loop, top_[:, :, :], ALU.subtract).then_inc(d_sb, 1)

                def elu(i, u):
                    g = i * 2 + u
                    dve.wait_ge(ex_sb, g + 1)
                    nc.vector.tensor_scalar(lin[:, :], ps_g[:, :], bcm1, -1.0, ALU.add, ALU.max).then_inc(lin_sb, 1)
                    dve.wait_ge(lin_sb, g + 1)
                    need(dve, o_ps, g)
                    nc.vector.scalar_tensor_tensor(el[:, :], ex[:, :], 1.0, lin[:, :], ALU.min, ALU.add).then_inc(el_sb, 1)

                def residual(i, u):
                    g = i * 2 + u
                    n = [0]

                    def chain(ins):
                        n[0] += 1
                        ins.then_inc(ln_step, 1)
                        dve.wait_ge(ln_step, g * LN_STEPS + n[0])
                    dve.wait_ge(o_ps, g + 1)
                    dve.wait_ge(xb_sb, g + 1)
                    need(dve, o_sb, g)
                    nc.vector.tensor_tensor(r[:, :, :], xb[:, :, :], ps_o[:, :].rearrange("p (k d) -> p k d", k=TILES),
                                            ALU.add).then_inc(r_sb, 1)
                    dve.wait_ge(r_sb, g + 1)
                    layer_norm(nc, dve, gate_dve, chain, r, stats, mv, rstd[:, :], nshift[:, :]).then_inc(nrm, 1)
                    assert n[0] == LN_STEPS, n[0]

                def weigh(i, u):
                    g = i * 2 + u
                    n = [0]

                    def chain(ins):
                        n[0] += 1
                        ins.then_inc(dstep, 1)
                        dve.wait_ge(dstep, g * 4 + n[0])
                    dve.wait_ge(f_sb, g + 1)
                    chain(nc.vector.tensor_tensor(den[:, :, :], sn[u][:, :, D:ROW3], ff[:, 0, :, :], ALU.mult))
                    chain(nc.vector.tensor_tensor(den[:, :, :], den[:, :, :], ff[:, 1, :, :], ALU.add))
                    chain(nc.vector.reciprocal(den[:, :, :], den[:, :, :]))
                    chain(nc.vector.tensor_tensor(ff[:, :, :, :], ff[:, :, :, :],
                                                  den[:, :, :].unsqueeze(1).broadcast_to([P, 2, TILES, HEADS]), ALU.mult))
                    need(dve, a_ps, g)
                    for k in range(TILES):
                        nc.vector.tensor_tensor(heads(a1[:, k, :]), heads(sn[u][:, k, 0:D]),
                                                ff[:, 0, k, :].unsqueeze(2).broadcast_to([P, HEADS, C]), ALU.mult)
                        last = nc.vector.tensor_tensor(heads(a2[:, k, :]), heads(ln[u][:, k, 0:D]),
                                                       ff[:, 1, k, :].unsqueeze(2).broadcast_to([P, HEADS, C]), ALU.mult)
                    last.then_inc(a_sb, 1)
                run_stages(dve, [(maxima, 0), (elu, 1), (weigh, 0), (residual, 1)], GROUPS)


_WEIGHTS = ["L0_gnn_W_msg", "L0_gnn_b_msg", "L0_gnn_W_upd", "L0_gnn_b_upd", "L0_gnn_prelu_a", "L0_gnn_gamma", "L0_gnn_beta",
            "L1_gnn_w_in", "L1_gnn_b_in", "L1_gnn_w_l", "L1_gnn_b_l", "L1_gnn_w_r", "L1_gnn_b_r", "L1_gnn_w_e", "L1_gnn_att",
            "L1_gnn_bias_conv", "L1_gnn_w_out", "L1_gnn_b_out"]


def kernel(**inputs):
    import numpy as np
    import concourse.bacc as bacc
    from concourse.bass_utils import run_bass_kernel_spmd as run

    x = np.asarray(inputs["x"])
    src, dst, ea = (np.asarray(inputs[k]) for k in ("src", "dst", "edge_attr_2"))
    n, e = x.shape[0], src.shape[0]
    pair = 2 * G
    n_pad, e_pad = -(-n // pair) * pair, -(-e // pair) * pair

    def rows(a):
        return np.ascontiguousarray(a.reshape(-1, G)[:, ::-1])

    def cols(a):
        return np.ascontiguousarray(rows(a).reshape(-1, P).T)

    src_e = np.pad(src, (0, e_pad - e))
    dst_e = np.pad(dst, (0, e_pad - e), constant_values=n)
    next_e = np.pad(dst_e[1:], (0, 1), constant_values=n + 1)
    prev_e = np.pad(dst_e[:-1], (1, 0), constant_values=-1)
    arrays = {
        "x": np.pad(x, ((0, n_pad - n), (0, 0))),
        "src_col": cols(src_e), "dst_col": cols(dst_e), "next_col": cols(next_e),
        "dst_row": rows(dst_e), "next_row": rows(next_e), "prev_row": rows(prev_e),
        "before_row": np.ascontiguousarray(prev_e[::G, None]),
        "ea_row": np.ascontiguousarray(np.pad(ea, ((0, e_pad - e), (0, 0))).reshape(-1, G, 2)[:, ::-1].transpose(0, 2, 1)),
    }
    for name in _WEIGHTS:
        arrays[name] = np.asarray(inputs[name])
    nc = bacc.Bacc("TRN2", target_bir_lowering=False, num_devices=1)
    args = [nc.dram_tensor("in_" + k, a.shape, mybir.dt.from_np(a.dtype), kind="ExternalInput").ap() for k, a in arrays.items()]
    out = nc.dram_tensor("out", (n_pad, D), F32, kind="ExternalOutput").ap()
    build(nc, *args, out, n, e)
    r = run(nc, [{"in_" + k: a for k, a in arrays.items()}], core_ids=[0])
    return r.results[0]["out"][:n]
```

```python
from contextlib import ExitStack

import concourse.bass as bass
from concourse import mybir
from concourse.alu_op_type import AluOpType as ALU

P = 128
D = 128
HEADS, C = 4, 32
TILES = 4
G = P * TILES
ROW3 = D + HEADS
ROWA = ROW3 + HEADS
BIG = 1.0e30
SKIP = 1 << 20
EPS = 1.0e-5
SLOPE = 0.2
LN_LINKS = 13

PARTS = 3
PAIRS = PARTS * PARTS

F32, I32, BF16 = mybir.dt.float32, mybir.dt.int32, mybir.dt.bfloat16
ACT = mybir.ActivationFunctionType
AX = mybir.AxisListType


def group_rows(table, g, width):
    return table[bass.ds(g * G, G), 0:width].rearrange("(p k) w -> p k w", k=TILES)


def slots(first, count):
    return first * count


def need(eng, sem, value, gate=None):
    if isinstance(value, int) and value <= 0:
        return
    eng.wait_ge(sem, value)
    if gate is not None:
        eng.sem_inc(gate, 1)


def run_stages(eng, stages, groups):
    def step(i, u, least, most):
        for stage, lag in stages:
            if least <= lag <= most:
                stage(i + (u - lag) // 2, (u - lag) % 2)
    deepest = max(lag for _, lag in stages)
    first = (deepest + 1) // 2 + 1
    for g in range(2 * first):
        step(g // 2, g % 2, 0, g)
    with eng.Fori(first, groups // 2) as i:
        for u in range(2):
            step(i, u, 0, deepest)
    for g in range(groups, groups + deepest):
        step(g // 2, g % 2, g - groups + 1, deepest)


def run_groups(eng, body, groups):
    for u in range(2):
        body(0, u)
    with eng.Fori(1, groups // 2) as i:
        for u in range(2):
            body(i, u)


def inv_sqrt_steps(nc, y, v, t):
    newton = [lambda: nc.vector.scalar_tensor_tensor(t, y, -0.5, y, ALU.mult, ALU.mult),
              lambda: nc.vector.tensor_tensor(t, t, v, ALU.mult),
              lambda: nc.vector.scalar_tensor_tensor(y, t, 1.5, y, ALU.add, ALU.mult)]
    return [lambda: nc.vector.tensor_scalar(v, v, EPS, None, ALU.add),
            lambda: nc.vector.tensor_scalar(t.bitcast(I32), v.bitcast(I32), 1, None, ALU.logical_shift_right),
            lambda: nc.vector.tensor_scalar(y.bitcast(I32), t.bitcast(I32), -1.0, float(0x5F3759DF), ALU.mult, ALU.add),
            *newton, *newton, *newton]


def norm_stages(nc, dve, gate, src, src_ready, stats, mv, tiny, stat_sb, mv_sb, step, used, done):
    def stat(k):
        def stage(i, u):
            g = i * 2 + u
            if k == 0:
                dve.wait_ge(src_ready, g + 1)
                need(dve, mv_sb, g)
                dve.sem_inc(gate, 1)
            last = nc.vector.bn_stats(stats[:, k, :], src[u][:, k, :])
            if k == TILES - 1:
                last.then_inc(stat_sb, 1)
        return stage

    def aggregate(i, u):
        g = i * 2 + u
        dve.wait_ge(stat_sb, g + 1)
        need(dve, done, g - 1)
        dve.sem_inc(gate, 1)
        for k in range(TILES):
            last = nc.vector.bn_aggr(mv[u][:, k, :], stats[:, k, :])
        last.then_inc(mv_sb, 1)

    def link(n):
        def stage(i, u):
            g = i * 2 + u
            y, shift, t = (tiny[u][:, j, :] for j in range(3))
            if n == 0:
                dve.wait_ge(mv_sb, g + 1)
                need(dve, used, g - 1)
            else:
                dve.wait_ge(step, g * (LN_LINKS - 1) + n)
            steps = inv_sqrt_steps(nc, y, mv[u][:, :, 1], t)
            if n < len(steps):
                steps[n]().then_inc(step, 1)
            else:
                nc.vector.scalar_tensor_tensor(shift, mv[u][:, :, 0], -1.0, y, ALU.mult, ALU.mult).then_inc(done, 1)
        return stage
    return [stat(k) for k in range(TILES)], aggregate, [link(n) for n in range(LN_LINKS)]


def build(nc, x, src_col, dst_col, next_col, dst_row, next_row, prev_row, before_row, ea_row,
          W_msg, b_msg, W_upd, b_upd, prelu_a, gamma, beta,
          w_in, b_in, w_l, b_l, w_r, b_r, w_e, att, bias_conv, w_out, b_out, out, n_nodes, n_edges):
    NP = x.shape[0]
    GROUPS = NP // G
    EG = dst_row.shape[0]
    ET = EG * TILES
    VALID = n_nodes - (GROUPS - 1) * G
    assert GROUPS == EG and EG % 2 == 0 and VALID % TILES == 0 and VALID > 0
    HALF = GROUPS // 2
    EHALF = EG // 2

    def scratch(name, shape):
        return nc.dram_tensor(name, shape, F32, kind="Internal").ap()

    sums0 = scratch("sums0", (NP, D))
    h_t = scratch("h_t", (D, NP))
    x1_t = scratch("x1", (NP, D))
    xl_t = scratch("xl", (NP, ROW3))
    xr_t = scratch("xr", (NP, D))
    sums1 = scratch("sums1", (NP, ROWA))
    masks = scratch("masks", (EG, 3, G))
    ea_parts = nc.dram_tensor("ea_parts", (EG, PAIRS * 2, G), BF16, kind="Internal").ap()
    we_parts = nc.dram_tensor("we_parts", (3, 2, D), BF16, kind="Internal").ap()

    top = ExitStack()
    with top:
        def sb(name, shape, dt=F32, ctx=top):
            return ctx.enter_context(nc.sbuf_tensor(name, shape, dt))

        def pb(name, shape=(P, G), ctx=top):
            return ctx.enter_context(nc.psum_tensor(name, list(shape), F32))

        def sem(name):
            return top.enter_context(nc.semaphore(name))

        def sem2(name):
            return [sem(f"{name}{u}") for u in range(2)]

        ident = sb("ident", [P, P])
        ones_col = sb("ones_col", [P, 1])
        wm = sb("wm", [P, 2, D])
        wu = sb("wu", [P, 2, D])
        win = sb("win", [P, D])
        wlr = sb("wlr", [P, 2, D])
        wsum = sb("wsum", [P, D])
        wout = sb("wout", [P, D])
        we = sb("we", [2, D])
        we18 = sb("we18", [PAIRS * 2, D], BF16)
        attb = sb("attb", [P, HEADS])
        cols = sb("cols", [P, 12])
        bmsg, bupd, gam, bet, bin_, bl, br, bconv, alpha, binm1, bz, bself = (cols[:, j:j + 1] for j in range(12))
        cols2 = sb("cols2", [P, 8])
        bc, bcm1, bn_scale, bn_shift, ebias = (cols2[:, j:j + 1] for j in range(5))
        bout = sb("bout", [P, D])
        srcc = sb("srcc", [P, ET], I32)
        dstc = sb("dstc", [P, ET], I32)
        nextc = sb("nextc", [P, ET], I32)
        dstf = sb("dstf", [P, ET])
        idx = sb("idx", [P, EG, 3, TILES], I32)
        bn = sb("bn", [P, GROUPS - 1 + TILES, 6])
        bnmv = sb("bnmv", [P, 2])
        blank = sb("blank", [P, TILES, ROWA])
        cleared0, cleared1 = sem("cleared0"), sem("cleared1")
        gate = sem("gate")

        with ExitStack() as ctx:
            rows = sb("rows", [EG, 4, G], I32, ctx)
            rowf = sb("rowf", [EG, 4, G], F32, ctx)
            befo = sb("befo", [EG, 1], I32, ctx)
            befof = sb("befof", [EG, 1], F32, ctx)
            mask = sb("mask", [EG, 3, G], F32, ctx)
            keep = sb("keep", [P, ET], F32, ctx)
            eag = sb("eag", [EG, 2, G], F32, ctx)
            eas = sb("eas", [EG, 2], F32, ctx)
            emean = sb("emean", [2, 1], F32, ctx)
            eap = sb("eap", [EG, PARTS, 2, G], BF16, ctx)
            earest = sb("earest", [EG, 2, G], F32, ctx)
            wep = sb("wep", [2, PARTS, D], BF16, ctx)
            werest = sb("werest", [2, D], F32, ctx)
            ps = pb("ps_setup", ctx=ctx)
            loaded, bias_in = sem("loaded"), sem("bias_in")
            zeros, id0, id1 = sem("zeros"), sem("id0"), sem("id1")
            mask_ready, masks_out = sem("mask_ready"), sem("masks_out")
            sum_ready, mean_sum, mean_ready, ebias_ready = sem("sum_ready"), sem("mean_sum"), sem("mean_ready"), sem("ebias_ready")
            att0, att_in = sem("att0"), sem("att_in")
            pst = sem("pstep_setup")
            parts_ready, parts_out, we_in = sem("parts_ready"), sem("parts_out"), sem("we_in")
            n_loads = 17
            block = ctx.enter_context(nc.Block())

            @block.sync
            def _(sp):
                def load(dst, src):
                    sp.dma_start(dst, src).then_inc(loaded, 16)
                load(srcc[:, :], src_col)
                load(dstc[:, :], dst_col)
                load(nextc[:, :], next_col)
                load(rows[:, 0, :], dst_row)
                load(rows[:, 1, :], next_row)
                load(rows[:, 2, :], prev_row)
                load(befo[:, :], before_row)
                load(eag[:, :, :], ea_row)
                for j in range(2):
                    load(wm[:, j, :], W_msg[j * D:(j + 1) * D, :])
                    load(wu[:, j, :], W_upd[j * D:(j + 1) * D, :])
                load(win[:, :], w_in)
                load(wlr[:, 0, :], w_l)
                load(wlr[:, 1, :], w_r)
                load(wout[:, :], w_out)
                load(we[:, :], w_e)
                sp.wait_ge(mask_ready, 1)
                sp.dma_start(masks, mask[:, :, :]).then_inc(masks_out, 16)
                sp.wait_ge(parts_ready, 1)
                for j in range(PARTS):
                    sp.dma_start(ea_parts[:, j * 2 * PARTS:(j + 1) * 2 * PARTS, :].rearrange("g (a d) q -> g a d q", a=PARTS),
                                 eap[:, :, :, :]).then_inc(parts_out, 16)
                sp.dma_start(we_parts.rearrange("a d f -> d a f"), wep[:, :, :]).then_inc(parts_out, 16)
                sp.wait_ge(parts_out, 16 * (PARTS + 1))
                for j in range(PARTS):
                    for a in range(PARTS):
                        row = (j * PARTS + a) * 2
                        sp.dma_start(we18[row:row + 2, :], we_parts[j, :, :]).then_inc(we_in, 16)
                sp.wait_ge(we_in, 16 * PAIRS)
                sp.wait_ge(masks_out, 16)

            @block.scalar
            def _(act):
                for col, vec in ((bmsg, b_msg), (bupd, b_upd), (gam, gamma), (bet, beta), (bin_, b_in), (bl, b_l),
                                 (br, b_r), (bconv, bias_conv)):
                    act.dma_start(col, vec.rearrange("(p o) -> p o", o=1)).then_inc(bias_in, 16)
                act.dma_start(alpha, prelu_a.partition_broadcast(P)).then_inc(bias_in, 16)
                act.dma_start(bout[:, :], b_out.partition_broadcast(P)).then_inc(bias_in, 16)
                act.wait_ge(att0, 1)
                for h in range(HEADS):
                    act.dma_start(attb[h * C:(h + 1) * C, h:h + 1], att[h:h + 1, :].rearrange("o c -> c o")).then_inc(att_in, 16)
                act.wait_ge(att_in, 16 * HEADS)
                act.wait_ge(zeros, 1)
                with act.Fori(0, GROUPS) as g:
                    act.dma_start(group_rows(sums0, g, D), blank[:, :, 0:D]).then_inc(cleared0, 16)

            @block.gpsimd
            def _(pool):
                nc.gpsimd.memset(ident[:, :], 0.0).then_inc(id0, 1)
                pool.wait_ge(id0, 1)
                nc.gpsimd.affine_select(out=ident[:, :], in_=ident[:, :], compare_op=ALU.not_equal, fill=1.0, base=0,
                                        pattern=[[-1, P]], channel_multiplier=1).then_inc(id1, 1)
                pool.wait_ge(id1, 1)

            @block.tensor
            def _(pe):
                pe.wait_ge(sum_ready, 1)
                nc.tensor.matmul(ps[0:2, 0:1], eas[:, :], ones_col[0:EG, :], start=True, stop=True).then_inc(mean_sum, 1)
                pe.wait_ge(mean_ready, 1)
                nc.tensor.matmul(ps[:, 1:2], we[:, :], emean[:, :], start=True, stop=True).then_inc(ebias_ready, 1)

            @block.vector
            def _(dve):
                n = [0]

                def chain(ins):
                    n[0] += 1
                    ins.then_inc(pst, 1)
                    dve.wait_ge(pst, n[0])

                nc.vector.memset(blank[:, :, ROW3:ROWA], -BIG)
                nc.vector.memset(ones_col[:, :], 1.0)
                nc.vector.memset(blank[:, :, 0:ROW3], 0.0).then_inc(zeros, 1)
                nc.vector.memset(attb[:, :], 0.0).then_inc(att0, 1)
                dve.wait_ge(loaded, 16 * n_loads)
                dve.wait_ge(bias_in, 16 * 10)
                chain(nc.vector.tensor_copy(dstf[:, :], dstc[:, :]))
                chain(nc.vector.tensor_tensor(keep[:, :], dstc[:, :], nextc[:, :], ALU.is_equal))
                by_group = "p (g k) -> p g k"
                chain(nc.vector.scalar_tensor_tensor(idx[:, :, 2, :], keep[:, :].rearrange(by_group, k=TILES), float(SKIP),
                                                     dstf[:, :].rearrange(by_group, k=TILES), ALU.mult, ALU.add))
                chain(nc.vector.tensor_copy(idx[:, :, 0, :], srcc[:, :].rearrange(by_group, k=TILES)))
                chain(nc.vector.tensor_copy(idx[:, :, 1, :], dstc[:, :].rearrange(by_group, k=TILES)))
                chain(nc.vector.tensor_copy(befof[:, :], befo[:, :]))
                chain(nc.vector.tensor_copy(rowf[:, 0:3, :], rows[:, 0:3, :]))
                chain(nc.vector.tensor_tensor(mask[:, 0, :], rowf[:, 0, :], rowf[:, 2, :], ALU.not_equal))
                chain(nc.vector.tensor_tensor(mask[:, 1, :], rowf[:, 0, :], rowf[:, 1, :], ALU.not_equal))
                chain(nc.vector.memset(mask[:, 1, :].rearrange("g (k p) -> g k p", p=P)[:, :, 0:1], 1.0))
                chain(nc.vector.tensor_scalar(mask[:, 0:2, :], mask[:, 0:2, :], -BIG, None, ALU.mult))
                for k in range(TILES - 1):
                    nc.vector.tensor_scalar(mask[:, 2, k * P:(k + 1) * P], rowf[:, 0, k * P:(k + 1) * P],
                                            rowf[:, 0, (k + 1) * P:(k + 1) * P + 1], None, ALU.is_equal)
                nc.vector.tensor_scalar(mask[:, 2, (TILES - 1) * P:], rowf[:, 0, (TILES - 1) * P:], befof[:, 0:1], None,
                                        ALU.is_equal).then_inc(mask_ready, 1)
                for parts, rest, full in ((eap[:, :, :, :].rearrange("g a d q -> g a (d q)"), earest[:, :, :].rearrange("g d q -> g (d q)"),
                                           eag[:, :, :].rearrange("g d q -> g (d q)")), (wep[:, :, :], werest[:, :], we[:, :])):
                    chain(nc.vector.tensor_copy(parts[:, 0, :], full))
                    chain(nc.vector.tensor_tensor(rest, full, parts[:, 0, :], ALU.subtract))
                    chain(nc.vector.tensor_copy(parts[:, 1, :], rest))
                    chain(nc.vector.tensor_tensor(rest, rest, parts[:, 1, :], ALU.subtract))
                    chain(nc.vector.tensor_copy(parts[:, 2, :], rest))
                dve.sem_inc(parts_ready, 1)
                chain(nc.vector.tensor_reduce(eas[:, :], eag[:, :, :], AX.X, ALU.add))
                dve.sem_inc(sum_ready, 1)
                dve.wait_ge(mean_sum, 1)
                nc.vector.tensor_scalar(emean[:, :], ps[0:2, 0:1], 1.0 / n_edges, None, ALU.mult).then_inc(mean_ready, 1)
                chain(nc.vector.tensor_tensor(bz, bl, br, ALU.add))
                chain(nc.vector.tensor_scalar(binm1, bin_, -1.0, None, ALU.add))
                chain(nc.vector.tensor_tensor(bc, bconv, bl, ALU.add))
                chain(nc.vector.tensor_scalar(bcm1, bc, -1.0, None, ALU.add))
                chain(nc.vector.tensor_tensor(wsum[:, :], wlr[:, 0, :], wlr[:, 1, :], ALU.add))
                dve.wait_ge(ebias_ready, 1)
                chain(nc.vector.tensor_tensor(bself, bz, ps[:, 1:2], ALU.add))

        with ExitStack() as ctx:
            gidx = [sb(f"gidx{u}", [P, 2, TILES], I32, ctx) for u in range(2)]
            sidx = [sb(f"sidx{u}", [P, TILES], I32, ctx) for u in range(2)]
            xe = [sb(f"xe{u}", [P, 2, TILES, D], F32, ctx) for u in range(2)]
            drow = [sb(f"drow{u}", [P, G], I32, ctx) for u in range(2)]
            frow = [sb(f"frow{u}", [1, G], F32, ctx) for u in range(2)]
            same = [sb(f"same{u}", [P, TILES, P], F32, ctx) for u in range(2)]
            xT = [sb(f"xT{j}", [P, G], F32, ctx) for j in range(2)]
            mT = sb("mT", [P, G], F32, ctx)
            mu = [sb(f"mu{u}", [P, TILES, D + 1], F32, ctx) for u in range(2)]
            carry = [sb(f"carry{j}", [1, D + 1], F32, ctx) for j in range(2)]
            rcnt = sb("rcnt", [P, TILES], F32, ctx)
            osum = [sb(f"osum{u}", [P, TILES, D], F32, ctx) for u in range(2)]
            ps_x = [pb(f"ps_x{j}", ctx=ctx) for j in range(2)]
            ps_m, ps_u = pb("ps_m", ctx=ctx), pb("ps_u", ctx=ctx)
            ps_a = [pb(f"ps_a{k}", ctx=ctx) for k in range(TILES)]

            gidx_set, sidx_set = sem2("gidx_set"), sem2("sidx_set")
            gathered, scattered, rows_in = sem2("gathered"), sem2("scattered"), sem2("rows_in")
            gathered_t = [sem2(f"xposed{j}_") for j in range(2)]
            xT_ready = [sem(f"xT_ready{j}") for j in range(2)]
            m_ps, m_sb, u_ps, u_sb = sem("m_ps"), sem("m_sb"), sem("u_ps"), sem("u_sb")
            same_ready, agg_ps, carry_ready = sem2("same_ready"), sem("agg_ps"), sem("carry_ready")
            osum_ready = sem2("osum_ready")
            init = sem("init_p1")
            rc = sem("rcnt_ready")
            block = ctx.enter_context(nc.Block())

            @block.sync
            def _(sp):
                def group(i, u):
                    g = i * 2 + u
                    need(sp, same_ready[u], i, gate)
                    need(sp, agg_ps, (g - 1) * TILES, gate)
                    sp.dma_start(drow[u][:, :], dst_row[bass.ds(g, 1), :].rearrange("o q -> (o q)").partition_broadcast(P)
                                 ).then_inc(rows_in[u], 16)
                    sp.dma_start(frow[u][:, :], masks[bass.ds(g, 1), 2, :]).then_inc(rows_in[u], 16)
                    sp.dma_start(group_rows(sums1, g, ROWA), blank[:, :, :]).then_inc(cleared1, 16)
                run_groups(sp, group, EG)
                sp.wait_ge(cleared1, 16 * EG)

            @block.gpsimd
            def _(pool):
                def hold(sem_, value):
                    need(pool, sem_, value, gate)

                def gather(i, u):
                    g = i * 2 + u
                    for j in range(2):
                        hold(gathered_t[j][u], i)
                    hold(gathered[u], i * (16 * 2 * TILES))
                    nc.gpsimd.tensor_copy(gidx[u][:, :, :], idx[:, bass.ds(g, 1), 0:2, :].rearrange("p o j k -> p (o j) k")
                                          ).then_inc(gidx_set[u], 1)
                    hold(gidx_set[u], i + 1)
                    for j in range(2):
                        for k in reversed(range(TILES)):
                            pool.indirect_dma_start(
                                out=xe[u][:, j, k, :], out_offset=None, in_=x,
                                in_offset=bass.IndirectOffsetOnAxis(ap=gidx[u][:, j, k:k + 1], axis=0)).then_inc(gathered[u], 16)

                def scatter(i, u):
                    g = i * 2 + u
                    hold(scattered[u], i * (16 * TILES))
                    nc.gpsimd.tensor_copy(sidx[u][:, :], idx[:, bass.ds(g, 1), 2, :].rearrange("p o k -> p (o k)")
                                          ).then_inc(sidx_set[u], 1)
                    hold(sidx_set[u], i + 1)
                    hold(osum_ready[u], i + 1)
                    if isinstance(i, int) and g == 0:
                        hold(cleared0, 16 * GROUPS)
                    for k in range(TILES):
                        pool.indirect_dma_start(
                            out=sums0, out_offset=bass.IndirectOffsetOnAxis(ap=sidx[u][:, k:k + 1], axis=0),
                            in_=osum[u][:, k, :], in_offset=None, bounds_check=NP - 1, oob_is_err=False).then_inc(scattered[u], 16)

                run_stages(pool, [(scatter, 3), (gather, 0)], EG)
                for u in range(2):
                    pool.wait_ge(scattered[u], 16 * TILES * EHALF)

            @block.tensor
            def _(pe):
                pe.wait_ge(init, 1)

                def group(i, u):
                    g = i * 2 + u
                    pe.wait_ge(gathered[u], (i + 1) * (16 * 2 * TILES))
                    for j in range(2):
                        need(pe, xT_ready[j], g)
                        for k in range(TILES):
                            last = nc.tensor.transpose(ps_x[j][:, k * P:(k + 1) * P], xe[u][:, j, k, :], ident[:, :])
                        last.then_inc(gathered_t[j][u], 1)
                    pe.wait_ge(xT_ready[0], g + 1)
                    need(pe, m_sb, g)
                    nc.tensor.matmul(ps_m[:, :], wm[:, 0, :], xT[0][:, :], start=True, stop=False)
                    pe.wait_ge(xT_ready[1], g + 1)
                    nc.tensor.matmul(ps_m[:, :], wm[:, 1, :], xT[1][:, :], start=False, stop=True).then_inc(m_ps, 1)
                    pe.wait_ge(m_sb, g + 1)
                    need(pe, u_sb, g)
                    for k in range(TILES):
                        last = nc.tensor.matmul(ps_u[:, k * D:(k + 1) * D], mT[:, k * P:(k + 1) * P], wu[:, 1, :],
                                                start=True, stop=True)
                    last.then_inc(u_ps, 1)
                    pe.wait_ge(same_ready[u], i + 1)
                    pe.wait_ge(u_sb, g + 1)
                    pe.wait_ge(rows_in[u], (i + 1) * 32)
                    need(pe, osum_ready[1 - u], i + u)
                    for n, k in enumerate(reversed(range(TILES))):
                        nc.tensor.matmul(ps_a[k][:, 0:D + 1], same[u][:, k, :], mu[u][:, k, :], start=True, stop=False)
                        t = g * TILES + n
                        need(pe, carry_ready, t)
                        nc.tensor.matmul(ps_a[k][:, 0:D + 1], frow[u][:, k * P:(k + 1) * P], carry[(n + 1) % 2][:, :],
                                         start=False, stop=True).then_inc(agg_ps, 1)
                run_groups(pe, group, EG)

            @block.scalar
            def _(act):
                def group(i, u):
                    g = i * 2 + u
                    act.wait_ge(gathered_t[0][u], i + 1)
                    need(act, m_ps, g)
                    nc.scalar.activation(xT[0][:, :], ps_x[0][:, :], ACT.Copy).then_inc(xT_ready[0], 1)
                    act.wait_ge(m_ps, g + 1)
                    need(act, u_ps, g)
                    nc.scalar.activation(mT[:, :], ps_m[:, :], ACT.Relu, bias=bmsg).then_inc(m_sb, 1)
                    for n, k in enumerate(reversed(range(TILES))):
                        act.wait_ge(agg_ps, g * TILES + (n + 1))
                        nc.scalar.activation(carry[n % 2][:, :], ps_a[k][0:1, 0:D + 1], ACT.Copy).then_inc(carry_ready, 1)
                run_groups(act, group, EG)

            @block.vector
            def _(dve):
                for u in range(2):
                    nc.vector.memset(mu[u][:, :, :], 1.0)
                nc.vector.memset(carry[0][:, :], 0.0)
                nc.vector.memset(carry[1][:, :], 0.0).then_inc(init, 1)
                dve.wait_ge(init, 1)

                def group(i, u):
                    g = i * 2 + u
                    dve.wait_ge(rows_in[u], (i + 1) * 32)
                    need(dve, agg_ps, (g - 1) * TILES)
                    nc.vector.tensor_tensor(same[u][:, :, :], drow[u][:, :].rearrange("p (k q) -> p k q", k=TILES),
                                            dstf[:, bass.ds(g * TILES, TILES)].unsqueeze(2).broadcast_to([P, TILES, P]),
                                            ALU.is_equal).then_inc(same_ready[u], 1)
                    dve.wait_ge(gathered_t[1][u], i + 1)
                    need(dve, m_ps, g)
                    nc.vector.tensor_copy(xT[1][:, :], ps_x[1][:, :]).then_inc(xT_ready[1], 1)
                    dve.wait_ge(u_ps, g + 1)
                    nc.vector.tensor_copy(mu[u][:, :, 0:D], ps_u[:, :].rearrange("p (k d) -> p k d", k=TILES)).then_inc(u_sb, 1)
                    need(dve, scattered[u], i * (16 * TILES))
                    for n, k in enumerate(reversed(range(TILES))):
                        dve.wait_ge(carry_ready, g * TILES + (n + 1))
                        nc.vector.reciprocal(rcnt[:, k:k + 1], ps_a[k][:, D:D + 1]).then_inc(rc, 1)
                        dve.wait_ge(rc, g * TILES + (n + 1))
                        last = nc.vector.tensor_scalar(osum[u][:, k, :], ps_a[k][:, 0:D], rcnt[:, k:k + 1], None, ALU.mult)
                    last.then_inc(osum_ready[u], 1)
                run_groups(dve, group, EG)

        with ExitStack() as ctx:
            xn = [sb(f"xn{u}", [P, TILES, D], F32, ctx) for u in range(2)]
            sn = [sb(f"sn{u}", [P, TILES, D], F32, ctx) for u in range(2)]
            xT = [sb(f"xTn{u}", [P, G], F32, ctx) for u in range(2)]
            hb, neg = [sb(f"hb{u}", [P, G], F32, ctx) for u in range(2)], sb("neg", [P, G], F32, ctx)
            hT = [sb(f"hT{u}", [P, G], F32, ctx) for u in range(2)]
            ps_x, ps_h = [pb(f"ps_xn{u}", ctx=ctx) for u in range(2)], [pb(f"ps_hn{u}", ctx=ctx) for u in range(2)]
            x_in, sums_in, stored = sem2("n1_x_in"), sem2("n1_sums_in"), sem2("n1_stored")
            xt_ps, xt_sb, h_ps, h_sb, stat = sem("n1_xt_ps"), sem("n1_xt_sb"), sem("n1_h_ps"), sem("n1_h_sb"), sem("n1_stat")
            hb_sb, neg_sb, bn_step = sem("n1_hb"), sem("n1_neg"), sem("bn_step")
            block = ctx.enter_context(nc.Block())

            @block.sync
            def _(sp):
                def load_x(i, u):
                    need(sp, xt_ps, i * 2 + u - 1, gate)
                    sp.dma_start(xn[u][:, :, :], group_rows(x, i * 2 + u, D)).then_inc(x_in[u], 16)

                def load_sums(i, u):
                    need(sp, h_ps, i * 2 + u - 1, gate)
                    sp.dma_start(sn[u][:, :, :], group_rows(sums0, i * 2 + u, D)).then_inc(sums_in[u], 16)
                run_stages(sp, [(load_x, 0), (load_sums, 1)], GROUPS)

            @block.gpsimd
            def _(pool):
                def group(i, u):
                    g = i * 2 + u
                    pool.wait_ge(h_sb, g + 1)
                    pool.sem_inc(gate, 1)
                    pool.dma_start(h_t[:, bass.ds(g * G, G)], hT[u][:, :]).then_inc(stored[u], 16)
                run_groups(pool, group, GROUPS)
                for u in range(2):
                    pool.wait_ge(stored[u], 16 * HALF)

            @block.tensor
            def _(pe):
                def turn(i, u):
                    g = i * 2 + u
                    pe.wait_ge(x_in[u], (i + 1) * 16)
                    need(pe, xt_sb, g - 1)
                    for k in range(TILES):
                        last = nc.tensor.transpose(ps_x[u][:, k * P:(k + 1) * P], xn[u][:, k, :], ident[:, :])
                    last.then_inc(xt_ps, 1)

                def hidden(i, u):
                    g = i * 2 + u
                    pe.wait_ge(xt_sb, g + 1)
                    need(pe, hb_sb, g - 1)
                    nc.tensor.matmul(ps_h[u][:, :], wu[:, 0, :], xT[u][:, :], start=True, stop=False)
                    pe.wait_ge(sums_in[u], (i + 1) * 16)
                    for k in range(TILES):
                        last = nc.tensor.matmul(ps_h[u][:, k * P:(k + 1) * P], sn[u][:, k, :], ident[:, :],
                                                start=False, stop=k == TILES - 1)
                    last.then_inc(h_ps, 1)
                run_stages(pe, [(turn, 0), (hidden, 1)], GROUPS)

            @block.scalar
            def _(act):
                def copy_xt(i, u):
                    g = i * 2 + u
                    act.wait_ge(xt_ps, g + 1)
                    need(act, h_ps, g - 1)
                    nc.scalar.activation(xT[u][:, :], ps_x[u][:, :], ACT.Copy).then_inc(xt_sb, 1)

                def with_bias(i, u):
                    g = i * 2 + u
                    act.wait_ge(h_ps, g + 1)
                    need(act, h_sb, g - 1)
                    nc.scalar.activation(hb[u][:, :], ps_h[u][:, :], ACT.Identity, bias=bupd).then_inc(hb_sb, 1)
                run_stages(act, [(copy_xt, 0), (with_bias, 1)], GROUPS)

            @block.vector
            def _(dve):
                def group(i, u, valid=P):
                    g = i * 2 + u
                    dve.wait_ge(hb_sb, g + 1)
                    nc.vector.tensor_scalar(neg[:, :], hb[u][:, :], 0.0, alpha, ALU.min, ALU.mult).then_inc(neg_sb, 1)
                    dve.wait_ge(neg_sb, g + 1)
                    need(dve, stored[u], i * 16)
                    nc.vector.scalar_tensor_tensor(hT[u][:, :], hb[u][:, :], 0.0, neg[:, :], ALU.max, ALU.add).then_inc(h_sb, 1)
                    dve.wait_ge(h_sb, g + 1)
                    dve.sem_inc(gate, 1)
                    if valid == P:
                        nc.vector.bn_stats(bn[:, bass.ds(g, 1), :].rearrange("p o s -> p (o s)"), hT[u][:, :]).then_inc(stat, 1)
                    else:
                        for k in range(TILES):
                            last = nc.vector.bn_stats(bn[:, g + k, :], hT[u][:, k * P:k * P + valid])
                        last.then_inc(stat, 1)
                for u in range(2):
                    group(0, u)
                with dve.Fori(1, HALF - 1) as i:
                    for u in range(2):
                        group(i, u)
                group(HALF - 1, 0)
                group(HALF - 1, 1, VALID // TILES)
                n = [0]

                def chain(ins):
                    n[0] += 1
                    ins.then_inc(bn_step, 1)
                    dve.wait_ge(bn_step, n[0])
                dve.wait_ge(stat, GROUPS)
                chain(nc.vector.bn_aggr(bnmv[:, :], bn[:, :, :].rearrange("p g s -> p (g s)")))
                for link in inv_sqrt_steps(nc, bn_scale, bnmv[:, 1:2], cols2[:, 5:6]):
                    chain(link())
                chain(nc.vector.tensor_tensor(bn_scale, bn_scale, gam, ALU.mult))
                chain(nc.vector.tensor_tensor(bn_shift, bnmv[:, 0:1], bn_scale, ALU.mult))
                chain(nc.vector.tensor_tensor(bn_shift, bet, bn_shift, ALU.subtract))

        with ExitStack() as ctx:
            xn = [sb(f"xn2{u}", [P, TILES, D], F32, ctx) for u in range(2)]
            hT = [sb(f"hT2{u}", [P, G], F32, ctx) for u in range(2)]
            yT = [sb(f"yT{u}", [P, G], F32, ctx) for u in range(2)]
            r = [sb(f"r2{u}", [P, TILES, D], F32, ctx) for u in range(2)]
            x1 = [sb(f"x1{u}", [P, TILES, D], F32, ctx) for u in range(2)]
            x1T = sb("x1T", [P, G], F32, ctx)
            lin = sb("lin2", [P, G], F32, ctx)
            ex, el, zb, zs = ([sb(f"{name}{u}", [P, G], F32, ctx) for u in range(2)] for name in ("ex2", "el2", "zb", "zs"))
            xl = [sb(f"xlo{u}", [P, TILES, ROW3], F32, ctx) for u in range(2)]
            xr = [sb(f"xro{u}", [P, TILES, D], F32, ctx) for u in range(2)]
            stats = sb("st2", [P, TILES, 6], F32, ctx)
            mv = [sb(f"mv2{u}", [P, TILES, 2], F32, ctx) for u in range(2)]
            tiny = [sb(f"ty2{u}", [P, 3, TILES], F32, ctx) for u in range(2)]
            ps_y = [pb(f"ps_y{u}", ctx=ctx) for u in range(2)]
            ps_t, ps_h, ps_z = pb("ps_t", ctx=ctx), pb("ps_h", ctx=ctx), pb("ps_z", ctx=ctx)
            ps_l, ps_r, ps_s = pb("ps_l", ctx=ctx), pb("ps_r", ctx=ctx), pb("ps_s", ctx=ctx)
            h_in, x_in = sem2("n2_h_in"), sem2("n2_x_in")
            st_x1, st_l, st_r = sem2("n2_st_x1"), sem2("n2_st_l"), sem2("n2_st_r")
            yt, y_ps, r_sb, nrm, x1_sb, x1t_ps, x1t_sb, h_ps = (sem("n2_" + s) for s in
                ("yt", "y_ps", "r_sb", "nrm", "x1_sb", "x1t_ps", "x1t_sb", "h_ps"))
            ex_sb, lin_sb, el_sb, l_ps, r_ps, z_ps, z_sb, s_ps, l_sb, r2_sb, s_sb = (sem("n2_" + s) for s in
                ("ex_sb", "lin_sb", "el_sb", "l_ps", "r_ps", "z_ps", "z_sb", "s_ps", "l_sb", "r2_sb", "s_sb"))
            zb_sb, stat_sb, mv_sb, dstep = sem("n2_zb"), sem("n2_stat"), sem("n2_mv"), sem("n2_step")
            block = ctx.enter_context(nc.Block())

            @block.sync
            def _(sp):
                def load(i, u):
                    g = i * 2 + u
                    need(sp, yt, g - 1, gate)
                    sp.dma_start(hT[u][:, :], h_t[:, bass.ds(g * G, G)]).then_inc(h_in[u], 16)
                    need(sp, r_sb, g - 1, gate)
                    sp.dma_start(xn[u][:, :, :], group_rows(x, g, D)).then_inc(x_in[u], 16)

                def store_x1(i, u):
                    g = i * 2 + u
                    need(sp, x1_sb, g + 1, gate)
                    sp.dma_start(group_rows(x1_t, g, D), x1[u][:, :, :]).then_inc(st_x1[u], 16)

                def store_lr(i, u):
                    g = i * 2 + u
                    need(sp, r2_sb, g + 1, gate)
                    sp.dma_start(group_rows(xr_t, g, D), xr[u][:, :, :]).then_inc(st_r[u], 16)
                    need(sp, l_sb, g + 1, gate)
                    need(sp, s_sb, g + 1, gate)
                    sp.dma_start(group_rows(xl_t, g, ROW3), xl[u][:, :, :]).then_inc(st_l[u], 16)
                run_stages(sp, [(load, 0), (store_x1, 4), (store_lr, 7)], GROUPS)
                for u in range(2):
                    for s in (st_x1[u], st_l[u], st_r[u]):
                        sp.wait_ge(s, 16 * HALF)

            @block.gpsimd
            def _(pool):
                def normalise(i, u):
                    g = i * 2 + u
                    need(pool, nrm, g + 1, gate)
                    need(pool, st_x1[u], i * 16, gate)
                    need(pool, x1t_ps, g - 1, gate)
                    for k in range(TILES):
                        last = nc.gpsimd.tensor_scalar(x1[u][:, k, :], r[u][:, k, :], tiny[u][:, 0, k:k + 1],
                                                       tiny[u][:, 1, k:k + 1], ALU.mult, ALU.add)
                    last.then_inc(x1_sb, 1)
                run_stages(pool, [(normalise, 0)], GROUPS)

            @block.tensor
            def _(pe):
                def turn_y(i, u):
                    g = i * 2 + u
                    pe.wait_ge(yt, g + 1)
                    need(pe, r_sb, g - 1)
                    for k in range(TILES):
                        last = nc.tensor.transpose(ps_y[u][:, k * P:(k + 1) * P], yT[u][:, k * P:(k + 1) * P], ident[:, :])
                    last.then_inc(y_ps, 1)

                def turn_x1(i, u):
                    g = i * 2 + u
                    pe.wait_ge(x1_sb, g + 1)
                    need(pe, x1t_sb, g)
                    for k in range(TILES):
                        last = nc.tensor.transpose(ps_t[:, k * P:(k + 1) * P], x1[u][:, k, :], ident[:, :])
                    last.then_inc(x1t_ps, 1)

                def hidden(i, u):
                    g = i * 2 + u
                    pe.wait_ge(x1t_sb, g + 1)
                    need(pe, lin_sb, g)
                    nc.tensor.matmul(ps_h[:, :], win[:, :], x1T[:, :], start=True, stop=True).then_inc(h_ps, 1)

                def self_scores(i, u):
                    g = i * 2 + u
                    pe.wait_ge(el_sb, g + 1)
                    need(pe, zb_sb, g)
                    nc.tensor.matmul(ps_z[:, :], wsum[:, :], el[u][:, :], start=True, stop=True).then_inc(z_ps, 1)

                def left(i, u):
                    g = i * 2 + u
                    need(pe, l_sb, g)
                    for k in range(TILES):
                        last = nc.tensor.matmul(ps_l[:, k * D:(k + 1) * D], el[u][:, k * P:(k + 1) * P], wlr[:, 0, :],
                                                start=True, stop=True)
                    last.then_inc(l_ps, 1)

                def right(i, u):
                    g = i * 2 + u
                    need(pe, r2_sb, g)
                    for k in range(TILES):
                        last = nc.tensor.matmul(ps_r[:, k * D:(k + 1) * D], el[u][:, k * P:(k + 1) * P], wlr[:, 1, :],
                                                start=True, stop=True)
                    last.then_inc(r_ps, 1)

                def scores(i, u):
                    g = i * 2 + u
                    pe.wait_ge(z_sb, g + 1)
                    need(pe, s_sb, g)
                    for k in range(TILES):
                        last = nc.tensor.matmul(ps_s[:, k * HEADS:(k + 1) * HEADS], zs[u][:, k * P:(k + 1) * P], attb[:, :],
                                                start=True, stop=True)
                    last.then_inc(s_ps, 1)
                run_stages(pe, [(scores, 6), (turn_y, 1), (self_scores, 5), (left, 5), (turn_x1, 3), (right, 5), (hidden, 3)], GROUPS)

            @block.scalar
            def _(act):
                def batch_norm(i, u):
                    g = i * 2 + u
                    act.wait_ge(h_in[u], (i + 1) * 16)
                    need(act, y_ps, g - 1)
                    nc.scalar.activation(yT[u][:, :], hT[u][:, :], ACT.Identity, bias=bn_shift, scale=bn_scale).then_inc(yt, 1)

                def exponentials(i, u):
                    g = i * 2 + u
                    act.wait_ge(h_ps, g + 1)
                    need(act, el_sb, g - 1)
                    nc.scalar.activation(ex[u][:, :], ps_h[:, :], ACT.Exp, bias=bin_).then_inc(ex_sb, 1)

                def copy_x1t(i, u):
                    g = i * 2 + u
                    act.wait_ge(x1t_ps, g + 1)
                    need(act, h_ps, g)
                    nc.scalar.activation(x1T[:, :], ps_t[:, :], ACT.Copy).then_inc(x1t_sb, 1)

                def with_bias(i, u):
                    g = i * 2 + u
                    act.wait_ge(z_ps, g + 1)
                    need(act, z_sb, g - 1)
                    nc.scalar.activation(zb[u][:, :], ps_z[:, :], ACT.Identity, bias=bself).then_inc(zb_sb, 1)

                def copy_left(i, u):
                    g = i * 2 + u
                    act.wait_ge(l_ps, g + 1)
                    need(act, st_l[u], i * 16)
                    nc.scalar.activation(xl[u][:, :, 0:D], ps_l[:, :].rearrange("p (k d) -> p k d", k=TILES), ACT.Copy
                                         ).then_inc(l_sb, 1)

                def copy_right(i, u):
                    g = i * 2 + u
                    act.wait_ge(r_ps, g + 1)
                    need(act, st_r[u], i * 16)
                    nc.scalar.activation(xr[u][:, :, :], ps_r[:, :].rearrange("p (k d) -> p k d", k=TILES), ACT.Copy
                                         ).then_inc(r2_sb, 1)

                def copy_scores(i, u):
                    g = i * 2 + u
                    act.wait_ge(s_ps, g + 1)
                    nc.scalar.activation(xl[u][:, :, D:ROW3], ps_s[:, 0:TILES * HEADS].rearrange("p (k h) -> p k h", k=TILES),
                                         ACT.Copy).then_inc(s_sb, 1)
                run_stages(act, [(exponentials, 4), (batch_norm, 0), (copy_scores, 6), (with_bias, 5), (copy_left, 5), (copy_x1t, 3),
                                 (copy_right, 5)], GROUPS)

            @block.vector
            def _(dve):
                def linear(i, u):
                    g = i * 2 + u
                    dve.wait_ge(ex_sb, g + 1)
                    need(dve, el_sb, g)
                    nc.vector.tensor_scalar(lin[:, :], ps_h[:, :], binm1, -1.0, ALU.add, ALU.max).then_inc(lin_sb, 1)

                def elu(i, u):
                    g = i * 2 + u
                    dve.wait_ge(lin_sb, g + 1)
                    need(dve, r_ps, g - 1)
                    nc.vector.scalar_tensor_tensor(el[u][:, :], ex[u][:, :], 1.0, lin[:, :], ALU.min, ALU.add).then_inc(el_sb, 1)

                def residual(i, u):
                    g = i * 2 + u
                    dve.wait_ge(y_ps, g + 1)
                    dve.wait_ge(x_in[u], (i + 1) * 16)
                    need(dve, x1_sb, g - 1)
                    nc.vector.tensor_tensor(r[u][:, :, :], xn[u][:, :, :], ps_y[u][:, :].rearrange("p (k d) -> p k d", k=TILES),
                                            ALU.add).then_inc(r_sb, 1)

                def leak(i, u):
                    g = i * 2 + u
                    dve.wait_ge(zb_sb, g + 1)
                    need(dve, s_ps, g - 1)
                    nc.vector.scalar_tensor_tensor(zs[u][:, :], zb[u][:, :], SLOPE, zb[u][:, :], ALU.mult, ALU.max).then_inc(z_sb, 1)

                stat, aggregate, t = norm_stages(nc, dve, gate, r, r_sb, stats, mv, tiny, stat_sb, mv_sb, dstep, x1_sb, nrm)
                run_stages(dve, [(t[0], 2), (linear, 4), (t[1], 2), (elu, 4), (t[2], 2), (residual, 1), (t[3], 2), (stat[0], 1),
                                 (t[4], 2), (stat[1], 1), (t[5], 2), (stat[2], 1), (t[6], 2), (stat[3], 1), (t[7], 2),
                                 (leak, 5), (t[8], 2), (aggregate, 1), (t[9], 2), (t[10], 2), (t[11], 2), (t[12], 2)], GROUPS)

        with ExitStack() as ctx:
            gidx = [sb(f"gidxa{u}", [P, 2, TILES], I32, ctx) for u in range(2)]
            sidx = [sb(f"sidxa{u}", [P, TILES], I32, ctx) for u in range(2)]
            gl = [sb(f"gl{u}", [P, TILES, ROW3], F32, ctx) for u in range(2)]
            gr = [sb(f"gr{u}", [P, TILES, D], F32, ctx) for u in range(2)]
            drow = [sb(f"drowa{u}", [P, G], I32, ctx) for u in range(2)]
            frow = [sb(f"frowa{u}", [1, G], F32, ctx) for u in range(2)]
            reset = [sb(f"reset{u}", [HEADS, 2, G], F32, ctx) for u in range(2)]
            ea = [sb(f"ea{u}", [PAIRS * 2, G], BF16, ctx) for u in range(2)]
            same = [sb(f"samea{u}", [P, TILES, P], F32, ctx) for u in range(2)]
            zr = sb("zr", [P, TILES, D], F32, ctx)
            eT = sb("eT", [P, G], F32, ctx)
            zb, zT = sb("zba", [P, G], F32, ctx), sb("zT", [P, G], F32, ctx)
            run = sb("run", [HEADS, G], F32, ctx)
            mx = [sb(f"mx{u}", [HEADS, G + 1], F32, ctx) for u in range(2)]
            off = sb("off", [HEADS, G], F32, ctx)
            dcar = sb("dcar", [HEADS, TILES], F32, ctx)
            ecar = sb("ecar", [1, TILES * HEADS], F32, ctx)
            ecx = [sb(f"ecx{u}", [1, TILES, ROW3], F32, ctx) for u in range(2)]
            pay = [sb(f"pay{u}", [P, TILES, ROW3], F32, ctx) for u in range(2)]
            carry = [sb(f"carrya{j}", [1, ROW3], F32, ctx) for j in range(2)]
            carrs = sb("carrs", [1, ROW3], F32, ctx)
            osum = [sb(f"osuma{u}", [P, TILES, ROWA], F32, ctx) for u in range(2)]
            ps_z, ps_al, ps_t = pb("psa_z", ctx=ctx), pb("psa_al", ctx=ctx), pb("psa_t", ctx=ctx)
            ps_e = pb("psa_e", ctx=ctx)
            ps_a = [pb(f"psa_a{k}", ctx=ctx) for k in range(TILES)]
            WE, WM, WC = 0, TILES * HEADS, 2 * TILES * HEADS

            gidx_set, sidx_set = sem2("a_gidx_set"), sem2("a_sidx_set")
            gathered, scattered, rows_in = sem2("a_gathered"), sem2("a_scattered"), sem2("a_rows_in")
            z_ps, z_sb, al_ps, off_sb, mx_sb, t_ps = (sem("a_" + s) for s in ("z_ps", "z_sb", "al_ps", "off_sb", "mx_sb", "t_ps"))
            e_ps, e_sb, zr_sb = sem("a_e_ps"), sem("a_e_sb"), sem("a_zr")
            w_sb, ecar_sb, ecx_sb, pay_sb, max_out = (sem("a_" + s) for s in ("w_sb", "ecar_sb", "ecx_sb", "pay_sb", "max_out"))
            same_ready, agg_ps, carry_ready, carry_scaled = sem2("a_same"), sem("a_agg_ps"), sem("a_carry"), sem("a_carrs")
            osum_ready, run_sb, dcar_sb = sem2("a_osum"), sem("a_run"), sem("a_dcar")
            init, zb_sb = sem("a_init"), sem("a_zb")
            block = ctx.enter_context(nc.Block())

            @block.sync
            def _(sp):
                def group(i, u):
                    g = i * 2 + u
                    need(sp, same_ready[u], i, gate)
                    need(sp, agg_ps, (g - 1) * TILES, gate)
                    need(sp, mx_sb, g - 1, gate)
                    sp.dma_start(drow[u][:, :], dst_row[bass.ds(g, 1), :].rearrange("o q -> (o q)").partition_broadcast(P)
                                 ).then_inc(rows_in[u], 16)
                    sp.dma_start(frow[u][:, :], masks[bass.ds(g, 1), 2, :]).then_inc(rows_in[u], 16)
                    sp.dma_start(reset[u][:, :, :], masks[bass.ds(g, 1), 0:2, :].rearrange("o j q -> (o j) q").partition_broadcast(HEADS)
                                 ).then_inc(rows_in[u], 16)
                    sp.dma_start(ea[u][:, :], ea_parts[bass.ds(g, 1), :, :].rearrange("o j q -> (o j) q")).then_inc(rows_in[u], 16)
                run_groups(sp, group, EG)

            @block.gpsimd
            def _(pool):
                def hold(sem_, value):
                    need(pool, sem_, value, gate)

                def gather(i, u):
                    g = i * 2 + u
                    hold(pay_sb, g - 1)
                    hold(gathered[u], i * (16 * 2 * TILES))
                    nc.gpsimd.tensor_copy(gidx[u][:, :, :], idx[:, bass.ds(g, 1), 0:2, :].rearrange("p o j k -> p (o j) k")
                                          ).then_inc(gidx_set[u], 1)
                    hold(gidx_set[u], i + 1)
                    for table, rows, j in ((xl_t, gl, 0), (xr_t, gr, 1)):
                        for k in range(TILES):
                            pool.indirect_dma_start(
                                out=rows[u][:, k, :], out_offset=None, in_=table,
                                in_offset=bass.IndirectOffsetOnAxis(ap=gidx[u][:, j, k:k + 1], axis=0)).then_inc(gathered[u], 16)

                def scatter(i, u):
                    g = i * 2 + u
                    hold(scattered[u], i * (16 * TILES))
                    nc.gpsimd.tensor_copy(sidx[u][:, :], idx[:, bass.ds(g, 1), 2, :].rearrange("p o k -> p (o k)")
                                          ).then_inc(sidx_set[u], 1)
                    hold(sidx_set[u], i + 1)
                    hold(osum_ready[u], i + 1)
                    for k in range(TILES):
                        pool.indirect_dma_start(
                            out=sums1, out_offset=bass.IndirectOffsetOnAxis(ap=sidx[u][:, k:k + 1], axis=0),
                            in_=osum[u][:, k, :], in_offset=None, bounds_check=NP - 1, oob_is_err=False).then_inc(scattered[u], 16)

                run_stages(pool, [(scatter, 3), (gather, 0)], EG)
                for u in range(2):
                    pool.wait_ge(scattered[u], 16 * TILES * EHALF)

            @block.tensor
            def _(pe):
                pe.wait_ge(init, 1)

                def edge_term(i, u):
                    g = i * 2 + u
                    pe.wait_ge(rows_in[u], (i + 1) * 64)
                    need(pe, e_sb, g)
                    nc.tensor.matmul(ps_e[:, :], we18[:, :], ea[u][:, :], start=True, stop=True).then_inc(e_ps, 1)

                def turn(i, u):
                    g = i * 2 + u
                    pe.wait_ge(zr_sb, g + 1)
                    need(pe, zb_sb, g)
                    for k in range(TILES):
                        last = nc.tensor.transpose(ps_z[:, k * P:(k + 1) * P], zr[:, k, :], ident[:, :])
                    last.then_inc(z_ps, 1)

                def scores(i, u):
                    g = i * 2 + u
                    pe.wait_ge(z_sb, g + 1)
                    need(pe, off_sb, g)
                    nc.tensor.matmul(ps_al[0:HEADS, :], attb[:, :], zT[:, :], start=True, stop=True).then_inc(al_ps, 1)

                def turn_back(i, u):
                    g = i * 2 + u
                    pe.wait_ge(off_sb, g + 1)
                    pe.wait_ge(dcar_sb, g * 2 + 2)
                    need(pe, max_out, g)
                    pe.sem_inc(gate, 1)
                    for k in range(TILES):
                        nc.tensor.transpose(ps_t[:, WE + k * HEADS:WE + (k + 1) * HEADS], off[:, k * P:(k + 1) * P],
                                            ident[0:HEADS, 0:HEADS])
                        nc.tensor.transpose(ps_t[:, WM + k * HEADS:WM + (k + 1) * HEADS], mx[u][:, k * P:(k + 1) * P],
                                            ident[0:HEADS, 0:HEADS])
                    for k in range(TILES):
                        last = nc.tensor.transpose(ps_t[0:1, WC + k * HEADS:WC + (k + 1) * HEADS], dcar[:, k:k + 1],
                                                   ident[0:HEADS, 0:HEADS])
                    last.then_inc(t_ps, 1)

                def sums(n):
                    k = TILES - 1 - n

                    def stage(i, u):
                        g = i * 2 + u
                        if n == 0:
                            pe.wait_ge(same_ready[u], i + 1)
                            pe.wait_ge(pay_sb, g + 1)
                            need(pe, osum_ready[1 - u], i + u)
                        nc.tensor.matmul(ps_a[k][:, 0:ROW3], same[u][:, k, :], pay[u][:, k, :], start=True, stop=False)
                        pe.wait_ge(carry_scaled, g * TILES + (n + 1))
                        nc.tensor.matmul(ps_a[k][:, 0:ROW3], frow[u][:, k * P:(k + 1) * P], carrs[:, :],
                                         start=False, stop=True).then_inc(agg_ps, 1)
                    return stage
                run_stages(pe, [(edge_term, 0), (sums(0), 1), (turn, 0), (sums(1), 1), (sums(2), 1), (scores, 0),
                                (sums(3), 1), (turn_back, 0)], EG)

            @block.scalar
            def _(act):
                def edge_term(i, u):
                    g = i * 2 + u
                    act.wait_ge(e_ps, g + 1)
                    need(act, zb_sb, g)
                    nc.scalar.activation(eT[:, :], ps_e[:, :], ACT.Identity, bias=bz).then_inc(e_sb, 1)

                def results(i, u):
                    g = i * 2 + u
                    for n, k in enumerate(reversed(range(TILES))):
                        act.wait_ge(carry_ready, g * TILES + (n + 1))
                        last = nc.scalar.activation(osum[u][:, k, 0:ROW3], ps_a[k][:, 0:ROW3], ACT.Copy)
                    last.then_inc(osum_ready[u], 1)

                def weights(i, u):
                    g = i * 2 + u
                    act.wait_ge(t_ps, g + 1)
                    need(act, agg_ps, (g - 1) * TILES)
                    nc.scalar.activation(pay[u][:, :, D:ROW3], ps_t[:, WE:WE + TILES * HEADS].rearrange("p (k h) -> p k h", k=TILES),
                                         ACT.Exp).then_inc(w_sb, 1)
                    need(act, ecx_sb, g)
                    nc.scalar.activation(ecar[:, :], ps_t[0:1, WC:WC + TILES * HEADS], ACT.Exp).then_inc(ecar_sb, 1)
                    need(act, scattered[u], i * (16 * TILES))
                    nc.scalar.activation(osum[u][:, :, ROW3:ROWA], ps_t[:, WM:WM + TILES * HEADS].rearrange("p (k h) -> p k h", k=TILES),
                                         ACT.Copy).then_inc(max_out, 1)
                run_stages(act, [(edge_term, 0), (results, 1), (weights, 0)], EG)

            @block.vector
            def _(dve):
                nc.vector.memset(mx[0][:, :], 0.0)
                nc.vector.memset(mx[1][:, :], 0.0)
                nc.vector.memset(carry[0][:, :], 0.0)
                nc.vector.memset(carry[1][:, :], 0.0).then_inc(init, 1)
                dve.wait_ge(init, 1)

                def add_rows(i, u):
                    g = i * 2 + u
                    dve.wait_ge(gathered[u], (i + 1) * (16 * 2 * TILES))
                    need(dve, z_ps, g)
                    nc.vector.tensor_tensor(zr[:, :, :], gl[u][:, :, 0:D], gr[u][:, :, :], ALU.add).then_inc(zr_sb, 1)

                def compare(i, u):
                    g = i * 2 + u
                    dve.wait_ge(rows_in[u], (i + 1) * 64)
                    need(dve, agg_ps, (g - 1) * TILES)
                    nc.vector.tensor_tensor(same[u][:, :, :], drow[u][:, :].rearrange("p (k q) -> p k q", k=TILES),
                                            dstf[:, bass.ds(g * TILES, TILES)].unsqueeze(2).broadcast_to([P, TILES, P]),
                                            ALU.is_equal).then_inc(same_ready[u], 1)

                def leak(i, u):
                    g = i * 2 + u
                    dve.wait_ge(z_ps, g + 1)
                    dve.wait_ge(e_sb, g + 1)
                    need(dve, z_sb, g)
                    nc.vector.tensor_tensor(zb[:, :], eT[:, :], ps_z[:, :], ALU.add).then_inc(zb_sb, 1)
                    dve.wait_ge(zb_sb, g + 1)
                    need(dve, al_ps, g)
                    nc.vector.scalar_tensor_tensor(zT[:, :], zb[:, :], SLOPE, zb[:, :], ALU.mult, ALU.max).then_inc(z_sb, 1)

                def running_maximum(i, u):
                    g = i * 2 + u
                    dve.wait_ge(al_ps, g + 1)
                    nc.vector.tensor_tensor_scan(run[:, ::-1], reset[u][:, 0, ::-1], ps_al[0:HEADS, ::-1], mx[1 - u][:, 0:1],
                                                 ALU.add, ALU.max).then_inc(run_sb, 1)

                def maxima(i, u):
                    g = i * 2 + u
                    dve.wait_ge(run_sb, g + 1)
                    need(dve, t_ps, g - 1)
                    nc.vector.tensor_copy(mx[u][:, G:G + 1], mx[1 - u][:, 0:1])
                    nc.vector.tensor_tensor_scan(mx[u][:, 0:G], reset[u][:, 1, :], run[:, :], 0.0, ALU.add, ALU.max
                                                 ).then_inc(mx_sb, 1)
                    dve.wait_ge(mx_sb, g + 1)
                    need(dve, t_ps, g)
                    edge = mx[u][:, 0:G].rearrange("h (k q) -> h k q", k=TILES)[:, :, P - 1]
                    nc.vector.tensor_tensor(dcar[:, :], mx[u][:, P:G + 1:P], edge, ALU.subtract).then_inc(dcar_sb, 1)
                    nc.vector.tensor_tensor(off[:, :], ps_al[0:HEADS, :], mx[u][:, 0:G], ALU.subtract).then_inc(off_sb, 1)
                    dve.wait_ge(dcar_sb, g * 2 + 1)
                    nc.vector.tensor_scalar(dcar[:, :], dcar[:, :], 0.0, None, ALU.min).then_inc(dcar_sb, 1)

                def payload(i, u):
                    g = i * 2 + u
                    dve.wait_ge(w_sb, g + 1)
                    for k in range(TILES):
                        last = nc.vector.tensor_tensor(pay[u][:, k, 0:D].rearrange("p (h c) -> p h c", h=HEADS),
                                                       gl[u][:, k, 0:D].rearrange("p (h c) -> p h c", h=HEADS),
                                                       pay[u][:, k, D:ROW3].unsqueeze(2).broadcast_to([P, HEADS, C]), ALU.mult)
                    last.then_inc(pay_sb, 1)
                    dve.wait_ge(ecar_sb, g + 1)
                    e2 = ecar[:, :].rearrange("o (k h) -> o k h", k=TILES)
                    for k in range(TILES):
                        nc.vector.tensor_copy(ecx[u][:, k, 0:D].rearrange("o (h c) -> o h c", h=HEADS),
                                              e2[:, k, :].unsqueeze(2).broadcast_to([1, HEADS, C]))
                    nc.vector.tensor_copy(ecx[u][:, :, D:ROW3], e2).then_inc(ecx_sb, 1)

                def scale(n):
                    def stage(i, u):
                        g = i * 2 + u
                        if n == 0:
                            dve.wait_ge(ecx_sb, g + 1)
                        need(dve, agg_ps, g * TILES + n)
                        need(dve, carry_ready, g * TILES + n)
                        nc.vector.tensor_tensor(carrs[:, :], carry[(n + 1) % 2][:, :], ecx[u][:, TILES - 1 - n, :], ALU.mult
                                                ).then_inc(carry_scaled, 1)
                    return stage

                def take(n):
                    def stage(i, u):
                        g = i * 2 + u
                        dve.wait_ge(agg_ps, g * TILES + (n + 1))
                        nc.vector.tensor_copy(carry[n % 2][:, :], ps_a[TILES - 1 - n][0:1, 0:ROW3]).then_inc(carry_ready, 1)
                    return stage
                run_stages(dve, [(scale(0), 1), (add_rows, 0), (take(0), 1), (scale(1), 1), (compare, 0), (take(1), 1),
                                 (scale(2), 1), (leak, 0), (take(2), 1), (scale(3), 1), (running_maximum, 0), (take(3), 1),
                                 (maxima, 0), (payload, 0)], EG)

        with ExitStack() as ctx:
            sn = [sb(f"sn3{u}", [P, TILES, ROWA], F32, ctx) for u in range(2)]
            ln = [sb(f"ln3{u}", [P, TILES, ROW3], F32, ctx) for u in range(2)]
            x1 = [sb(f"x13{u}", [P, TILES, D], F32, ctx) for u in range(2)]
            xb = [sb(f"xb3{u}", [P, TILES, D], F32, ctx) for u in range(2)]
            top_ = sb("top3", [P, TILES, HEADS], F32, ctx)
            dd = sb("dd3", [P, 2, TILES, HEADS], F32, ctx)
            ff = [sb(f"ff3{u}", [P, 2, TILES, HEADS], F32, ctx) for u in range(2)]
            den = sb("den3", [P, TILES, HEADS], F32, ctx)
            a1, a2 = ([sb(f"{name}{u}", [P, TILES, D], F32, ctx) for u in range(2)] for name in ("a13", "a23"))
            ex, el = ([sb(f"{name}{u}", [P, G], F32, ctx) for u in range(2)] for name in ("ex3", "el3"))
            lin = sb("lin3", [P, G], F32, ctx)
            r = [sb(f"r3{u}", [P, TILES, D], F32, ctx) for u in range(2)]
            o = [sb(f"o3{u}", [P, TILES, D], F32, ctx) for u in range(2)]
            stats = sb("st3", [P, TILES, 6], F32, ctx)
            mv = [sb(f"mv3{u}", [P, TILES, 2], F32, ctx) for u in range(2)]
            tiny = [sb(f"ty3{u}", [P, 3, TILES], F32, ctx) for u in range(2)]
            ps_g, ps_o = ([pb(f"{name}{u}", ctx=ctx) for u in range(2)] for name in ("ps3_g", "ps3_o"))
            rows_in, x_in, stored = sem2("n3_in"), sem2("n3_x_in"), sem2("n3_stored")
            top_sb, wstep, stat_sb, mv_sb, dstep = (sem("n3_" + s) for s in ("top", "wstep", "stat", "mv", "step"))
            d_sb, f_sb, ff_sb, a_sb, a_ps, ex_sb, lin_sb, el_sb, o_ps, xb_sb, r_sb, nrm, o_sb = (sem("n3_" + s) for s in
                ("d", "f", "ff", "a", "a_ps", "ex", "lin", "el", "o_ps", "xb", "r", "nrm", "o"))
            block = ctx.enter_context(nc.Block())

            def heads(t):
                return t.rearrange("p (h c) -> p h c", h=HEADS)

            @block.sync
            def _(sp):
                def load(i, u):
                    g = i * 2 + u
                    need(sp, a_sb, g - 1, gate)
                    sp.dma_start(sn[u][:, :, :], group_rows(sums1, g, ROWA)).then_inc(rows_in[u], 16)
                    sp.dma_start(ln[u][:, :, :], group_rows(xl_t, g, ROW3)).then_inc(rows_in[u], 16)

                def load_x1(i, u):
                    g = i * 2 + u
                    need(sp, xb_sb, g - 1, gate)
                    sp.dma_start(x1[u][:, :, :], group_rows(x1_t, g, D)).then_inc(x_in[u], 16)

                def store(i, u):
                    g = i * 2 + u
                    need(sp, o_sb, g + 1, gate)
                    sp.dma_start(group_rows(out, g, D), o[u][:, :, :]).then_inc(stored[u], 16)
                run_stages(sp, [(load_x1, 3), (store, 7), (load, 0)], GROUPS)
                for u in range(2):
                    sp.wait_ge(stored[u], 16 * HALF)

            @block.gpsimd
            def _(pool):
                def with_bias(i, u):
                    g = i * 2 + u
                    need(pool, x_in[u], (i + 1) * 16, gate)
                    need(pool, r_sb, g - 1, gate)
                    nc.gpsimd.tensor_tensor(xb[u][:, :, :], x1[u][:, :, :], bout[:, :].unsqueeze(1).broadcast_to([P, TILES, D]),
                                            ALU.add).then_inc(xb_sb, 1)

                def weigh(out, rows, part):
                    def stage(i, u):
                        g = i * 2 + u
                        need(pool, ff_sb, g + 1, gate)
                        need(pool, a_ps, g - 1, gate)
                        for k in range(TILES):
                            last = nc.gpsimd.tensor_tensor(heads(out[u][:, k, :]), heads(rows[u][:, k, 0:D]),
                                                           ff[u][:, part, k, :].unsqueeze(2).broadcast_to([P, HEADS, C]),
                                                           ALU.mult)
                        if part == 1:
                            last.then_inc(a_sb, 1)
                    return stage
                run_stages(pool, [(weigh(a1, sn, 0), 1), (weigh(a2, ln, 1), 1), (with_bias, 3)], GROUPS)

            @block.tensor
            def _(pe):
                def project(i, u):
                    g = i * 2 + u
                    pe.wait_ge(el_sb, g + 1)
                    need(pe, r_sb, g - 1)
                    for k in range(TILES):
                        last = nc.tensor.matmul(ps_o[u][:, k * D:(k + 1) * D], el[u][:, k * P:(k + 1) * P], wout[:, :],
                                                start=True, stop=True)
                    last.then_inc(o_ps, 1)

                def join(i, u):
                    g = i * 2 + u
                    need(pe, lin_sb, g - 1)
                    pe.wait_ge(a_sb, g + 1)
                    for k in range(TILES):
                        nc.tensor.matmul(ps_g[u][:, k * P:(k + 1) * P], a1[u][:, k, :], ident[:, :], start=True, stop=False)
                        last = nc.tensor.matmul(ps_g[u][:, k * P:(k + 1) * P], a2[u][:, k, :], ident[:, :], start=False, stop=True)
                    last.then_inc(a_ps, 1)
                run_stages(pe, [(join, 2), (project, 3)], GROUPS)

            @block.scalar
            def _(act):
                def exponentials(i, u):
                    g = i * 2 + u
                    act.wait_ge(a_ps, g + 1)
                    need(act, el_sb, g - 1)
                    nc.scalar.activation(ex[u][:, :], ps_g[u][:, :], ACT.Exp, bias=bc).then_inc(ex_sb, 1)

                def factors(i, u):
                    g = i * 2 + u
                    act.wait_ge(d_sb, g + 1)
                    need(act, a_sb, g - 1)
                    nc.scalar.activation(ff[u][:, :, :, :], dd[:, :, :, :], ACT.Exp).then_inc(f_sb, 1)

                def normalise(i, u):
                    g = i * 2 + u
                    act.wait_ge(nrm, g + 1)
                    need(act, stored[u], i * 16)
                    for k in range(TILES):
                        last = nc.scalar.activation(o[u][:, k, :], r[u][:, k, :], ACT.Identity, bias=tiny[u][:, 1, k:k + 1],
                                                    scale=tiny[u][:, 0, k:k + 1])
                    last.then_inc(o_sb, 1)
                run_stages(act, [(normalise, 6), (exponentials, 2), (factors, 0)], GROUPS)

            @block.vector
            def _(dve):
                def maxima(i, u):
                    g = i * 2 + u
                    dve.wait_ge(rows_in[u], (i + 1) * 32)
                    need(dve, d_sb, g)
                    nc.vector.tensor_tensor(top_[:, :, :], sn[u][:, :, ROW3:ROWA], ln[u][:, :, D:ROW3], ALU.max).then_inc(top_sb, 1)

                def differences(i, u):
                    g = i * 2 + u
                    dve.wait_ge(top_sb, g + 1)
                    need(dve, f_sb, g)
                    nc.vector.tensor_tensor(dd[:, 0, :, :], sn[u][:, :, ROW3:ROWA], top_[:, :, :], ALU.subtract)
                    nc.vector.tensor_tensor(dd[:, 1, :, :], ln[u][:, :, D:ROW3], top_[:, :, :], ALU.subtract).then_inc(d_sb, 1)

                def linear(i, u):
                    g = i * 2 + u
                    dve.wait_ge(ex_sb, g + 1)
                    need(dve, el_sb, g)
                    nc.vector.tensor_scalar(lin[:, :], ps_g[u][:, :], bcm1, -1.0, ALU.add, ALU.max).then_inc(lin_sb, 1)

                def elu(i, u):
                    g = i * 2 + u
                    dve.wait_ge(lin_sb, g + 1)
                    need(dve, o_ps, g - 1)
                    nc.vector.scalar_tensor_tensor(el[u][:, :], ex[u][:, :], 1.0, lin[:, :], ALU.min, ALU.add).then_inc(el_sb, 1)

                def residual(i, u):
                    g = i * 2 + u
                    dve.wait_ge(o_ps, g + 1)
                    dve.wait_ge(xb_sb, g + 1)
                    need(dve, o_sb, g - 1)
                    nc.vector.tensor_tensor(r[u][:, :, :], xb[u][:, :, :], ps_o[u][:, :].rearrange("p (k d) -> p k d", k=TILES),
                                            ALU.add).then_inc(r_sb, 1)

                def denominators(n):
                    def stage(i, u):
                        g = i * 2 + u
                        if n == 0:
                            dve.wait_ge(f_sb, g + 1)
                            last = nc.vector.tensor_tensor(den[:, :, :], sn[u][:, :, D:ROW3], ff[u][:, 0, :, :], ALU.mult)
                        else:
                            dve.wait_ge(wstep, g * 3 + n)
                        if n == 1:
                            last = nc.vector.tensor_tensor(den[:, :, :], den[:, :, :], ff[u][:, 1, :, :], ALU.add)
                        if n == 2:
                            last = nc.vector.reciprocal(den[:, :, :], den[:, :, :])
                        if n < 3:
                            last.then_inc(wstep, 1)
                        else:
                            nc.vector.tensor_tensor(ff[u][:, :, :, :], ff[u][:, :, :, :],
                                                    den[:, :, :].unsqueeze(1).broadcast_to([P, 2, TILES, HEADS]), ALU.mult
                                                    ).then_inc(ff_sb, 1)
                    return stage

                stat, aggregate, t = norm_stages(nc, dve, gate, r, r_sb, stats, mv, tiny, stat_sb, mv_sb, dstep, o_sb, nrm)
                dn = [denominators(n) for n in range(4)]
                run_stages(dve, [(stat[0], 5), (stat[1], 5), (stat[2], 5), (stat[3], 5), (aggregate, 5), (t[0], 5), (linear, 3),
                                 (t[1], 5), (elu, 3), (t[2], 5), (maxima, 0), (t[3], 5), (differences, 0), (t[4], 5), (t[5], 5),
                                 (residual, 4), (t[6], 5), (dn[0], 0), (t[7], 5), (dn[1], 0), (t[8], 5), (dn[2], 0), (t[9], 5),
                                 (dn[3], 0), (t[10], 5), (t[11], 5), (t[12], 5)], GROUPS)


_WEIGHTS = ["L0_gnn_W_msg", "L0_gnn_b_msg", "L0_gnn_W_upd", "L0_gnn_b_upd", "L0_gnn_prelu_a", "L0_gnn_gamma", "L0_gnn_beta",
            "L1_gnn_w_in", "L1_gnn_b_in", "L1_gnn_w_l", "L1_gnn_b_l", "L1_gnn_w_r", "L1_gnn_b_r", "L1_gnn_w_e", "L1_gnn_att",
            "L1_gnn_bias_conv", "L1_gnn_w_out", "L1_gnn_b_out"]


def kernel(**inputs):
    import numpy as np
    import concourse.bacc as bacc
    from concourse.bass_utils import run_bass_kernel_spmd as run

    x = np.asarray(inputs["x"])
    src, dst, ea = (np.asarray(inputs[k]) for k in ("src", "dst", "edge_attr_2"))
    n, e = x.shape[0], src.shape[0]
    pair = 2 * G
    n_pad, e_pad = -(-n // pair) * pair, -(-e // pair) * pair

    def rows(a):
        return np.ascontiguousarray(a.reshape(-1, G)[:, ::-1])

    def cols(a):
        return np.ascontiguousarray(rows(a).reshape(-1, P).T)

    src_e = np.pad(src, (0, e_pad - e))
    dst_e = np.pad(dst, (0, e_pad - e), constant_values=n)
    next_e = np.pad(dst_e[1:], (0, 1), constant_values=n + 1)
    prev_e = np.pad(dst_e[:-1], (1, 0), constant_values=-1)
    arrays = {
        "x": np.pad(x, ((0, n_pad - n), (0, 0))),
        "src_col": cols(src_e), "dst_col": cols(dst_e), "next_col": cols(next_e),
        "dst_row": rows(dst_e), "next_row": rows(next_e), "prev_row": rows(prev_e),
        "before_row": np.ascontiguousarray(prev_e[::G, None]),
        "ea_row": np.ascontiguousarray(np.pad(ea, ((0, e_pad - e), (0, 0))).reshape(-1, G, 2)[:, ::-1].transpose(0, 2, 1)),
    }
    for name in _WEIGHTS:
        arrays[name] = np.asarray(inputs[name])
    nc = bacc.Bacc("TRN2", target_bir_lowering=False, num_devices=1)
    args = [nc.dram_tensor("in_" + k, a.shape, mybir.dt.from_np(a.dtype), kind="ExternalInput").ap() for k, a in arrays.items()]
    out = nc.dram_tensor("out", (n_pad, D), F32, kind="ExternalOutput").ap()
    build(nc, *args, out, n, e)
    r = run(nc, [{"in_" + k: a for k, a in arrays.items()}], core_ids=[0])
    return r.results[0]["out"][:n]
```

```python
from contextlib import ExitStack

import concourse.bass as bass
from concourse import mybir
from concourse.alu_op_type import AluOpType as ALU

P = 128
D = 128
HEADS, C = 4, 32
TILES = 4
G = P * TILES
ROW3 = D + HEADS
ROWA = ROW3 + HEADS
BIG = 1.0e30
SKIP = 1 << 20
EPS = 1.0e-5
SLOPE = 0.2
LN_LINKS = 13

WINDOW = 2 * P
HALVES = WINDOW // P
PARTS = 3
PAIRS = PARTS * PARTS

F32, I32, BF16 = mybir.dt.float32, mybir.dt.int32, mybir.dt.bfloat16
ACT = mybir.ActivationFunctionType
AX = mybir.AxisListType


def group_rows(table, g, width):
    return table[bass.ds(g * G, G), 0:width].rearrange("(p k) w -> p k w", k=TILES)


def need(eng, sem, value, gate=None):
    if isinstance(value, int) and value <= 0:
        return
    eng.wait_ge(sem, value)
    if gate is not None:
        eng.sem_inc(gate, 1)


def run_stages(eng, stages, groups):
    def step(i, u, least, most):
        for stage, lag in stages:
            if least <= lag <= most:
                stage(i + (u - lag) // 2, (u - lag) % 2)
    deepest = max(lag for _, lag in stages)
    pairs = groups // 2
    first = (deepest + 1) // 2 + 1
    first += (pairs - first) % 2
    for g in range(2 * first):
        step(g // 2, g % 2, 0, g)
    with eng.Fori(0, (pairs - first) // 2) as j:
        for u in range(4):
            step(j * 2 + first, u, 0, deepest)
    for g in range(groups, groups + deepest):
        step(g // 2, g % 2, g - groups + 1, deepest)


def run_groups(eng, body, groups):
    for u in range(2):
        body(0, u)
    with eng.Fori(1, groups // 2) as i:
        for u in range(2):
            body(i, u)


def inv_sqrt_steps(nc, y, v, t):
    newton = [lambda: nc.vector.scalar_tensor_tensor(t, y, -0.5, y, ALU.mult, ALU.mult),
              lambda: nc.vector.tensor_tensor(t, t, v, ALU.mult),
              lambda: nc.vector.scalar_tensor_tensor(y, t, 1.5, y, ALU.add, ALU.mult)]
    return [lambda: nc.vector.tensor_scalar(v, v, EPS, None, ALU.add),
            lambda: nc.vector.tensor_scalar(t.bitcast(I32), v.bitcast(I32), 1, None, ALU.logical_shift_right),
            lambda: nc.vector.tensor_scalar(y.bitcast(I32), t.bitcast(I32), -1.0, float(0x5F3759DF), ALU.mult, ALU.add),
            *newton, *newton, *newton]


def load_windows(sp, i, u, table, windows, bases, loaded):
    for k in range(TILES):
        base = sp.value_load(bases[0:1, bass.ds((i * 2 + u) * TILES + k, 1)], min_val=0, max_val=table.shape[0] - WINDOW)
        sp.dma_start(windows[u][:, k, :, :], table[bass.ds(base, WINDOW), 0:D].rearrange("(w p) d -> p w d", p=P)
                     ).then_inc(loaded[u], 16)


def gather_wide(pool, gate, i, u, table, windows, rows, wide, loaded, wide_in, whole):
    count = pool.value_load(wide[0:1, bass.ds(i * 2 + u, 1)], min_val=0, max_val=16 * TILES * wide.shape[1])
    with pool.If(count):
        need(pool, loaded[u], (i + 1) * (16 * TILES), gate)
        for k in range(TILES):
            pool.indirect_dma_start(
                out=windows[u][:, k, 0, :], out_offset=None, in_=table,
                in_offset=bass.IndirectOffsetOnAxis(ap=rows[u][:, 1, k:k + 1], axis=0)).then_inc(wide_in, 16)
        pool.wait_ge(wide_in, count)
    pool.sem_inc(whole, 1)


def norm_stages(nc, dve, gate, src, src_ready, stats, mv, tiny, stat_sb, mv_sb, step, used, done):
    def stat(k):
        def stage(i, u):
            g = i * 2 + u
            if k == 0:
                dve.wait_ge(src_ready, g + 1)
                need(dve, mv_sb, g)
                dve.sem_inc(gate, 1)
            last = nc.vector.bn_stats(stats[:, k, :], src[u][:, k, :])
            if k == TILES - 1:
                last.then_inc(stat_sb, 1)
        return stage

    def aggregate(i, u):
        g = i * 2 + u
        dve.wait_ge(stat_sb, g + 1)
        need(dve, done, g - 1)
        dve.sem_inc(gate, 1)
        for k in range(TILES):
            last = nc.vector.bn_aggr(mv[u][:, k, :], stats[:, k, :])
        last.then_inc(mv_sb, 1)

    def link(n):
        def stage(i, u):
            g = i * 2 + u
            y, shift, t = (tiny[u][:, j, :] for j in range(3))
            if n == 0:
                dve.wait_ge(mv_sb, g + 1)
                need(dve, used, g - 1)
            else:
                dve.wait_ge(step, g * (LN_LINKS - 1) + n)
            steps = inv_sqrt_steps(nc, y, mv[u][:, :, 1], t)
            if n < len(steps):
                steps[n]().then_inc(step, 1)
            else:
                nc.vector.scalar_tensor_tensor(shift, mv[u][:, :, 0], -1.0, y, ALU.mult, ALU.mult).then_inc(done, 1)
        return stage
    return [stat(k) for k in range(TILES)], aggregate, [link(n) for n in range(LN_LINKS)]


def build(nc, x, src_col, dst_col, next_col, dst_row, next_row, prev_row, before_row, ea_row,
          W_msg, b_msg, W_upd, b_upd, prelu_a, gamma, beta,
          w_in, b_in, w_l, b_l, w_r, b_r, w_e, att, bias_conv, w_out, b_out, out, n_nodes, n_edges):
    NP = x.shape[0]
    GROUPS = NP // G
    EG = dst_row.shape[0]
    ET = EG * TILES
    VALID = n_nodes - (GROUPS - 1) * G
    assert GROUPS == EG and EG % 2 == 0 and VALID % TILES == 0 and VALID > 0
    HALF = GROUPS // 2
    EHALF = EG // 2

    def scratch(name, shape):
        return nc.dram_tensor(name, shape, F32, kind="Internal").ap()

    sums0 = scratch("sums0", (NP, D))
    h_t = scratch("h_t", (D, NP))
    x1_t = scratch("x1", (NP, D))
    xl_t = scratch("xl", (NP, ROW3))
    xr_t = scratch("xr", (NP, D))
    sums1 = scratch("sums1", (NP, ROWA))
    positions = scratch("positions", (EG, G))
    bases_t = nc.dram_tensor("bases_t", (EG, TILES), I32, kind="Internal").ap()
    wide_t = scratch("wide_t", (EG, 1))
    masks = scratch("masks", (EG, 3, G))
    ea_parts = nc.dram_tensor("ea_parts", (EG, PAIRS * 2, G), BF16, kind="Internal").ap()
    we_parts = nc.dram_tensor("we_parts", (3, 2, D), BF16, kind="Internal").ap()

    top = ExitStack()
    with top:
        def sb(name, shape, dt=F32, ctx=top):
            return ctx.enter_context(nc.sbuf_tensor(name, shape, dt))

        def pb(name, shape=(P, G), ctx=top):
            return ctx.enter_context(nc.psum_tensor(name, list(shape), F32))

        def sem(name):
            return top.enter_context(nc.semaphore(name))

        def sem2(name):
            return [sem(f"{name}{u}") for u in range(2)]

        ident = sb("ident", [P, P])
        ones_col = sb("ones_col", [P, 1])
        wm = sb("wm", [P, 2, D])
        wu = sb("wu", [P, 2, D])
        win = sb("win", [P, D])
        wlr = sb("wlr", [P, 2, D])
        wsum = sb("wsum", [P, D])
        wout = sb("wout", [P, D])
        we = sb("we", [2, D])
        we18 = sb("we18", [PAIRS * 2, D], BF16)
        attb = sb("attb", [P, HEADS])
        cols = sb("cols", [P, 12])
        bmsg, bupd, gam, bet, bin_, bl, br, bconv, alpha, binm1, bz, bself = (cols[:, j:j + 1] for j in range(12))
        cols2 = sb("cols2", [P, 8])
        bc, bcm1, bn_scale, bn_shift = (cols2[:, j:j + 1] for j in range(4))
        bout = sb("bout", [P, D])
        srcc = sb("srcc", [P, ET], I32)
        dstc = sb("dstc", [P, ET], I32)
        nextc = sb("nextc", [P, ET], I32)
        dstf = sb("dstf", [P, ET])
        idx = sb("idx", [P, EG, 3, TILES], I32)
        bn = sb("bn", [P, GROUPS - 1 + TILES, 6])
        bnmv = sb("bnmv", [P, 2])
        lane = sb("lane", [P, HALVES])
        bases = sb("bases", [1, EG * TILES], I32)
        wide = sb("wide", [1, EG], I32)
        chained, links = sem("chained"), [0]
        blank = sb("blank", [P, TILES, ROWA])
        cleared0, cleared1 = sem("cleared0"), sem("cleared1")
        init = sem("init")
        gate = sem("gate")

        with ExitStack() as ctx:
            rows = sb("rows", [EG, 4, G], I32, ctx)
            rowf = sb("rowf", [EG, 4, G], F32, ctx)
            lanes, lanef = sb("lanes", [EG, G], I32, ctx), sb("lanef", [EG, G], F32, ctx)
            lanec = sb("lanec", [P, HALVES], I32, ctx)
            base, widef = sb("base", [EG, TILES], F32, ctx), sb("widef", [EG, 1], F32, ctx)
            basei, ones_row = sb("basei", [EG, TILES], I32, ctx), sb("ones_row", [1, EG], F32, ctx)
            wide_row, wide_sum = sb("wide_row", [1, EG], F32, ctx), sb("wide_sum", [1, EG], F32, ctx)
            pos = sb("pos", [EG, G], F32, ctx)
            befo = sb("befo", [EG, 1], I32, ctx)
            befof = sb("befof", [EG, 1], F32, ctx)
            mask = sb("mask", [EG, 3, G], F32, ctx)
            keep = sb("keep", [P, ET], F32, ctx)
            eag = sb("eag", [EG, 2, G], F32, ctx)
            eas = sb("eas", [EG, 2], F32, ctx)
            emean = sb("emean", [2, 1], F32, ctx)
            eap = sb("eap", [EG, PARTS, 2, G], BF16, ctx)
            earest = sb("earest", [EG, 2, G], F32, ctx)
            wep = sb("wep", [2, PARTS, D], BF16, ctx)
            werest = sb("werest", [2, D], F32, ctx)
            ps = pb("ps_setup", ctx=ctx)
            loaded = sem("loaded")
            zeros, made = sem("zeros"), sem("made")
            tables_ready = sem("tables_ready")
            mean_sb, mean_ps = sem("mean_sb"), sem("mean_ps")
            att0, att_in = sem("att0"), sem("att_in")
            written, again_in, wide_back = sem("written"), sem("again_in"), sem("wide_back")
            n_loads = 17 + 10
            block = ctx.enter_context(nc.Block())

            @block.sync
            def _(sp):
                def load(dst, src):
                    sp.dma_start(dst, src).then_inc(loaded, 16)
                load(srcc[:, :], src_col)
                load(dstc[:, :], dst_col)
                load(nextc[:, :], next_col)
                load(rows[:, 0, :], dst_row)
                load(rows[:, 1, :], next_row)
                load(rows[:, 2, :], prev_row)
                load(befo[:, :], before_row)
                load(eag[:, :, :], ea_row)
                for j in range(2):
                    load(wm[:, j, :], W_msg[j * D:(j + 1) * D, :])
                    load(wu[:, j, :], W_upd[j * D:(j + 1) * D, :])
                load(win[:, :], w_in)
                load(wlr[:, 0, :], w_l)
                load(wlr[:, 1, :], w_r)
                load(wout[:, :], w_out)
                load(we[:, :], w_e)
                sp.wait_ge(tables_ready, 1)
                sp.dma_start(positions, pos[:, :]).then_inc(written, 16)
                sp.dma_start(bases_t, basei[:, :]).then_inc(written, 16)
                sp.dma_start(wide_t, widef[:, :]).then_inc(written, 16)
                sp.wait_ge(tables_ready, 2)
                sp.dma_start(masks, mask[:, :, :]).then_inc(written, 16)
                sp.wait_ge(tables_ready, 3)
                for j in range(PARTS):
                    sp.dma_start(ea_parts[:, j * 2 * PARTS:(j + 1) * 2 * PARTS, :].rearrange("g (a d) q -> g a d q", a=PARTS),
                                 eap[:, :, :, :]).then_inc(written, 16)
                sp.dma_start(we_parts.rearrange("a d f -> d a f"), wep[:, :, :]).then_inc(written, 16)
                sp.wait_ge(written, 16 * (4 + PARTS + 1))
                for j in range(PARTS):
                    for a in range(PARTS):
                        row = (j * PARTS + a) * 2
                        sp.dma_start(we18[row:row + 2, :], we_parts[j, :, :]).then_inc(again_in, 16)
                sp.dma_start(bases[:, :], bases_t.rearrange("g k -> (g k)").rearrange("(o q) -> o q", o=1)).then_inc(again_in, 16)
                sp.dma_start(wide_row[:, :], wide_t.rearrange("g o -> o g")).then_inc(wide_back, 16)
                sp.wait_ge(again_in, 16 * (PAIRS + 1))

            @block.scalar
            def _(act):
                for col, vec in ((bmsg, b_msg), (bupd, b_upd), (gam, gamma), (bet, beta), (bin_, b_in), (bl, b_l),
                                 (br, b_r), (bconv, bias_conv)):
                    act.dma_start(col, vec.rearrange("(p o) -> p o", o=1)).then_inc(loaded, 16)
                act.dma_start(alpha, prelu_a.partition_broadcast(P)).then_inc(loaded, 16)
                act.dma_start(bout[:, :], b_out.partition_broadcast(P)).then_inc(loaded, 16)
                act.wait_ge(att0, 1)
                for h in range(HEADS):
                    act.dma_start(attb[h * C:(h + 1) * C, h:h + 1], att[h:h + 1, :].rearrange("o c -> c o")).then_inc(att_in, 16)
                act.wait_ge(att_in, 16 * HEADS)
                act.wait_ge(zeros, 1)
                with act.Fori(0, GROUPS) as g:
                    act.dma_start(group_rows(sums0, g, D), blank[:, :, 0:D]).then_inc(cleared0, 16)

            @block.gpsimd
            def _(pool):
                nc.gpsimd.memset(ident[:, :], 0.0).then_inc(made, 1)
                pool.wait_ge(made, 1)
                nc.gpsimd.affine_select(out=ident[:, :], in_=ident[:, :], compare_op=ALU.not_equal, fill=1.0, base=0,
                                        pattern=[[-1, P]], channel_multiplier=1).then_inc(made, 1)
                nc.gpsimd.iota(lanes[:, :].rearrange("g (k p) -> g k p", k=TILES), pattern=[[0, TILES], [1, P]], base=0,
                               channel_multiplier=0).then_inc(made, 1)
                nc.gpsimd.iota(lanec[:, :], pattern=[[P, HALVES]], base=0, channel_multiplier=1).then_inc(made, 1)
                pool.wait_ge(made, 4)

            @block.tensor
            def _(pe):
                pe.wait_ge(mean_sb, 1)
                nc.tensor.matmul(ps[0:2, 0:1], eas[:, :], ones_col[0:EG, :], start=True, stop=True).then_inc(mean_ps, 1)
                pe.wait_ge(mean_sb, 2)
                nc.tensor.matmul(ps[:, 1:2], we[:, :], emean[:, :], start=True, stop=True).then_inc(mean_ps, 1)

            @block.vector
            def _(dve):
                def chain(ins):
                    links[0] += 1
                    ins.then_inc(chained, 1)
                    dve.wait_ge(chained, links[0])

                nc.vector.memset(blank[:, :, ROW3:ROWA], -BIG)
                nc.vector.memset(ones_col[:, :], 1.0)
                nc.vector.memset(blank[:, :, 0:ROW3], 0.0).then_inc(zeros, 1)
                nc.vector.memset(attb[:, :], 0.0).then_inc(att0, 1)
                dve.wait_ge(loaded, 16 * n_loads)
                chain(nc.vector.tensor_copy(dstf[:, :], dstc[:, :]))
                chain(nc.vector.tensor_tensor(keep[:, :], dstc[:, :], nextc[:, :], ALU.is_equal))
                by_group = "p (g k) -> p g k"
                chain(nc.vector.scalar_tensor_tensor(idx[:, :, 2, :], keep[:, :].rearrange(by_group, k=TILES), float(SKIP),
                                                     dstf[:, :].rearrange(by_group, k=TILES), ALU.mult, ALU.add))
                chain(nc.vector.tensor_copy(idx[:, :, 0, :], srcc[:, :].rearrange(by_group, k=TILES)))
                chain(nc.vector.tensor_copy(idx[:, :, 1, :], dstc[:, :].rearrange(by_group, k=TILES)))
                chain(nc.vector.tensor_copy(befof[:, :], befo[:, :]))
                chain(nc.vector.tensor_copy(rowf[:, 0:3, :], rows[:, 0:3, :]))
                tiles = "g (k p) -> g k p"
                chain(nc.vector.tensor_scalar(base[:, :], rowf[:, 0, :].rearrange(tiles, p=P)[:, :, P - 1], float(NP - WINDOW), None,
                                              ALU.min))
                chain(nc.vector.tensor_tensor(pos[:, :].rearrange(tiles, p=P), rowf[:, 0, :].rearrange(tiles, p=P),
                                              base[:, :].unsqueeze(2).broadcast_to([EG, TILES, P]), ALU.subtract))
                chain(nc.vector.tensor_reduce(widef[:, :], pos[:, :].rearrange(tiles, p=P)[:, :, 0], AX.X, ALU.max))
                chain(nc.vector.tensor_scalar(widef[:, :], widef[:, :], float(WINDOW - 1), None, ALU.is_gt))
                dve.wait_ge(made, 4)
                chain(nc.vector.tensor_copy(lanef[:, :], lanes[:, :]))
                chain(nc.vector.tensor_copy(lane[:, :], lanec[:, :]))
                chain(nc.vector.tensor_tensor(lanef[:, :], lanef[:, :], pos[:, :], ALU.subtract))
                chain(nc.vector.scalar_tensor_tensor(pos[:, :], lanef[:, :], widef[:, 0:1], pos[:, :], ALU.mult, ALU.add))
                chain(nc.vector.tensor_copy(basei[:, :], base[:, :]))
                dve.sem_inc(tables_ready, 1)
                chain(nc.vector.tensor_tensor(mask[:, 0, :], rowf[:, 0, :], rowf[:, 2, :], ALU.not_equal))
                chain(nc.vector.tensor_tensor(mask[:, 1, :], rowf[:, 0, :], rowf[:, 1, :], ALU.not_equal))
                chain(nc.vector.memset(mask[:, 1, :].rearrange("g (k p) -> g k p", p=P)[:, :, 0:1], 1.0))
                chain(nc.vector.tensor_scalar(mask[:, 0:2, :], mask[:, 0:2, :], -BIG, None, ALU.mult))
                for k in range(TILES - 1):
                    nc.vector.tensor_scalar(mask[:, 2, k * P:(k + 1) * P], rowf[:, 0, k * P:(k + 1) * P],
                                            rowf[:, 0, (k + 1) * P:(k + 1) * P + 1], None, ALU.is_equal)
                nc.vector.tensor_scalar(mask[:, 2, (TILES - 1) * P:], rowf[:, 0, (TILES - 1) * P:], befof[:, 0:1], None,
                                        ALU.is_equal).then_inc(tables_ready, 1)
                for parts, rest, full in ((eap[:, :, :, :].rearrange("g a d q -> g a (d q)"), earest[:, :, :].rearrange("g d q -> g (d q)"),
                                           eag[:, :, :].rearrange("g d q -> g (d q)")), (wep[:, :, :], werest[:, :], we[:, :])):
                    chain(nc.vector.tensor_copy(parts[:, 0, :], full))
                    chain(nc.vector.tensor_tensor(rest, full, parts[:, 0, :], ALU.subtract))
                    chain(nc.vector.tensor_copy(parts[:, 1, :], rest))
                    chain(nc.vector.tensor_tensor(rest, rest, parts[:, 1, :], ALU.subtract))
                    chain(nc.vector.tensor_copy(parts[:, 2, :], rest))
                dve.sem_inc(tables_ready, 1)
                chain(nc.vector.tensor_reduce(eas[:, :], eag[:, :, :], AX.X, ALU.add))
                dve.sem_inc(mean_sb, 1)
                dve.wait_ge(mean_ps, 1)
                nc.vector.tensor_scalar(emean[:, :], ps[0:2, 0:1], 1.0 / n_edges, None, ALU.mult).then_inc(mean_sb, 1)
                chain(nc.vector.tensor_tensor(bz, bl, br, ALU.add))
                chain(nc.vector.tensor_scalar(binm1, bin_, -1.0, None, ALU.add))
                chain(nc.vector.tensor_tensor(bc, bconv, bl, ALU.add))
                chain(nc.vector.tensor_scalar(bcm1, bc, -1.0, None, ALU.add))
                chain(nc.vector.tensor_tensor(wsum[:, :], wlr[:, 0, :], wlr[:, 1, :], ALU.add))
                dve.wait_ge(mean_ps, 2)
                chain(nc.vector.tensor_tensor(bself, bz, ps[:, 1:2], ALU.add))
                chain(nc.vector.memset(ones_row[:, :], 1.0))
                dve.wait_ge(wide_back, 16)
                chain(nc.vector.tensor_tensor_scan(wide_sum[:, :], ones_row[:, :], wide_row[:, :], 0.0, ALU.mult, ALU.add))
                chain(nc.vector.scalar_tensor_tensor(wide[:, :], wide_sum[:, :], float(16 * TILES), wide_row[:, :], ALU.mult, ALU.mult))

        with ExitStack() as ctx:
            gidx = [sb(f"gidx{u}", [P, 2, TILES], I32, ctx) for u in range(2)]
            sidx = [sb(f"sidx{u}", [P, TILES], I32, ctx) for u in range(2)]
            xe = [sb(f"xe{u}", [P, TILES, D], F32, ctx) for u in range(2)]
            xw = [sb(f"xw{u}", [P, TILES, HALVES, D], F32, ctx) for u in range(2)]
            posb = [sb(f"posb{u}", [P, G], F32, ctx) for u in range(2)]
            pick = [sb(f"pick{u}", [P, HALVES, G], F32, ctx) for u in range(2)]
            drow = [sb(f"drow{u}", [P, G], I32, ctx) for u in range(2)]
            frow = [sb(f"frow{u}", [1, G], F32, ctx) for u in range(2)]
            same = [sb(f"same{u}", [P, TILES, P], F32, ctx) for u in range(2)]
            xT = [[sb(f"xT{j}{u}", [P, G], F32, ctx) for u in range(2)] for j in range(2)]
            mT = [sb(f"mT{u}", [P, G], F32, ctx) for u in range(2)]
            mu = [sb(f"mu{u}", [P, TILES, D + 1], F32, ctx) for u in range(2)]
            carry = [sb(f"carry{j}", [1, D + 1], F32, ctx) for j in range(2)]
            rcnt = sb("rcnt", [P, TILES], F32, ctx)
            osum = [sb(f"osum{u}", [P, TILES, D], F32, ctx) for u in range(2)]
            ps_x = [pb(f"ps_x{j}", ctx=ctx) for j in range(2)]
            ps_m, ps_u = pb("ps_m", ctx=ctx), pb("ps_u", ctx=ctx)
            ps_a = [pb(f"ps_a{k}", ctx=ctx) for k in range(TILES)]

            gidx_set, sidx_set, pos_in = sem("gidx_set"), sem("sidx_set"), sem2("pos_in")
            gathered, scattered, rows_in = sem2("gathered"), sem2("scattered"), sem2("rows_in")
            gathered_t = [sem2(f"xposed{j}_") for j in range(2)]
            xT_ready = [sem(f"xT_ready{j}") for j in range(2)]
            m_ps, m_sb, u_ps, u_sb = sem("m_ps"), sem("m_sb"), sem("u_ps"), sem("u_sb")
            same_ready, agg_ps, carry_ready = sem("same_ready"), sem("agg_ps"), sem("carry_ready")
            osum_ready = sem2("osum_ready")
            win_in, wide_in, whole = sem2("win_in"), sem("wide_in"), sem("whole")
            pick_sb = sem("pick_sb")
            rc = sem("rcnt_ready")
            block = ctx.enter_context(nc.Block())

            @block.sync
            def _(sp):
                def load_windows_and_positions(i, u):
                    need(sp, gathered_t[1][u], i, gate)
                    load_windows(sp, i, u, x, xw, bases, win_in)
                    sp.dma_start(posb[u][:, :], positions[bass.ds(i * 2 + u, 1), :].rearrange("o q -> (o q)").partition_broadcast(P)
                                 ).then_inc(pos_in[u], 16)

                def load_rows(i, u):
                    g = i * 2 + u
                    need(sp, same_ready, g - 1, gate)
                    need(sp, agg_ps, (g - 1) * TILES, gate)
                    sp.dma_start(drow[u][:, :], dst_row[bass.ds(g, 1), :].rearrange("o q -> (o q)").partition_broadcast(P)
                                 ).then_inc(rows_in[u], 16)
                    sp.dma_start(frow[u][:, :], masks[bass.ds(g, 1), 2, :]).then_inc(rows_in[u], 16)
                    sp.dma_start(group_rows(sums1, g, ROWA), blank[:, :, :]).then_inc(cleared1, 16)
                run_stages(sp, [(load_windows_and_positions, 0), (load_rows, 1)], EG)
                sp.wait_ge(cleared1, 16 * EG)

            @block.gpsimd
            def _(pool):
                def hold(sem_, value):
                    need(pool, sem_, value, gate)

                def gather(i, u):
                    g = i * 2 + u
                    hold(gathered_t[0][u], i)
                    hold(gathered[u], i * (16 * TILES))
                    nc.gpsimd.tensor_copy(gidx[u][:, :, :], idx[:, bass.ds(g, 1), 0:2, :].rearrange("p o j k -> p (o j) k")
                                          ).then_inc(gidx_set, 1)
                    hold(gidx_set, g + 1)
                    for k in reversed(range(TILES)):
                        pool.indirect_dma_start(
                            out=xe[u][:, k, :], out_offset=None, in_=x,
                            in_offset=bass.IndirectOffsetOnAxis(ap=gidx[u][:, 0, k:k + 1], axis=0)).then_inc(gathered[u], 16)
                    gather_wide(pool, gate, i, u, x, xw, gidx, wide, win_in, wide_in, whole)

                def scatter(i, u):
                    g = i * 2 + u
                    hold(scattered[u], i * (16 * TILES))
                    nc.gpsimd.tensor_copy(sidx[u][:, :], idx[:, bass.ds(g, 1), 2, :].rearrange("p o k -> p (o k)")
                                          ).then_inc(sidx_set, 1)
                    hold(sidx_set, g + 1)
                    hold(osum_ready[u], i + 1)
                    if isinstance(i, int) and g == 0:
                        hold(cleared0, 16 * GROUPS)
                    for k in range(TILES):
                        pool.indirect_dma_start(
                            out=sums0, out_offset=bass.IndirectOffsetOnAxis(ap=sidx[u][:, k:k + 1], axis=0),
                            in_=osum[u][:, k, :], in_offset=None, bounds_check=NP - 1, oob_is_err=False).then_inc(scattered[u], 16)

                run_stages(pool, [(scatter, 4), (gather, 0)], EG)
                for u in range(2):
                    pool.wait_ge(scattered[u], 16 * TILES * EHALF)

            @block.tensor
            def _(pe):
                pe.wait_ge(init, 1)

                def turn(i, u):
                    g = i * 2 + u
                    pe.wait_ge(gathered[u], (i + 1) * (16 * TILES))
                    need(pe, xT_ready[0], g)
                    for k in range(TILES):
                        last = nc.tensor.transpose(ps_x[0][:, k * P:(k + 1) * P], xe[u][:, k, :], ident[:, :])
                    last.then_inc(gathered_t[0][u], 1)

                def pick_rows(i, u):
                    g = i * 2 + u
                    pe.wait_ge(win_in[u], (i + 1) * (16 * TILES))
                    pe.wait_ge(whole, g + 1)
                    pe.wait_ge(pick_sb, g + 1)
                    need(pe, xT_ready[1], g)
                    for k in range(TILES):
                        for w in range(HALVES):
                            last = nc.tensor.matmul(ps_x[1][:, k * P:(k + 1) * P], xw[u][:, k, w, :], pick[u][:, w, k * P:(k + 1) * P],
                                                    start=w == 0, stop=w == HALVES - 1)
                    last.then_inc(gathered_t[1][u], 1)

                def messages(i, u):
                    g = i * 2 + u
                    pe.wait_ge(xT_ready[0], g + 1)
                    need(pe, m_sb, g)
                    nc.tensor.matmul(ps_m[:, :], wm[:, 0, :], xT[0][u][:, :], start=True, stop=False)
                    pe.wait_ge(xT_ready[1], g + 1)
                    nc.tensor.matmul(ps_m[:, :], wm[:, 1, :], xT[1][u][:, :], start=False, stop=True).then_inc(m_ps, 1)

                def updates(i, u):
                    g = i * 2 + u
                    pe.wait_ge(m_sb, g + 1)
                    need(pe, u_sb, g)
                    for k in range(TILES):
                        last = nc.tensor.matmul(ps_u[:, k * D:(k + 1) * D], mT[u][:, k * P:(k + 1) * P], wu[:, 1, :],
                                                start=True, stop=True)
                    last.then_inc(u_ps, 1)

                def sums(n):
                    k = TILES - 1 - n

                    def stage(i, u):
                        g = i * 2 + u
                        if n == 0:
                            pe.wait_ge(same_ready, g + 1)
                            pe.wait_ge(u_sb, g + 1)
                            pe.wait_ge(rows_in[u], (i + 1) * 32)
                            need(pe, osum_ready[1 - u], i + u)
                        nc.tensor.matmul(ps_a[k][:, 0:D + 1], same[u][:, k, :], mu[u][:, k, :], start=True, stop=False)
                        need(pe, carry_ready, g * TILES + n)
                        nc.tensor.matmul(ps_a[k][:, 0:D + 1], frow[u][:, k * P:(k + 1) * P], carry[(n + 1) % 2][:, :],
                                         start=False, stop=True).then_inc(agg_ps, 1)
                    return stage
                run_stages(pe, [(messages, 1), (sums(0), 2), (turn, 0), (sums(1), 2), (pick_rows, 0), (sums(2), 2), (updates, 1),
                                (sums(3), 2)], EG)

            @block.scalar
            def _(act):
                def copy_x(i, u):
                    act.wait_ge(gathered_t[0][u], i + 1)
                    need(act, m_ps, i * 2 + u - 1)
                    nc.scalar.activation(xT[0][u][:, :], ps_x[0][:, :], ACT.Copy).then_inc(xT_ready[0], 1)

                def relu(i, u):
                    g = i * 2 + u
                    act.wait_ge(m_ps, g + 1)
                    need(act, u_ps, g - 1)
                    nc.scalar.activation(mT[u][:, :], ps_m[:, :], ACT.Relu, bias=bmsg).then_inc(m_sb, 1)

                def hand_over(n):
                    def stage(i, u):
                        act.wait_ge(agg_ps, (i * 2 + u) * TILES + (n + 1))
                        nc.scalar.activation(carry[n % 2][:, :], ps_a[TILES - 1 - n][0:1, 0:D + 1], ACT.Copy).then_inc(carry_ready, 1)
                    return stage
                run_stages(act, [(relu, 1), (hand_over(0), 2), (copy_x, 0), (hand_over(1), 2), (hand_over(2), 2), (hand_over(3), 2)],
                           EG)

            @block.vector
            def _(dve):
                for u in range(2):
                    nc.vector.memset(mu[u][:, :, :], 1.0)
                nc.vector.memset(carry[0][:, :], 0.0)
                nc.vector.memset(carry[1][:, :], 0.0).then_inc(init, 1)
                dve.wait_ge(init, 1)

                def compare(i, u):
                    g = i * 2 + u
                    dve.wait_ge(rows_in[u], (i + 1) * 32)
                    need(dve, agg_ps, (g - 1) * TILES)
                    nc.vector.tensor_tensor(same[u][:, :, :], drow[u][:, :].rearrange("p (k q) -> p k q", k=TILES),
                                            dstf[:, bass.ds(g * TILES, TILES)].unsqueeze(2).broadcast_to([P, TILES, P]),
                                            ALU.is_equal).then_inc(same_ready, 1)

                def choose(i, u):
                    dve.wait_ge(pos_in[u], (i + 1) * 16)
                    need(dve, gathered_t[1][u], i)
                    for w in range(HALVES):
                        last = nc.vector.tensor_scalar(pick[u][:, w, :], posb[u][:, :], lane[:, w:w + 1], None, ALU.is_equal)
                    last.then_inc(pick_sb, 1)

                def copy_x(i, u):
                    dve.wait_ge(gathered_t[1][u], i + 1)
                    need(dve, m_ps, i * 2 + u - 1)
                    nc.vector.tensor_copy(xT[1][u][:, :], ps_x[1][:, :]).then_inc(xT_ready[1], 1)

                def copy_updates(i, u):
                    g = i * 2 + u
                    dve.wait_ge(u_ps, g + 1)
                    need(dve, agg_ps, (g - 1) * TILES)
                    nc.vector.tensor_copy(mu[u][:, :, 0:D], ps_u[:, :].rearrange("p (k d) -> p k d", k=TILES)).then_inc(u_sb, 1)

                def average(n):
                    k = TILES - 1 - n

                    def stage(i, u):
                        t = (i * 2 + u) * TILES + (n + 1)
                        if n == 0:
                            need(dve, scattered[u], i * (16 * TILES))
                        dve.wait_ge(carry_ready, t)
                        nc.vector.reciprocal(rcnt[:, k:k + 1], ps_a[k][:, D:D + 1]).then_inc(rc, 1)
                        dve.wait_ge(rc, t)
                        last = nc.vector.tensor_scalar(osum[u][:, k, :], ps_a[k][:, 0:D], rcnt[:, k:k + 1], None, ALU.mult)
                        if n == TILES - 1:
                            last.then_inc(osum_ready[u], 1)
                    return stage
                run_stages(dve, [(copy_updates, 2), (choose, 0), (average(0), 2), (compare, 1), (average(1), 2), (copy_x, 0),
                                 (average(2), 2), (average(3), 2)], EG)

        with ExitStack() as ctx:
            xn = [sb(f"xn{u}", [P, TILES, D], F32, ctx) for u in range(2)]
            sn = [sb(f"sn{u}", [P, TILES, D], F32, ctx) for u in range(2)]
            xT = [sb(f"xTn{u}", [P, G], F32, ctx) for u in range(2)]
            hb, neg = [sb(f"hb{u}", [P, G], F32, ctx) for u in range(2)], sb("neg", [P, G], F32, ctx)
            hT = [sb(f"hT{u}", [P, G], F32, ctx) for u in range(2)]
            ps_x, ps_h = [pb(f"ps_xn{u}", ctx=ctx) for u in range(2)], [pb(f"ps_hn{u}", ctx=ctx) for u in range(2)]
            x_in, sums_in, stored = sem2("n1_x_in"), sem2("n1_sums_in"), sem2("n1_stored")
            xt_ps, xt_sb, h_ps, h_sb, stat = sem("n1_xt_ps"), sem("n1_xt_sb"), sem("n1_h_ps"), sem("n1_h_sb"), sem("n1_stat")
            hb_sb, neg_sb = sem("n1_hb"), sem("n1_neg")
            block = ctx.enter_context(nc.Block())

            @block.sync
            def _(sp):
                def load_x(i, u):
                    need(sp, xt_ps, i * 2 + u - 1, gate)
                    sp.dma_start(xn[u][:, :, :], group_rows(x, i * 2 + u, D)).then_inc(x_in[u], 16)

                def load_sums(i, u):
                    need(sp, h_ps, i * 2 + u - 1, gate)
                    sp.dma_start(sn[u][:, :, :], group_rows(sums0, i * 2 + u, D)).then_inc(sums_in[u], 16)
                run_stages(sp, [(load_x, 0), (load_sums, 1)], GROUPS)

            @block.gpsimd
            def _(pool):
                def group(i, u):
                    g = i * 2 + u
                    pool.wait_ge(h_sb, g + 1)
                    pool.sem_inc(gate, 1)
                    pool.dma_start(h_t[:, bass.ds(g * G, G)], hT[u][:, :]).then_inc(stored[u], 16)
                run_groups(pool, group, GROUPS)
                for u in range(2):
                    pool.wait_ge(stored[u], 16 * HALF)

            @block.tensor
            def _(pe):
                def turn(i, u):
                    g = i * 2 + u
                    pe.wait_ge(x_in[u], (i + 1) * 16)
                    need(pe, xt_sb, g - 1)
                    for k in range(TILES):
                        last = nc.tensor.transpose(ps_x[u][:, k * P:(k + 1) * P], xn[u][:, k, :], ident[:, :])
                    last.then_inc(xt_ps, 1)

                def hidden(i, u):
                    g = i * 2 + u
                    pe.wait_ge(xt_sb, g + 1)
                    need(pe, hb_sb, g - 1)
                    nc.tensor.matmul(ps_h[u][:, :], wu[:, 0, :], xT[u][:, :], start=True, stop=False)
                    pe.wait_ge(sums_in[u], (i + 1) * 16)
                    for k in range(TILES):
                        last = nc.tensor.matmul(ps_h[u][:, k * P:(k + 1) * P], sn[u][:, k, :], ident[:, :],
                                                start=False, stop=k == TILES - 1)
                    last.then_inc(h_ps, 1)
                run_stages(pe, [(turn, 0), (hidden, 1)], GROUPS)

            @block.scalar
            def _(act):
                def copy_xt(i, u):
                    g = i * 2 + u
                    act.wait_ge(xt_ps, g + 1)
                    need(act, h_ps, g - 1)
                    nc.scalar.activation(xT[u][:, :], ps_x[u][:, :], ACT.Copy).then_inc(xt_sb, 1)

                def with_bias(i, u):
                    g = i * 2 + u
                    act.wait_ge(h_ps, g + 1)
                    need(act, h_sb, g - 1)
                    nc.scalar.activation(hb[u][:, :], ps_h[u][:, :], ACT.Identity, bias=bupd).then_inc(hb_sb, 1)
                run_stages(act, [(copy_xt, 0), (with_bias, 1)], GROUPS)

            @block.vector
            def _(dve):
                def group(i, u, valid=P):
                    g = i * 2 + u
                    dve.wait_ge(hb_sb, g + 1)
                    nc.vector.tensor_scalar(neg[:, :], hb[u][:, :], 0.0, alpha, ALU.min, ALU.mult).then_inc(neg_sb, 1)
                    dve.wait_ge(neg_sb, g + 1)
                    need(dve, stored[u], i * 16)
                    nc.vector.scalar_tensor_tensor(hT[u][:, :], hb[u][:, :], 0.0, neg[:, :], ALU.max, ALU.add).then_inc(h_sb, 1)
                    dve.wait_ge(h_sb, g + 1)
                    dve.sem_inc(gate, 1)
                    if valid == P:
                        nc.vector.bn_stats(bn[:, bass.ds(g, 1), :].rearrange("p o s -> p (o s)"), hT[u][:, :]).then_inc(stat, 1)
                    else:
                        for k in range(TILES):
                            last = nc.vector.bn_stats(bn[:, g + k, :], hT[u][:, k * P:k * P + valid])
                        last.then_inc(stat, 1)
                for u in range(2):
                    group(0, u)
                with dve.Fori(1, HALF - 1) as i:
                    for u in range(2):
                        group(i, u)
                group(HALF - 1, 0)
                group(HALF - 1, 1, VALID // TILES)
                def chain(ins):
                    links[0] += 1
                    ins.then_inc(chained, 1)
                    dve.wait_ge(chained, links[0])
                dve.wait_ge(stat, GROUPS)
                chain(nc.vector.bn_aggr(bnmv[:, :], bn[:, :, :].rearrange("p g s -> p (g s)")))
                for link in inv_sqrt_steps(nc, bn_scale, bnmv[:, 1:2], cols2[:, 5:6]):
                    chain(link())
                chain(nc.vector.tensor_tensor(bn_scale, bn_scale, gam, ALU.mult))
                chain(nc.vector.tensor_tensor(bn_shift, bnmv[:, 0:1], bn_scale, ALU.mult))
                chain(nc.vector.tensor_tensor(bn_shift, bet, bn_shift, ALU.subtract))

        with ExitStack() as ctx:
            xn = [sb(f"xn2{u}", [P, TILES, D], F32, ctx) for u in range(2)]
            hT = [sb(f"hT2{u}", [P, G], F32, ctx) for u in range(2)]
            yT = [sb(f"yT{u}", [P, G], F32, ctx) for u in range(2)]
            r = [sb(f"r2{u}", [P, TILES, D], F32, ctx) for u in range(2)]
            x1 = [sb(f"x1{u}", [P, TILES, D], F32, ctx) for u in range(2)]
            x1T = sb("x1T", [P, G], F32, ctx)
            lin = sb("lin2", [P, G], F32, ctx)
            ex, el, zb, zs = ([sb(f"{name}{u}", [P, G], F32, ctx) for u in range(2)] for name in ("ex2", "el2", "zb", "zs"))
            xl = [sb(f"xlo{u}", [P, TILES, ROW3], F32, ctx) for u in range(2)]
            xr = [sb(f"xro{u}", [P, TILES, D], F32, ctx) for u in range(2)]
            stats = sb("st2", [P, TILES, 6], F32, ctx)
            mv = [sb(f"mv2{u}", [P, TILES, 2], F32, ctx) for u in range(2)]
            tiny = [sb(f"ty2{u}", [P, 3, TILES], F32, ctx) for u in range(2)]
            ps_y = [pb(f"ps_y{u}", ctx=ctx) for u in range(2)]
            ps_t, ps_h, ps_z = pb("ps_t", ctx=ctx), pb("ps_h", ctx=ctx), pb("ps_z", ctx=ctx)
            ps_l, ps_r, ps_s = pb("ps_l", ctx=ctx), pb("ps_r", ctx=ctx), pb("ps_s", ctx=ctx)
            h_in, x_in = sem2("n2_h_in"), sem2("n2_x_in")
            st_x1, st_l, st_r = sem2("n2_st_x1"), sem2("n2_st_l"), sem2("n2_st_r")
            yt, y_ps, r_sb, nrm, x1_sb, x1t_ps, x1t_sb, h_ps = (sem("n2_" + s) for s in
                ("yt", "y_ps", "r_sb", "nrm", "x1_sb", "x1t_ps", "x1t_sb", "h_ps"))
            ex_sb, lin_sb, el_sb, l_ps, r_ps, z_ps, z_sb, s_ps, l_sb, r2_sb, s_sb = (sem("n2_" + s) for s in
                ("ex_sb", "lin_sb", "el_sb", "l_ps", "r_ps", "z_ps", "z_sb", "s_ps", "l_sb", "r2_sb", "s_sb"))
            zb_sb, stat_sb, mv_sb, dstep = sem("n2_zb"), sem("n2_stat"), sem("n2_mv"), sem("n2_step")
            block = ctx.enter_context(nc.Block())

            @block.sync
            def _(sp):
                def load(i, u):
                    g = i * 2 + u
                    need(sp, yt, g - 1, gate)
                    sp.dma_start(hT[u][:, :], h_t[:, bass.ds(g * G, G)]).then_inc(h_in[u], 16)
                    need(sp, r_sb, g - 1, gate)
                    sp.dma_start(xn[u][:, :, :], group_rows(x, g, D)).then_inc(x_in[u], 16)

                def store_x1(i, u):
                    g = i * 2 + u
                    need(sp, x1_sb, g + 1, gate)
                    sp.dma_start(group_rows(x1_t, g, D), x1[u][:, :, :]).then_inc(st_x1[u], 16)

                def store_lr(i, u):
                    g = i * 2 + u
                    need(sp, r2_sb, g + 1, gate)
                    sp.dma_start(group_rows(xr_t, g, D), xr[u][:, :, :]).then_inc(st_r[u], 16)
                    need(sp, l_sb, g + 1, gate)
                    need(sp, s_sb, g + 1, gate)
                    sp.dma_start(group_rows(xl_t, g, ROW3), xl[u][:, :, :]).then_inc(st_l[u], 16)
                run_stages(sp, [(load, 0), (store_x1, 4), (store_lr, 7)], GROUPS)
                for u in range(2):
                    for s in (st_x1[u], st_l[u], st_r[u]):
                        sp.wait_ge(s, 16 * HALF)

            @block.gpsimd
            def _(pool):
                def normalise(i, u):
                    g = i * 2 + u
                    need(pool, nrm, g + 1, gate)
                    need(pool, st_x1[u], i * 16, gate)
                    need(pool, x1t_ps, g - 1, gate)
                    for k in range(TILES):
                        last = nc.gpsimd.tensor_scalar(x1[u][:, k, :], r[u][:, k, :], tiny[u][:, 0, k:k + 1],
                                                       tiny[u][:, 1, k:k + 1], ALU.mult, ALU.add)
                    last.then_inc(x1_sb, 1)
                run_stages(pool, [(normalise, 0)], GROUPS)

            @block.tensor
            def _(pe):
                def turn_y(i, u):
                    g = i * 2 + u
                    pe.wait_ge(yt, g + 1)
                    need(pe, r_sb, g - 1)
                    for k in range(TILES):
                        last = nc.tensor.transpose(ps_y[u][:, k * P:(k + 1) * P], yT[u][:, k * P:(k + 1) * P], ident[:, :])
                    last.then_inc(y_ps, 1)

                def turn_x1(i, u):
                    g = i * 2 + u
                    pe.wait_ge(x1_sb, g + 1)
                    need(pe, x1t_sb, g)
                    for k in range(TILES):
                        last = nc.tensor.transpose(ps_t[:, k * P:(k + 1) * P], x1[u][:, k, :], ident[:, :])
                    last.then_inc(x1t_ps, 1)

                def hidden(i, u):
                    g = i * 2 + u
                    pe.wait_ge(x1t_sb, g + 1)
                    need(pe, lin_sb, g)
                    nc.tensor.matmul(ps_h[:, :], win[:, :], x1T[:, :], start=True, stop=True).then_inc(h_ps, 1)

                def self_scores(i, u):
                    g = i * 2 + u
                    pe.wait_ge(el_sb, g + 1)
                    need(pe, zb_sb, g)
                    nc.tensor.matmul(ps_z[:, :], wsum[:, :], el[u][:, :], start=True, stop=True).then_inc(z_ps, 1)

                def left(i, u):
                    g = i * 2 + u
                    need(pe, l_sb, g)
                    for k in range(TILES):
                        last = nc.tensor.matmul(ps_l[:, k * D:(k + 1) * D], el[u][:, k * P:(k + 1) * P], wlr[:, 0, :],
                                                start=True, stop=True)
                    last.then_inc(l_ps, 1)

                def right(i, u):
                    g = i * 2 + u
                    need(pe, r2_sb, g)
                    for k in range(TILES):
                        last = nc.tensor.matmul(ps_r[:, k * D:(k + 1) * D], el[u][:, k * P:(k + 1) * P], wlr[:, 1, :],
                                                start=True, stop=True)
                    last.then_inc(r_ps, 1)

                def scores(i, u):
                    g = i * 2 + u
                    pe.wait_ge(z_sb, g + 1)
                    need(pe, s_sb, g)
                    for k in range(TILES):
                        last = nc.tensor.matmul(ps_s[:, k * HEADS:(k + 1) * HEADS], zs[u][:, k * P:(k + 1) * P], attb[:, :],
                                                start=True, stop=True)
                    last.then_inc(s_ps, 1)
                run_stages(pe, [(turn_y, 1), (self_scores, 5), (scores, 6), (left, 5), (turn_x1, 3), (right, 5), (hidden, 3)], GROUPS)

            @block.scalar
            def _(act):
                def batch_norm(i, u):
                    g = i * 2 + u
                    act.wait_ge(h_in[u], (i + 1) * 16)
                    need(act, y_ps, g - 1)
                    nc.scalar.activation(yT[u][:, :], hT[u][:, :], ACT.Identity, bias=bn_shift, scale=bn_scale).then_inc(yt, 1)

                def exponentials(i, u):
                    g = i * 2 + u
                    act.wait_ge(h_ps, g + 1)
                    need(act, el_sb, g - 1)
                    nc.scalar.activation(ex[u][:, :], ps_h[:, :], ACT.Exp, bias=bin_).then_inc(ex_sb, 1)

                def copy_x1t(i, u):
                    g = i * 2 + u
                    act.wait_ge(x1t_ps, g + 1)
                    need(act, h_ps, g)
                    nc.scalar.activation(x1T[:, :], ps_t[:, :], ACT.Copy).then_inc(x1t_sb, 1)

                def with_bias(i, u):
                    g = i * 2 + u
                    act.wait_ge(z_ps, g + 1)
                    need(act, z_sb, g - 1)
                    nc.scalar.activation(zb[u][:, :], ps_z[:, :], ACT.Identity, bias=bself).then_inc(zb_sb, 1)

                def copy_left(i, u):
                    g = i * 2 + u
                    act.wait_ge(l_ps, g + 1)
                    need(act, st_l[u], i * 16)
                    nc.scalar.activation(xl[u][:, :, 0:D], ps_l[:, :].rearrange("p (k d) -> p k d", k=TILES), ACT.Copy
                                         ).then_inc(l_sb, 1)

                def copy_right(i, u):
                    g = i * 2 + u
                    act.wait_ge(r_ps, g + 1)
                    need(act, st_r[u], i * 16)
                    nc.scalar.activation(xr[u][:, :, :], ps_r[:, :].rearrange("p (k d) -> p k d", k=TILES), ACT.Copy
                                         ).then_inc(r2_sb, 1)

                def copy_scores(i, u):
                    g = i * 2 + u
                    act.wait_ge(s_ps, g + 1)
                    nc.scalar.activation(xl[u][:, :, D:ROW3], ps_s[:, 0:TILES * HEADS].rearrange("p (k h) -> p k h", k=TILES),
                                         ACT.Copy).then_inc(s_sb, 1)
                run_stages(act, [(exponentials, 4), (batch_norm, 0), (with_bias, 5), (copy_scores, 6), (copy_left, 5), (copy_x1t, 3),
                                 (copy_right, 5)], GROUPS)

            @block.vector
            def _(dve):
                def linear(i, u):
                    g = i * 2 + u
                    dve.wait_ge(ex_sb, g + 1)
                    need(dve, el_sb, g)
                    nc.vector.tensor_scalar(lin[:, :], ps_h[:, :], binm1, -1.0, ALU.add, ALU.max).then_inc(lin_sb, 1)

                def elu(i, u):
                    g = i * 2 + u
                    dve.wait_ge(lin_sb, g + 1)
                    need(dve, r_ps, g - 1)
                    nc.vector.scalar_tensor_tensor(el[u][:, :], ex[u][:, :], 1.0, lin[:, :], ALU.min, ALU.add).then_inc(el_sb, 1)

                def residual(i, u):
                    g = i * 2 + u
                    dve.wait_ge(y_ps, g + 1)
                    dve.wait_ge(x_in[u], (i + 1) * 16)
                    need(dve, x1_sb, g - 1)
                    nc.vector.tensor_tensor(r[u][:, :, :], xn[u][:, :, :], ps_y[u][:, :].rearrange("p (k d) -> p k d", k=TILES),
                                            ALU.add).then_inc(r_sb, 1)

                def leak(i, u):
                    g = i * 2 + u
                    dve.wait_ge(zb_sb, g + 1)
                    need(dve, s_ps, g - 1)
                    nc.vector.scalar_tensor_tensor(zs[u][:, :], zb[u][:, :], SLOPE, zb[u][:, :], ALU.mult, ALU.max).then_inc(z_sb, 1)

                stat, aggregate, t = norm_stages(nc, dve, gate, r, r_sb, stats, mv, tiny, stat_sb, mv_sb, dstep, x1_sb, nrm)
                run_stages(dve, [(t[0], 2), (leak, 6), (t[1], 2), (linear, 4), (t[2], 2), (elu, 4), (t[3], 2), (residual, 1),
                                 (t[4], 2), (stat[0], 1), (t[5], 2), (stat[1], 1), (t[6], 2), (stat[2], 1), (t[7], 2), (stat[3], 1),
                                 (t[8], 2), (t[9], 2), (aggregate, 1), (t[10], 2), (t[11], 2), (t[12], 2)], GROUPS)

        with ExitStack() as ctx:
            gidx = [sb(f"gidxa{u}", [P, 2, TILES], I32, ctx) for u in range(2)]
            sidx = [sb(f"sidxa{u}", [P, TILES], I32, ctx) for u in range(2)]
            gl = [sb(f"gl{u}", [P, TILES, ROW3], F32, ctx) for u in range(2)]
            gk = [sb(f"gk{u}", [P, TILES, D], F32, ctx) for u in range(2)]
            xw = [sb(f"xwa{u}", [P, TILES, HALVES, D], F32, ctx) for u in range(2)]
            posb = [sb(f"posba{u}", [P, G], F32, ctx) for u in range(2)]
            pick = [sb(f"picka{u}", [P, HALVES, G], F32, ctx) for u in range(2)]
            drow = [sb(f"drowa{u}", [P, G], I32, ctx) for u in range(2)]
            frow = [sb(f"frowa{u}", [1, G], F32, ctx) for u in range(2)]
            reset = [sb(f"reset{u}", [HEADS, 2, G], F32, ctx) for u in range(2)]
            ea = [sb(f"ea{u}", [PAIRS * 2, G], BF16, ctx) for u in range(2)]
            same = [sb(f"samea{u}", [P, TILES, P], F32, ctx) for u in range(2)]
            zb, zT = sb("zba", [P, G], F32, ctx), sb("zT", [P, G], F32, ctx)
            run = sb("run", [HEADS, G], F32, ctx)
            mx = [sb(f"mx{u}", [HEADS, G + 1], F32, ctx) for u in range(2)]
            off = sb("off", [HEADS, G], F32, ctx)
            dcar = sb("dcar", [HEADS, TILES], F32, ctx)
            ecar = sb("ecar", [1, TILES * HEADS], F32, ctx)
            ecx = [sb(f"ecx{u}", [1, TILES, ROW3], F32, ctx) for u in range(2)]
            pay = [sb(f"pay{u}", [P, TILES, ROW3], F32, ctx) for u in range(2)]
            carry = [sb(f"carrya{j}", [1, ROW3], F32, ctx) for j in range(2)]
            carrs = sb("carrs", [1, ROW3], F32, ctx)
            maxe = [sb(f"maxe{u}", [P, TILES, HEADS], F32, ctx) for u in range(2)]
            osum = [sb(f"osuma{u}", [P, TILES, ROWA], F32, ctx) for u in range(2)]
            ps_z = [pb(f"psa_z{u}", ctx=ctx) for u in range(2)]
            ps_al, ps_t = pb("psa_al", ctx=ctx), pb("psa_t", ctx=ctx)
            ps_a = [pb(f"psa_a{k}", ctx=ctx) for k in range(TILES)]
            WE, WM, WC = 0, TILES * HEADS, 2 * TILES * HEADS

            gidx_set, sidx_set, win_in, wide_in, whole = sem("a_gidx_set"), sem("a_sidx_set"), sem2("a_win_in"), sem("a_wide_in"), sem("a_whole")
            gathered, scattered, dst_in, mask_in = sem2("a_gathered"), sem2("a_scattered"), sem2("a_dst_in"), sem2("a_mask_in")
            z_ps, z_sb, al_ps, off_sb, mx_sb, t_ps = (sem("a_" + s) for s in ("z_ps", "z_sb", "al_ps", "off_sb", "mx_sb", "t_ps"))
            pos_in, reset_in, pick_sb, rows_sb = sem2("a_pos_in"), sem2("a_reset_in"), sem("a_pick"), sem("a_rows_sb")
            w_sb, ecar_sb, ecx_sb, pay_sb, max_out = (sem("a_" + s) for s in ("w_sb", "ecar_sb", "ecx_sb", "pay_sb", "max_out"))
            same_ready, agg_ps, carry_ready, carry_scaled = sem("a_same"), sem("a_agg_ps"), sem("a_carry"), sem("a_carrs")
            osum_ready, run_sb, dcar_sb = sem2("a_osum"), sem("a_run"), sem("a_dcar")
            zb_sb = sem("a_zb")
            block = ctx.enter_context(nc.Block())

            @block.sync
            def _(sp):
                def load_windows_and_positions(i, u):
                    g = i * 2 + u
                    need(sp, z_ps, g - 1, gate)
                    load_windows(sp, i, u, xr_t, xw, bases, win_in)
                    need(sp, pick_sb, g - 1, gate)
                    sp.dma_start(posb[u][:, :], positions[bass.ds(g, 1), :].rearrange("o q -> (o q)").partition_broadcast(P)
                                 ).then_inc(pos_in[u], 16)
                    sp.dma_start(ea[u][:, :], ea_parts[bass.ds(g, 1), :, :].rearrange("o j q -> (o j) q")).then_inc(pos_in[u], 16)

                def load_resets(i, u):
                    g = i * 2 + u
                    need(sp, mx_sb, g - 1, gate)
                    sp.dma_start(reset[u][:, :, :], masks[bass.ds(g, 1), 0:2, :].rearrange("o j q -> (o j) q").partition_broadcast(HEADS)
                                 ).then_inc(reset_in[u], 16)

                def load_destinations(i, u):
                    g = i * 2 + u
                    need(sp, same_ready, g - 1, gate)
                    sp.dma_start(drow[u][:, :], dst_row[bass.ds(g, 1), :].rearrange("o q -> (o q)").partition_broadcast(P)
                                 ).then_inc(dst_in[u], 16)

                def load_carry_mask(i, u):
                    g = i * 2 + u
                    need(sp, agg_ps, (g - 1) * TILES, gate)
                    sp.dma_start(frow[u][:, :], masks[bass.ds(g, 1), 2, :]).then_inc(mask_in[u], 16)
                run_stages(sp, [(load_destinations, 2), (load_windows_and_positions, 0), (load_resets, 1), (load_carry_mask, 2)], EG)

            @block.gpsimd
            def _(pool):
                def hold(sem_, value):
                    need(pool, sem_, value, gate)

                def gather(i, u):
                    g = i * 2 + u
                    hold(z_ps, g - 1)
                    hold(rows_sb, g - 1)
                    hold(gathered[u], i * (16 * TILES))
                    nc.gpsimd.tensor_copy(gidx[u][:, :, :], idx[:, bass.ds(g, 1), 0:2, :].rearrange("p o j k -> p (o j) k")
                                          ).then_inc(gidx_set, 1)
                    hold(gidx_set, g + 1)
                    for k in range(TILES):
                        pool.indirect_dma_start(
                            out=gl[u][:, k, :], out_offset=None, in_=xl_t,
                            in_offset=bass.IndirectOffsetOnAxis(ap=gidx[u][:, 0, k:k + 1], axis=0)).then_inc(gathered[u], 16)
                    gather_wide(pool, gate, i, u, xr_t, xw, gidx, wide, win_in, wide_in, whole)

                def scatter(i, u):
                    g = i * 2 + u
                    hold(scattered[u], i * (16 * TILES))
                    nc.gpsimd.tensor_copy(sidx[u][:, :], idx[:, bass.ds(g, 1), 2, :].rearrange("p o k -> p (o k)")
                                          ).then_inc(sidx_set, 1)
                    hold(sidx_set, g + 1)
                    hold(osum_ready[u], i + 1)
                    for k in range(TILES):
                        pool.indirect_dma_start(
                            out=sums1, out_offset=bass.IndirectOffsetOnAxis(ap=sidx[u][:, k:k + 1], axis=0),
                            in_=osum[u][:, k, :], in_offset=None, bounds_check=NP - 1, oob_is_err=False).then_inc(scattered[u], 16)

                run_stages(pool, [(scatter, 5), (gather, 0)], EG)
                for u in range(2):
                    pool.wait_ge(scattered[u], 16 * TILES * EHALF)

            @block.tensor
            def _(pe):
                pe.wait_ge(init, 2)

                def turn(part):
                    def stage(i, u):
                        g = i * 2 + u
                        if part == 0:
                            pe.wait_ge(pos_in[u], (i + 1) * 32)
                            need(pe, zb_sb, g - 1)
                            nc.tensor.matmul(ps_z[u][:, :], we18[:, :], ea[u][:, :], start=True, stop=False)
                            pe.wait_ge(gathered[u], (i + 1) * (16 * TILES))
                            pe.wait_ge(win_in[u], (i + 1) * (16 * TILES))
                            pe.wait_ge(whole, g + 1)
                            pe.wait_ge(pick_sb, g + 1)
                        for k in (0, 1) if part == 0 else (2, 3):
                            edges = slice(k * P, (k + 1) * P)
                            nc.tensor.matmul(ps_z[u][:, edges], gl[u][:, k, 0:D], ident[:, :], start=False, stop=False)
                            for w in range(HALVES):
                                last = nc.tensor.matmul(ps_z[u][:, edges], xw[u][:, k, w, :], pick[u][:, w, edges],
                                                        start=False, stop=k == TILES - 1 and w == HALVES - 1)
                        if part == 1:
                            last.then_inc(z_ps, 1)
                    return stage

                def scores(i, u):
                    g = i * 2 + u
                    pe.wait_ge(z_sb, g + 1)
                    need(pe, off_sb, g)
                    nc.tensor.matmul(ps_al[0:HEADS, :], attb[:, :], zT[:, :], start=True, stop=True).then_inc(al_ps, 1)

                def turn_back(i, u):
                    g = i * 2 + u
                    pe.wait_ge(off_sb, g + 1)
                    pe.wait_ge(dcar_sb, g * 2 + 2)
                    need(pe, max_out, g)
                    pe.sem_inc(gate, 1)
                    for k in range(TILES):
                        nc.tensor.transpose(ps_t[:, WE + k * HEADS:WE + (k + 1) * HEADS], off[:, k * P:(k + 1) * P],
                                            ident[0:HEADS, 0:HEADS])
                        nc.tensor.transpose(ps_t[:, WM + k * HEADS:WM + (k + 1) * HEADS], mx[u][:, k * P:(k + 1) * P],
                                            ident[0:HEADS, 0:HEADS])
                    for k in range(TILES):
                        last = nc.tensor.transpose(ps_t[0:1, WC + k * HEADS:WC + (k + 1) * HEADS], dcar[:, k:k + 1],
                                                   ident[0:HEADS, 0:HEADS])
                    last.then_inc(t_ps, 1)

                def sums(n):
                    k = TILES - 1 - n

                    def stage(i, u):
                        g = i * 2 + u
                        if n == 0:
                            pe.wait_ge(same_ready, g + 1)
                            pe.wait_ge(mask_in[u], (i + 1) * 16)
                            pe.wait_ge(pay_sb, g + 1)
                            need(pe, osum_ready[1 - u], i + u)
                        nc.tensor.matmul(ps_a[k][:, 0:ROW3], same[u][:, k, :], pay[u][:, k, :], start=True, stop=False)
                        pe.wait_ge(carry_scaled, g * TILES + (n + 1))
                        nc.tensor.matmul(ps_a[k][:, 0:ROW3], frow[u][:, k * P:(k + 1) * P], carrs[:, :],
                                         start=False, stop=True).then_inc(agg_ps, 1)
                    return stage
                run_stages(pe, [(sums(0), 3), (turn(0), 1), (sums(1), 3), (turn(1), 1), (turn_back, 2), (sums(2), 3), (scores, 1),
                                (sums(3), 3)], EG)

            @block.scalar
            def _(act):
                def copy_rows(i, u):
                    g = i * 2 + u
                    act.wait_ge(gathered[u], (i + 1) * (16 * TILES))
                    need(act, pay_sb, g - 1)
                    nc.scalar.activation(gk[u][:, :, :], gl[u][:, :, 0:D], ACT.Copy).then_inc(rows_sb, 1)

                def with_bias(i, u):
                    g = i * 2 + u
                    act.wait_ge(z_ps, g + 1)
                    need(act, z_sb, g)
                    nc.scalar.activation(zb[:, :], ps_z[u][:, :], ACT.Identity, bias=bz).then_inc(zb_sb, 1)

                def results(i, u):
                    g = i * 2 + u
                    need(act, scattered[u], i * (16 * TILES))
                    act.wait_ge(max_out, g + 1)
                    nc.scalar.activation(osum[u][:, :, ROW3:ROWA], maxe[u][:, :, :], ACT.Copy)
                    for n, k in enumerate(reversed(range(TILES))):
                        act.wait_ge(carry_ready, g * TILES + (n + 1))
                        last = nc.scalar.activation(osum[u][:, k, 0:ROW3], ps_a[k][:, 0:ROW3], ACT.Copy)
                    last.then_inc(osum_ready[u], 1)

                def weights(i, u):
                    g = i * 2 + u
                    act.wait_ge(t_ps, g + 1)
                    need(act, agg_ps, (g - 1) * TILES)
                    nc.scalar.activation(pay[u][:, :, D:ROW3], ps_t[:, WE:WE + TILES * HEADS].rearrange("p (k h) -> p k h", k=TILES),
                                         ACT.Exp).then_inc(w_sb, 1)
                    need(act, ecx_sb, g)
                    nc.scalar.activation(ecar[:, :], ps_t[0:1, WC:WC + TILES * HEADS], ACT.Exp).then_inc(ecar_sb, 1)
                    nc.scalar.activation(maxe[u][:, :, :], ps_t[:, WM:WM + TILES * HEADS].rearrange("p (k h) -> p k h", k=TILES),
                                         ACT.Copy).then_inc(max_out, 1)
                run_stages(act, [(copy_rows, 1), (with_bias, 1), (weights, 2), (results, 3)], EG)

            @block.vector
            def _(dve):
                nc.vector.memset(mx[0][:, :], 0.0)
                nc.vector.memset(mx[1][:, :], 0.0)
                nc.vector.memset(carry[0][:, :], 0.0)
                nc.vector.memset(carry[1][:, :], 0.0).then_inc(init, 1)
                dve.wait_ge(init, 2)

                def choose(i, u):
                    dve.wait_ge(pos_in[u], (i + 1) * 32)
                    need(dve, z_ps, i * 2 + u - 1)
                    for w in range(HALVES):
                        last = nc.vector.tensor_scalar(pick[u][:, w, :], posb[u][:, :], lane[:, w:w + 1], None, ALU.is_equal)
                    last.then_inc(pick_sb, 1)

                def compare(i, u):
                    g = i * 2 + u
                    dve.wait_ge(dst_in[u], (i + 1) * 16)
                    need(dve, agg_ps, (g - 1) * TILES)
                    nc.vector.tensor_tensor(same[u][:, :, :], drow[u][:, :].rearrange("p (k q) -> p k q", k=TILES),
                                            dstf[:, bass.ds(g * TILES, TILES)].unsqueeze(2).broadcast_to([P, TILES, P]),
                                            ALU.is_equal).then_inc(same_ready, 1)

                def leak(i, u):
                    g = i * 2 + u
                    dve.wait_ge(zb_sb, g + 1)
                    need(dve, al_ps, g)
                    nc.vector.scalar_tensor_tensor(zT[:, :], zb[:, :], SLOPE, zb[:, :], ALU.mult, ALU.max).then_inc(z_sb, 1)

                def running_maximum(i, u):
                    g = i * 2 + u
                    dve.wait_ge(al_ps, g + 1)
                    dve.wait_ge(reset_in[u], (i + 1) * 16)
                    nc.vector.tensor_tensor_scan(run[:, ::-1], reset[u][:, 0, ::-1], ps_al[0:HEADS, ::-1], mx[1 - u][:, 0:1],
                                                 ALU.add, ALU.max).then_inc(run_sb, 1)

                def maxima(i, u):
                    g = i * 2 + u
                    dve.wait_ge(run_sb, g + 1)
                    need(dve, t_ps, g - 1)
                    nc.vector.tensor_copy(mx[u][:, G:G + 1], mx[1 - u][:, 0:1])
                    nc.vector.tensor_tensor_scan(mx[u][:, 0:G], reset[u][:, 1, :], run[:, :], 0.0, ALU.add, ALU.max
                                                 ).then_inc(mx_sb, 1)
                    dve.wait_ge(mx_sb, g + 1)
                    need(dve, t_ps, g)
                    edge = mx[u][:, 0:G].rearrange("h (k q) -> h k q", k=TILES)[:, :, P - 1]
                    nc.vector.tensor_tensor(dcar[:, :], mx[u][:, P:G + 1:P], edge, ALU.subtract).then_inc(dcar_sb, 1)
                    nc.vector.tensor_tensor(off[:, :], ps_al[0:HEADS, :], mx[u][:, 0:G], ALU.subtract).then_inc(off_sb, 1)
                    dve.wait_ge(dcar_sb, g * 2 + 1)
                    nc.vector.tensor_scalar(dcar[:, :], dcar[:, :], 0.0, None, ALU.min).then_inc(dcar_sb, 1)

                def payload(i, u):
                    g = i * 2 + u
                    dve.wait_ge(w_sb, g + 1)
                    dve.wait_ge(rows_sb, g + 1)
                    for k in range(TILES):
                        last = nc.vector.tensor_tensor(pay[u][:, k, 0:D].rearrange("p (h c) -> p h c", h=HEADS),
                                                       gk[u][:, k, :].rearrange("p (h c) -> p h c", h=HEADS),
                                                       pay[u][:, k, D:ROW3].unsqueeze(2).broadcast_to([P, HEADS, C]), ALU.mult)
                    last.then_inc(pay_sb, 1)
                    dve.wait_ge(ecar_sb, g + 1)
                    e2 = ecar[:, :].rearrange("o (k h) -> o k h", k=TILES)
                    for k in range(TILES):
                        nc.vector.tensor_copy(ecx[u][:, k, 0:D].rearrange("o (h c) -> o h c", h=HEADS),
                                              e2[:, k, :].unsqueeze(2).broadcast_to([1, HEADS, C]))
                    nc.vector.tensor_copy(ecx[u][:, :, D:ROW3], e2).then_inc(ecx_sb, 1)

                def scale(n):
                    def stage(i, u):
                        g = i * 2 + u
                        if n == 0:
                            dve.wait_ge(ecx_sb, g + 1)
                        need(dve, agg_ps, g * TILES + n)
                        need(dve, carry_ready, g * TILES + n)
                        nc.vector.tensor_tensor(carrs[:, :], carry[(n + 1) % 2][:, :], ecx[u][:, TILES - 1 - n, :], ALU.mult
                                                ).then_inc(carry_scaled, 1)
                    return stage

                def take(n):
                    def stage(i, u):
                        g = i * 2 + u
                        dve.wait_ge(agg_ps, g * TILES + (n + 1))
                        nc.vector.tensor_copy(carry[n % 2][:, :], ps_a[TILES - 1 - n][0:1, 0:ROW3]).then_inc(carry_ready, 1)
                    return stage
                run_stages(dve, [(scale(0), 3), (running_maximum, 2), (take(0), 3), (scale(1), 3), (maxima, 2), (take(1), 3),
                                 (scale(2), 3), (choose, 0), (compare, 2), (leak, 1), (take(2), 3), (scale(3), 3), (payload, 2),
                                 (take(3), 3)], EG)

        with ExitStack() as ctx:
            sn = [sb(f"sn3{u}", [P, TILES, ROWA], F32, ctx) for u in range(2)]
            ln = [sb(f"ln3{u}", [P, TILES, ROW3], F32, ctx) for u in range(2)]
            x1 = [sb(f"x13{u}", [P, TILES, D], F32, ctx) for u in range(2)]
            xb = [sb(f"xb3{u}", [P, TILES, D], F32, ctx) for u in range(2)]
            top_ = sb("top3", [P, TILES, HEADS], F32, ctx)
            dd = sb("dd3", [P, 2, TILES, HEADS], F32, ctx)
            ff = [sb(f"ff3{u}", [P, 2, TILES, HEADS], F32, ctx) for u in range(2)]
            den = sb("den3", [P, TILES, HEADS], F32, ctx)
            a1, a2 = ([sb(f"{name}{u}", [P, TILES, D], F32, ctx) for u in range(2)] for name in ("a13", "a23"))
            ex, el = ([sb(f"{name}{u}", [P, G], F32, ctx) for u in range(2)] for name in ("ex3", "el3"))
            lin = sb("lin3", [P, G], F32, ctx)
            r = [sb(f"r3{u}", [P, TILES, D], F32, ctx) for u in range(2)]
            o = [sb(f"o3{u}", [P, TILES, D], F32, ctx) for u in range(2)]
            stats = sb("st3", [P, TILES, 6], F32, ctx)
            mv = [sb(f"mv3{u}", [P, TILES, 2], F32, ctx) for u in range(2)]
            tiny = [sb(f"ty3{u}", [P, 3, TILES], F32, ctx) for u in range(2)]
            ps_g, ps_o = ([pb(f"{name}{u}", ctx=ctx) for u in range(2)] for name in ("ps3_g", "ps3_o"))
            rows_in, x_in, stored = sem2("n3_in"), sem2("n3_x_in"), sem2("n3_stored")
            top_sb, wstep, stat_sb, mv_sb, dstep = (sem("n3_" + s) for s in ("top", "wstep", "stat", "mv", "step"))
            d_sb, f_sb, ff_sb, a_sb, a_ps, ex_sb, lin_sb, el_sb, o_ps, xb_sb, r_sb, nrm, o_sb = (sem("n3_" + s) for s in
                ("d", "f", "ff", "a", "a_ps", "ex", "lin", "el", "o_ps", "xb", "r", "nrm", "o"))
            block = ctx.enter_context(nc.Block())

            def heads(t):
                return t.rearrange("p (h c) -> p h c", h=HEADS)

            @block.sync
            def _(sp):
                def load(i, u):
                    g = i * 2 + u
                    need(sp, a_sb, g - 1, gate)
                    sp.dma_start(sn[u][:, :, :], group_rows(sums1, g, ROWA)).then_inc(rows_in[u], 16)
                    sp.dma_start(ln[u][:, :, :], group_rows(xl_t, g, ROW3)).then_inc(rows_in[u], 16)

                def load_x1(i, u):
                    g = i * 2 + u
                    need(sp, xb_sb, g - 1, gate)
                    sp.dma_start(x1[u][:, :, :], group_rows(x1_t, g, D)).then_inc(x_in[u], 16)

                def store(i, u):
                    g = i * 2 + u
                    need(sp, o_sb, g + 1, gate)
                    sp.dma_start(group_rows(out, g, D), o[u][:, :, :]).then_inc(stored[u], 16)
                run_stages(sp, [(load_x1, 3), (store, 7), (load, 0)], GROUPS)
                for u in range(2):
                    sp.wait_ge(stored[u], 16 * HALF)

            @block.gpsimd
            def _(pool):
                def with_bias(i, u):
                    g = i * 2 + u
                    need(pool, x_in[u], (i + 1) * 16, gate)
                    need(pool, r_sb, g - 1, gate)
                    nc.gpsimd.tensor_tensor(xb[u][:, :, :], x1[u][:, :, :], bout[:, :].unsqueeze(1).broadcast_to([P, TILES, D]),
                                            ALU.add).then_inc(xb_sb, 1)

                def weigh(out, rows, part):
                    def stage(i, u):
                        g = i * 2 + u
                        need(pool, ff_sb, g + 1, gate)
                        need(pool, a_ps, g - 1, gate)
                        for k in range(TILES):
                            last = nc.gpsimd.tensor_tensor(heads(out[u][:, k, :]), heads(rows[u][:, k, 0:D]),
                                                           ff[u][:, part, k, :].unsqueeze(2).broadcast_to([P, HEADS, C]),
                                                           ALU.mult)
                        if part == 1:
                            last.then_inc(a_sb, 1)
                    return stage
                run_stages(pool, [(weigh(a1, sn, 0), 1), (weigh(a2, ln, 1), 1), (with_bias, 3)], GROUPS)

            @block.tensor
            def _(pe):
                def project(i, u):
                    g = i * 2 + u
                    pe.wait_ge(el_sb, g + 1)
                    need(pe, r_sb, g - 1)
                    for k in range(TILES):
                        last = nc.tensor.matmul(ps_o[u][:, k * D:(k + 1) * D], el[u][:, k * P:(k + 1) * P], wout[:, :],
                                                start=True, stop=True)
                    last.then_inc(o_ps, 1)

                def join(i, u):
                    g = i * 2 + u
                    need(pe, lin_sb, g - 1)
                    pe.wait_ge(a_sb, g + 1)
                    for k in range(TILES):
                        nc.tensor.matmul(ps_g[u][:, k * P:(k + 1) * P], a1[u][:, k, :], ident[:, :], start=True, stop=False)
                        last = nc.tensor.matmul(ps_g[u][:, k * P:(k + 1) * P], a2[u][:, k, :], ident[:, :], start=False, stop=True)
                    last.then_inc(a_ps, 1)
                run_stages(pe, [(join, 2), (project, 3)], GROUPS)

            @block.scalar
            def _(act):
                def exponentials(i, u):
                    g = i * 2 + u
                    act.wait_ge(a_ps, g + 1)
                    need(act, el_sb, g - 1)
                    nc.scalar.activation(ex[u][:, :], ps_g[u][:, :], ACT.Exp, bias=bc).then_inc(ex_sb, 1)

                def factors(i, u):
                    g = i * 2 + u
                    act.wait_ge(d_sb, g + 1)
                    need(act, a_sb, g - 1)
                    nc.scalar.activation(ff[u][:, :, :, :], dd[:, :, :, :], ACT.Exp).then_inc(f_sb, 1)

                def normalise(i, u):
                    g = i * 2 + u
                    act.wait_ge(nrm, g + 1)
                    need(act, stored[u], i * 16)
                    for k in range(TILES):
                        last = nc.scalar.activation(o[u][:, k, :], r[u][:, k, :], ACT.Identity, bias=tiny[u][:, 1, k:k + 1],
                                                    scale=tiny[u][:, 0, k:k + 1])
                    last.then_inc(o_sb, 1)
                run_stages(act, [(normalise, 6), (exponentials, 2), (factors, 0)], GROUPS)

            @block.vector
            def _(dve):
                def maxima(i, u):
                    g = i * 2 + u
                    dve.wait_ge(rows_in[u], (i + 1) * 32)
                    need(dve, d_sb, g)
                    nc.vector.tensor_tensor(top_[:, :, :], sn[u][:, :, ROW3:ROWA], ln[u][:, :, D:ROW3], ALU.max).then_inc(top_sb, 1)

                def differences(i, u):
                    g = i * 2 + u
                    dve.wait_ge(top_sb, g + 1)
                    need(dve, f_sb, g)
                    nc.vector.tensor_tensor(dd[:, 0, :, :], sn[u][:, :, ROW3:ROWA], top_[:, :, :], ALU.subtract)
                    nc.vector.tensor_tensor(dd[:, 1, :, :], ln[u][:, :, D:ROW3], top_[:, :, :], ALU.subtract).then_inc(d_sb, 1)

                def linear(i, u):
                    g = i * 2 + u
                    dve.wait_ge(ex_sb, g + 1)
                    need(dve, el_sb, g)
                    nc.vector.tensor_scalar(lin[:, :], ps_g[u][:, :], bcm1, -1.0, ALU.add, ALU.max).then_inc(lin_sb, 1)

                def elu(i, u):
                    g = i * 2 + u
                    dve.wait_ge(lin_sb, g + 1)
                    need(dve, o_ps, g - 1)
                    nc.vector.scalar_tensor_tensor(el[u][:, :], ex[u][:, :], 1.0, lin[:, :], ALU.min, ALU.add).then_inc(el_sb, 1)

                def residual(i, u):
                    g = i * 2 + u
                    dve.wait_ge(o_ps, g + 1)
                    dve.wait_ge(xb_sb, g + 1)
                    need(dve, o_sb, g - 1)
                    nc.vector.tensor_tensor(r[u][:, :, :], xb[u][:, :, :], ps_o[u][:, :].rearrange("p (k d) -> p k d", k=TILES),
                                            ALU.add).then_inc(r_sb, 1)

                def denominators(n):
                    def stage(i, u):
                        g = i * 2 + u
                        if n == 0:
                            dve.wait_ge(f_sb, g + 1)
                            last = nc.vector.tensor_tensor(den[:, :, :], sn[u][:, :, D:ROW3], ff[u][:, 0, :, :], ALU.mult)
                        else:
                            dve.wait_ge(wstep, g * 3 + n)
                        if n == 1:
                            last = nc.vector.tensor_tensor(den[:, :, :], den[:, :, :], ff[u][:, 1, :, :], ALU.add)
                        if n == 2:
                            last = nc.vector.reciprocal(den[:, :, :], den[:, :, :])
                        if n < 3:
                            last.then_inc(wstep, 1)
                        else:
                            nc.vector.tensor_tensor(ff[u][:, :, :, :], ff[u][:, :, :, :],
                                                    den[:, :, :].unsqueeze(1).broadcast_to([P, 2, TILES, HEADS]), ALU.mult
                                                    ).then_inc(ff_sb, 1)
                    return stage

                stat, aggregate, t = norm_stages(nc, dve, gate, r, r_sb, stats, mv, tiny, stat_sb, mv_sb, dstep, o_sb, nrm)
                dn = [denominators(n) for n in range(4)]
                run_stages(dve, [(t[0], 5), (linear, 3), (t[1], 5), (elu, 3), (t[2], 5), (maxima, 0), (t[3], 5), (differences, 0),
                                 (t[4], 5), (residual, 4), (t[5], 5), (stat[0], 4), (t[6], 5), (dn[0], 0), (stat[1], 4), (t[7], 5),
                                 (dn[1], 0), (stat[2], 4), (t[8], 5), (dn[2], 0), (stat[3], 4), (t[9], 5), (dn[3], 0), (t[10], 5),
                                 (aggregate, 4), (t[11], 5), (t[12], 5)], GROUPS)


_WEIGHTS = ["L0_gnn_W_msg", "L0_gnn_b_msg", "L0_gnn_W_upd", "L0_gnn_b_upd", "L0_gnn_prelu_a", "L0_gnn_gamma", "L0_gnn_beta",
            "L1_gnn_w_in", "L1_gnn_b_in", "L1_gnn_w_l", "L1_gnn_b_l", "L1_gnn_w_r", "L1_gnn_b_r", "L1_gnn_w_e", "L1_gnn_att",
            "L1_gnn_bias_conv", "L1_gnn_w_out", "L1_gnn_b_out"]


def kernel(**inputs):
    import numpy as np
    import concourse.bacc as bacc
    from concourse.bass_utils import run_bass_kernel_spmd as run

    x = np.asarray(inputs["x"])
    src, dst, ea = (np.asarray(inputs[k]) for k in ("src", "dst", "edge_attr_2"))
    n, e = x.shape[0], src.shape[0]
    pair = 2 * G
    n_pad, e_pad = -(-n // pair) * pair, -(-e // pair) * pair

    def rows(a):
        return np.ascontiguousarray(a.reshape(-1, G)[:, ::-1])

    def cols(a):
        return np.ascontiguousarray(rows(a).reshape(-1, P).T)

    src_e = np.pad(src, (0, e_pad - e))
    dst_e = np.pad(dst, (0, e_pad - e), constant_values=n)
    next_e = np.pad(dst_e[1:], (0, 1), constant_values=n + 1)
    prev_e = np.pad(dst_e[:-1], (1, 0), constant_values=-1)
    arrays = {
        "x": np.pad(x, ((0, n_pad - n), (0, 0))),
        "src_col": cols(src_e), "dst_col": cols(dst_e), "next_col": cols(next_e),
        "dst_row": rows(dst_e), "next_row": rows(next_e), "prev_row": rows(prev_e),
        "before_row": np.ascontiguousarray(prev_e[::G, None]),
        "ea_row": np.ascontiguousarray(np.pad(ea, ((0, e_pad - e), (0, 0))).reshape(-1, G, 2)[:, ::-1].transpose(0, 2, 1)),
    }
    for name in _WEIGHTS:
        arrays[name] = np.asarray(inputs[name])
    nc = bacc.Bacc("TRN2", target_bir_lowering=False, num_devices=1)
    args = [nc.dram_tensor("in_" + k, a.shape, mybir.dt.from_np(a.dtype), kind="ExternalInput").ap() for k, a in arrays.items()]
    out = nc.dram_tensor("out", (n_pad, D), F32, kind="ExternalOutput").ap()
    build(nc, *args, out, n, e)
    r = run(nc, [{"in_" + k: a for k, a in arrays.items()}], core_ids=[0])
    return r.results[0]["out"][:n]
```
